# Optimizing a Trainium2 kernel written in Bass

```python
import numpy as np
import jax
import jax.numpy as jnp

def _softmax(x, axis=-1):
    return jax.nn.softmax(x, axis=axis)
def _gelu(x):
    return jax.nn.gelu(x, approximate=True)
def _silu(x):
    return jax.nn.silu(x)
def _sigmoid(x):
    return jax.nn.sigmoid(x)
def _layernorm(x, axis=-1, eps=1e-5):
    m = jnp.mean(x, axis=axis, keepdims=True)
    v = jnp.var(x, axis=axis, keepdims=True)
    return (x - m) / jnp.sqrt(v + eps)
def _scatter_add(tgt, idx, src, axis=0):
    return tgt.at[idx].add(src)
def _segment_sum(src, seg, n):
    return jax.ops.segment_sum(src, seg, n)

kernel_name = 'mk_conv_preact_d4_conv_nchw32_e1967a'

def setup_inputs(seed: int = 0):
    np.random.seed(seed)
    _w = jnp.asarray
    def _rec_inputs():
        import jax
        import jax.numpy as jnp
        _gk = jax.random.key(seed)
        x = -7.109e-05 + 0.9999 * jax.random.normal(jax.random.fold_in(_gk, 1), (16, 32, 256, 256), jnp.float32)
        return x
    x = _rec_inputs()
    def _L0_conv_setup():
        import jax, jax.numpy as jnp
        import numpy as np
        N_ROWS, N_COLS = (4, 4)
        EPS = 1e-05
        key = jax.random.key(seed)
        ks = jax.random.split(key, 4)
        x = jax.random.normal(ks[0], (32, 32, 256, 256), dtype=jnp.float32)
        gamma = jnp.ones((32,), dtype=jnp.float32)
        beta = jnp.zeros((32,), dtype=jnp.float32)
        prelu_a = jnp.full((1,), 0.25, dtype=jnp.float32)
        conv_w = jax.random.normal(ks[1], (32, 32, 3, 3), dtype=jnp.float32) * (1.0 / np.sqrt(32 * 9))
        conv_b = jax.random.normal(ks[2], (32,), dtype=jnp.float32) * 0.01
        return {'x': x, 'gamma': gamma, 'beta': beta, 'prelu_a': prelu_a, 'conv_w': conv_w, 'conv_b': conv_b}
    _L0_conv_all = _L0_conv_setup()
    _L0_conv_in = {k: v for k, v in _L0_conv_all.items() if k in ('gamma', 'beta', 'prelu_a', 'conv_w', 'conv_b', )}
    del _L0_conv_all

    def _L1_conv_setup():
        import jax, jax.numpy as jnp
        import numpy as np
        STRIDE = 1
        PADDING = 1
        key = jax.random.key(seed)
        k1, k2, k3 = jax.random.split(key, 3)
        x = jax.random.normal(k1, (8, 32, 512, 512), dtype=jnp.float32)
        W = jax.random.normal(k2, (32, 32, 3, 3), dtype=jnp.float32)
        b = jax.random.normal(k3, (32,), dtype=jnp.float32)
        return {'x': x, 'W': W, 'b': b}
    _L1_conv_all = _L1_conv_setup()
    _L1_conv_in = {k: v for k, v in _L1_conv_all.items() if k in ('W', 'b', )}
    del _L1_conv_all

    def _L2_conv_setup():
        import jax, jax.numpy as jnp
        import numpy as np
        PI = np.pi
        EPS_A = 0.0001

        def _frft_1d(x, a):
            a = jnp.clip(a, EPS_A, 2.0 - EPS_A)
            N = x.shape[-1]
            x = jnp.fft.ifftshift(x, axes=-1)
            alpha = a * PI / 2.0
            tan_a2 = jnp.tan(a * PI / 4.0)
            sin_a = jnp.sin(alpha)
            n = jnp.arange(N, dtype=jnp.float32) - N // 2
            c1 = jnp.exp(-1j * PI * n ** 2 * tan_a2 / N)
            c2 = jnp.exp(-1j * PI * n ** 2 / (N * sin_a))
            y = jnp.fft.ifft(jnp.fft.fft(x * c1, axis=-1) * c2, axis=-1)
            y = y * c1 / jnp.sqrt(jnp.abs(sin_a) + 1e-12)
            return jnp.fft.fftshift(y, axes=-1)

        def _frft2d(x, ax, ay):
            y = _frft_1d(x, ay)
            y = jnp.swapaxes(_frft_1d(jnp.swapaxes(y, -1, -2), ax), -1, -2)
            return y
        key = jax.random.key(seed)
        kx, = jax.random.split(key, 1)
        B, C, H, W = (4, 32, 256, 256)
        x = jax.random.normal(kx, (B, C, H, W), dtype=jnp.float32)
        alpha = jnp.float32(0.5)
        w = jnp.zeros((C, 2 * C), dtype=jnp.float32)
        w = w.at[jnp.arange(C), jnp.arange(C)].set(1.0)
        return {'x': x, 'alpha': alpha, 'w': w}
    _L2_conv_all = _L2_conv_setup()
    _L2_conv_in = {k: v for k, v in _L2_conv_all.items() if k in ('alpha', 'w', )}
    del _L2_conv_all

    def _L3_conv_setup():
        import jax, jax.numpy as jnp
        import numpy as np
        B, C, H, W, K = (16, 32, 256, 256, 3)
        OFFSET_RANGE_FACTOR = 1.0
        BN_EPS = 1e-05

        def _grid_sample_bilinear(img, grid):
            Bq, Cq, Hq, Wq = img.shape
            gx = (grid[..., 0] + 1.0) * 0.5 * (Wq - 1)
            gy = (grid[..., 1] + 1.0) * 0.5 * (Hq - 1)
            x0 = jnp.floor(gx)
            y0 = jnp.floor(gy)
            wx1 = gx - x0
            wy1 = gy - y0

            def corner(yi, xi, w):
                yc = jnp.clip(yi, 0, Hq - 1).astype(jnp.int32)
                xc = jnp.clip(xi, 0, Wq - 1).astype(jnp.int32)
                valid = (yi >= 0) & (yi <= Hq - 1) & (xi >= 0) & (xi <= Wq - 1)
                v = jax.vmap(lambda im, y, x: im[:, y, x])(img, yc, xc)
                return v * (w * valid.astype(img.dtype))[:, None, :, :]
            return corner(y0, x0, (1 - wy1) * (1 - wx1)) + corner(y0, x0 + 1, (1 - wy1) * wx1) + corner(y0 + 1, x0, wy1 * (1 - wx1)) + corner(y0 + 1, x0 + 1, wy1 * wx1)
        key = jax.random.key(seed)
        ks = jax.random.split(key, 5)
        s = lambda k, shp: jax.random.normal(k, shp, jnp.float32) * 0.1
        return dict(x=jax.random.normal(ks[0], (B, C, H, W), jnp.float32), proj_w=s(ks[1], (C, C, 1, 1)), proj_b=jnp.zeros((C,), jnp.float32), dw_w=s(ks[2], (C, 1, K, K)), dw_b=jnp.zeros((C,), jnp.float32), bn_g=jnp.ones((C,), jnp.float32), bn_b=jnp.zeros((C,), jnp.float32), off_w=s(ks[3], (2, C, 1, 1)))
    _L3_conv_all = _L3_conv_setup()
    _L3_conv_in = {k: v for k, v in _L3_conv_all.items() if k in ('proj_w', 'proj_b', 'dw_w', 'dw_b', 'bn_g', 'bn_b', 'off_w', )}
    del _L3_conv_all

    return {
        "x": x,
        "L0_conv_gamma": _L0_conv_in["gamma"],
        "L0_conv_beta": _L0_conv_in["beta"],
        "L0_conv_prelu_a": _L0_conv_in["prelu_a"],
        "L0_conv_conv_w": _L0_conv_in["conv_w"],
        "L0_conv_conv_b": _L0_conv_in["conv_b"],
        "L1_conv_W": _L1_conv_in["W"],
        "L1_conv_b": _L1_conv_in["b"],
        "L2_conv_alpha": _L2_conv_in["alpha"],
        "L2_conv_w": _L2_conv_in["w"],
        "L3_conv_proj_w": _L3_conv_in["proj_w"],
        "L3_conv_proj_b": _L3_conv_in["proj_b"],
        "L3_conv_dw_w": _L3_conv_in["dw_w"],
        "L3_conv_dw_b": _L3_conv_in["dw_b"],
        "L3_conv_bn_g": _L3_conv_in["bn_g"],
        "L3_conv_bn_b": _L3_conv_in["bn_b"],
        "L3_conv_off_w": _L3_conv_in["off_w"],
    }

def reference(x, L0_conv_gamma, L0_conv_beta, L0_conv_prelu_a, L0_conv_conv_w, L0_conv_conv_b, L1_conv_W, L1_conv_b, L2_conv_alpha, L2_conv_w, L3_conv_proj_w, L3_conv_proj_b, L3_conv_dw_w, L3_conv_dw_b, L3_conv_bn_g, L3_conv_bn_b, L3_conv_off_w):
    import jax
    import jax.numpy as jnp
    def _L0_conv_ref(x, gamma, beta, prelu_a, conv_w, conv_b):
        import jax, jax.numpy as jnp
        import numpy as np
        N_ROWS, N_COLS = (4, 4)
        EPS = 1e-05
        B, C, H, W = x.shape
        rh, rw = (H // N_ROWS, W // N_COLS)
        xr = x.reshape(B, C, N_ROWS, rh, N_COLS, rw)
        xr = xr.transpose(2, 4, 0, 1, 3, 5).reshape(N_ROWS * N_COLS, B, C, rh, rw)
        mean = xr.mean(axis=(1, 3, 4), keepdims=True)
        var = jnp.mean((xr - mean) ** 2, axis=(1, 3, 4), keepdims=True)
        g = gamma[None, None, :, None, None]
        b = beta[None, None, :, None, None]
        y = (xr - mean) * jax.lax.rsqrt(var + EPS) * g + b
        y = jnp.where(y > 0, y, prelu_a[0] * y)
        yb = y.reshape(N_ROWS * N_COLS * B, C, rh, rw)
        out = jax.lax.conv_general_dilated(yb, conv_w, window_strides=(1, 1), padding=((1, 1), (1, 1)), dimension_numbers=('NCHW', 'OIHW', 'NCHW'))
        out = out + conv_b[None, :, None, None]
        out = out.reshape(N_ROWS, N_COLS, B, C, rh, rw)
        out = out.transpose(2, 3, 0, 4, 1, 5).reshape(B, C, H, W)
        return out

    def _L1_conv_ref(x, W, b):
        import jax, jax.numpy as jnp
        import numpy as np
        STRIDE = 1
        PADDING = 1
        out = jax.lax.conv_general_dilated(x, W, window_strides=(STRIDE, STRIDE), padding=((PADDING, PADDING), (PADDING, PADDING)), dimension_numbers=('NCHW', 'OIHW', 'NCHW'))
        out = out + b[None, :, None, None]
        return out

    def _L2_conv_ref(x, alpha, w):
        import jax, jax.numpy as jnp
        import numpy as np
        PI = np.pi
        EPS_A = 0.0001

        def _frft_1d(x, a):
            a = jnp.clip(a, EPS_A, 2.0 - EPS_A)
            N = x.shape[-1]
            x = jnp.fft.ifftshift(x, axes=-1)
            alpha = a * PI / 2.0
            tan_a2 = jnp.tan(a * PI / 4.0)
            sin_a = jnp.sin(alpha)
            n = jnp.arange(N, dtype=jnp.float32) - N // 2
            c1 = jnp.exp(-1j * PI * n ** 2 * tan_a2 / N)
            c2 = jnp.exp(-1j * PI * n ** 2 / (N * sin_a))
            y = jnp.fft.ifft(jnp.fft.fft(x * c1, axis=-1) * c2, axis=-1)
            y = y * c1 / jnp.sqrt(jnp.abs(sin_a) + 1e-12)
            return jnp.fft.fftshift(y, axes=-1)

        def _frft2d(x, ax, ay):
            y = _frft_1d(x, ay)
            y = jnp.swapaxes(_frft_1d(jnp.swapaxes(y, -1, -2), ax), -1, -2)
            return y
        Xc = x.astype(jnp.complex64)
        Y = _frft2d(Xc, alpha, alpha)
        out = jnp.concatenate([jnp.abs(Y), jnp.angle(Y) / PI], axis=1)
        out = jnp.einsum('oc,bchw->bohw', w, out)
        return out.astype(x.dtype)

    def _L3_conv_ref(x, proj_w, proj_b, dw_w, dw_b, bn_g, bn_b, off_w):
        import jax, jax.numpy as jnp
        import numpy as np
        B, C, H, W, K = (16, 32, 256, 256, 3)
        OFFSET_RANGE_FACTOR = 1.0
        BN_EPS = 1e-05

        def _grid_sample_bilinear(img, grid):
            Bq, Cq, Hq, Wq = img.shape
            gx = (grid[..., 0] + 1.0) * 0.5 * (Wq - 1)
            gy = (grid[..., 1] + 1.0) * 0.5 * (Hq - 1)
            x0 = jnp.floor(gx)
            y0 = jnp.floor(gy)
            wx1 = gx - x0
            wy1 = gy - y0

            def corner(yi, xi, w):
                yc = jnp.clip(yi, 0, Hq - 1).astype(jnp.int32)
                xc = jnp.clip(xi, 0, Wq - 1).astype(jnp.int32)
                valid = (yi >= 0) & (yi <= Hq - 1) & (xi >= 0) & (xi <= Wq - 1)
                v = jax.vmap(lambda im, y, x: im[:, y, x])(img, yc, xc)
                return v * (w * valid.astype(img.dtype))[:, None, :, :]
            return corner(y0, x0, (1 - wy1) * (1 - wx1)) + corner(y0, x0 + 1, (1 - wy1) * wx1) + corner(y0 + 1, x0, wy1 * (1 - wx1)) + corner(y0 + 1, x0 + 1, wy1 * wx1)
        out = jnp.einsum('oi,bihw->bohw', proj_w[:, :, 0, 0], x) + proj_b[None, :, None, None]
        h = jax.lax.conv_general_dilated(out, dw_w, window_strides=(1, 1), padding=((1, 1), (1, 1)), feature_group_count=C, dimension_numbers=('NCHW', 'OIHW', 'NCHW'))
        h = h + dw_b[None, :, None, None]
        mean = h.mean(axis=(0, 2, 3))
        var = h.var(axis=(0, 2, 3))
        h = (h - mean[None, :, None, None]) * jax.lax.rsqrt(var + BN_EPS)[None, :, None, None]
        h = h * bn_g[None, :, None, None] + bn_b[None, :, None, None]
        h = jax.nn.gelu(h, approximate=False)
        offset = jnp.einsum('oc,bchw->bohw', off_w[:, :, 0, 0], h)
        Hk, Wk = (offset.shape[2], offset.shape[3])
        rng = jnp.array([1.0 / (Hk - 1.0), 1.0 / (Wk - 1.0)], jnp.float32)
        offset = jnp.tanh(offset) * rng[None, :, None, None] * OFFSET_RANGE_FACTOR
        offset = jnp.transpose(offset, (0, 2, 3, 1))
        ry = jnp.linspace(0.5, Hk - 0.5, Hk, dtype=jnp.float32) / (Hk - 1.0) * 2.0 - 1.0
        rx = jnp.linspace(0.5, Wk - 0.5, Wk, dtype=jnp.float32) / (Wk - 1.0) * 2.0 - 1.0
        ref = jnp.stack(jnp.meshgrid(ry, rx, indexing='ij'), axis=-1)
        pos = offset + ref[None]
        grid = pos[..., ::-1]
        return _grid_sample_bilinear(x, grid)

    def _gn(v, G=16, eps=1e-5):
        B_, C_, H_, W_ = v.shape
        g = v.reshape(B_, G, C_ // G, H_, W_)
        m = jnp.mean(g, axis=(2, 3, 4), keepdims=True)
        s = jnp.var(g, axis=(2, 3, 4), keepdims=True)
        return ((g - m) / jnp.sqrt(s + eps)).reshape(v.shape)

    def _ln_c(v, eps=1e-6):
        m = jnp.mean(v, axis=1, keepdims=True)
        s = jnp.var(v, axis=1, keepdims=True)
        return (v - m) / jnp.sqrt(s + eps)

    def _ln_t(v, eps=1e-5):
        m = jnp.mean(v, axis=-1, keepdims=True)
        s = jnp.var(v, axis=-1, keepdims=True)
        return (v - m) / jnp.sqrt(s + eps)

    def _to_tokens(v):
        B_, C_, H_, W_ = v.shape
        return v.reshape(B_, C_, H_ * W_).transpose(0, 2, 1)
    def _from_tokens(t, like):
        B_, C_, H_, W_ = like.shape
        return t.transpose(0, 2, 1).reshape(B_, C_, H_, W_)

    x = x + _L0_conv_ref(_gn(x), L0_conv_gamma, L0_conv_beta, L0_conv_prelu_a, L0_conv_conv_w, L0_conv_conv_b)
    x = x + _L1_conv_ref(_gn(x), L1_conv_W, L1_conv_b)
    x = x + _L2_conv_ref(_gn(x), L2_conv_alpha, L2_conv_w)
    x = x + _L3_conv_ref(_gn(x), L3_conv_proj_w, L3_conv_proj_b, L3_conv_dw_w, L3_conv_dw_b, L3_conv_bn_g, L3_conv_bn_b, L3_conv_off_w)
    return x


_drawn_inputs = setup_inputs


def setup_inputs(seed=0):
    import zlib

    import numpy as np

    out = dict(_drawn_inputs(seed))
    spreads = {'L0_conv_gamma': (1.0, 0.2),
     'L0_conv_beta': (0.0, 0.1),
     'L3_conv_proj_b': (0.0, 2.0),
     'L3_conv_dw_b': (0.0, 2.0),
     'L3_conv_bn_g': (1.0, 0.6),
     'L3_conv_bn_b': (0.0, 2.0)}
    factors = {'L0_conv_conv_b': 7.31,
     'L3_conv_proj_w': 4.348,
     'L3_conv_dw_w': 4.458,
     'L3_conv_off_w': 3.568}
    for name, (base, spread) in spreads.items():
        noise = np.random.default_rng([zlib.crc32(name.encode()), seed]).standard_normal(out[name].shape)
        drawn = base * np.exp(spread * noise) if base else spread * noise
        out[name] = jnp.asarray(drawn.astype(out[name].dtype))
    for name, factor in factors.items():
        out[name] = (out[name] * factor).astype(out[name].dtype)
    return out
```

```python
from contextlib import ExitStack

import numpy as np
import concourse.bass as bass
from concourse import mybir

FP32 = mybir.dt.float32
U32 = mybir.dt.uint32
ALU = mybir.AluOpType
ACT = mybir.ActivationFunctionType
AX = mybir.AxisListType

C = 32
H = W = 256
R = 4
G = H // R
P = R * C
GS = 8
STRIPS = G // GS
PAIRS = STRIPS // 2
NT = 4
TC = 4
TW = W // TC
CI = 4
EPS = 1e-5
BIG = 12582912.0

(COL_GAMMA, COL_BETA, COL_PRELU, COL_B0, COL_B1, COL_DWB, COL_BNG, COL_BNB, COL_ALPHA, NCOL) = range(10)


class Chain:

    def __init__(self, eng, sem):
        self.eng, self.sem, self.n = eng, sem, 0

    def __call__(self, ins):
        self.n += 1
        ins.then_inc(self.sem, 1)
        self.eng.wait_ge(self.sem, self.n)


def build(nc, B, t):
    with ExitStack() as ctx:
        def sb(name, shape, dt=FP32):
            return ctx.enter_context(nc.sbuf_tensor(name, shape, dt))

        cols = sb("cols", [P, NCOL])
        gavg = sb("gavg", [P, P])
        cavg = sb("cavg", [P, P])
        scale = sb("scale", [P, B])
        bias = sb("bias", [P, B])
        mean = sb("mean", [P, B])
        stats = sb("stats", [P, B, 2])
        dram = {}
        for name, shape in (("x1", [B, P, G + 2, W]), ("x2", [R, B * C, G, W]), ("mag", [R, B * C, G, W]),
                            ("ang", [R, B * C, G, W]), ("x3", [B, P, G + 2, W]), ("h", [B, P, G, W])):
            dram[name] = nc.dram_tensor(name + "_dram", shape, FP32, kind="Internal").ap()
        keep = dict(cols=cols, gavg=gavg, cavg=cavg, scale=scale, bias=bias, mean=mean, stats=stats)
        with ExitStack() as tiles:
            tile_scale = tiles.enter_context(nc.sbuf_tensor("tile_scale", [P, B, PAIRS * TC], FP32))
            tile_bias = tiles.enter_context(nc.sbuf_tensor("tile_bias", [P, B, PAIRS * TC], FP32))
            x_stats(nc, B, t, keep, tile_scale, tile_bias)
            conv_phase(nc, B, t, keep, "l0", t["xr"], dram["x1"], t["w0m"], t["w0e"], COL_B0,
                       tile_scale, tile_bias)
        group_scalars(nc, B, keep, "n1", dram["x1"])
        conv_phase(nc, B, t, keep, "l1", dram["x1"], dram["x2"], t["w1m"], t["w1e"], COL_B1)
        group_scalars(nc, B, keep, "n2", None)
        fourier_phase(nc, B, t, keep, dram["x2"], dram["mag"], dram["ang"])
        mix_phase(nc, B, t, keep, dram["x2"], dram["mag"], dram["ang"], dram["x3"])
        group_scalars(nc, B, keep, "n3", dram["x3"])
        conv_phase(nc, B, t, keep, "l3", dram["x3"], dram["h"], t["w3m"], t["w3e"], COL_DWB)
        sample_phase(nc, B, t, keep, dram["x3"], dram["h"], t["out"])


def x_stats(nc, B, t, keep, tile_scale, tile_bias):
    NTILE = PAIRS * TC
    with ExitStack() as ctx:
        sb = lambda name, shape: ctx.enter_context(nc.sbuf_tensor("xs_" + name, shape, FP32))
        raw = [sb(f"raw{k}", [P, GS, W]) for k in range(2)]
        st = [sb(f"st{k}", [P, TC, 6]) for k in range(2)]
        raw_stats = sb("raw_stats", [P, B * PAIRS * 2, TC, 6])
        tile_stats = sb("tile_stats", [P, B, NTILE, 2])
        a = sb("a", [P, B, NTILE])
        b2 = sb("b2", [P, B, NTILE])
        small = sb("small", [P, 4, B])
        tl = sb("tl", [P, 4, NTILE])
        ps = ctx.enter_context(nc.psum_tensor("xs_ps", [P, 4, 512], FP32))
        sem = lambda name: ctx.enter_context(nc.semaphore("xs_" + name))
        const_in, chain, to_pe, from_pe, to_act, from_act = (
            sem("const_in"), sem("chain"), sem("to_pe"), sem("from_pe"), sem("to_act"), sem("from_act"))
        loaded = [sem(f"loaded{k}") for k in range(2)]
        freed = [sem(f"freed{k}") for k in range(2)]
        stat_done = sem("stat_done")
        block = ctx.enter_context(nc.Block())

        @block.sync
        def _(sp):
            sp.dma_start(keep["cols"][:, :], t["cols"]).then_inc(const_in, 16)
            sp.dma_start(keep["gavg"][:, :], t["gavg"]).then_inc(const_in, 16)
            sp.dma_start(keep["cavg"][:, :], t["cavg"]).then_inc(const_in, 16)
            with sp.Fori(0, B * PAIRS) as m:
                b, s = sp.snap(m // PAIRS), sp.snap(m % PAIRS)
                for k in range(2):
                    sp.wait_ge(freed[k], m + 1)
                    sp.dma_start(raw[k][:, :, :],
                                 t["xr"][bass.ds(b, 1), :, bass.ds(s * (2 * GS) + (1 + k * GS), GS), :]
                                 .rearrange("a p g w -> (a p) g w")).then_inc(loaded[k], 16)

        @block.vector
        def _(dve):
            for k in range(2):
                dve.sem_inc(freed[k], 1)
            with dve.Fori(0, B * PAIRS) as m:
                for k in range(2):
                    dve.wait_ge(loaded[k], (m + 1) * 16)
                    for c in range(TC):
                        ins = nc.vector.bn_stats(st[k][:, c, :], raw[k][:, :, c * TW:(c + 1) * TW])
                    ins.then_inc(freed[k], 1)
                    dve.wait_ge(freed[k], m + 2)
                    nc.vector.tensor_scalar(
                        raw_stats[:, bass.ds(m * 2 + k, 1), :, :]
                        .rearrange("p n c v -> p (n c) v"),
                        st[k][:, :, :], 1.0, None, ALU.mult).then_inc(stat_done, 1)
            dve.wait_ge(stat_done, B * PAIRS * 2)
            link = Chain(dve, chain)
            for b in range(B):
                for n in range(NTILE):
                    ins = nc.vector.bn_aggr(tile_stats[:, b, n, :],
                                            raw_stats[:, 2 * (b * PAIRS + n // TC):2 * (b * PAIRS + n // TC) + 2, n % TC, :])
            link(ins)
            mu, var = tile_stats[:, :, :, 0], tile_stats[:, :, :, 1]
            link(nc.vector.reduce_sum(small[:, 0, :], mu, axis=AX.X))
            dve.wait_ge(const_in, 48)
            nc.vector.tensor_scalar(small[:, 0, :], small[:, 0, :], 1.0 / NTILE, None, ALU.mult).then_inc(to_pe, 1)
            dve.wait_ge(from_pe, 1)
            link(nc.vector.tensor_copy(small[:, 1, :], ps[:, 0, 0:B]))
            gm = small[:, 1, :].unsqueeze(2).to_broadcast([P, B, NTILE])
            link(nc.vector.tensor_tensor(a[:, :, :], mu, gm, ALU.subtract))
            link(nc.vector.tensor_tensor(b2[:, :, :], a[:, :, :], a[:, :, :], ALU.mult))
            link(nc.vector.tensor_tensor(b2[:, :, :], b2[:, :, :], var, ALU.add))
            link(nc.vector.reduce_sum(small[:, 2, :], b2[:, :, :], axis=AX.X))
            nc.vector.tensor_scalar(small[:, 2, :], small[:, 2, :], 1.0 / NTILE, None, ALU.mult).then_inc(to_pe, 1)
            dve.wait_ge(from_pe, 2)
            nc.vector.tensor_scalar(small[:, 2, :], ps[:, 1, 0:B], EPS, None, ALU.add).then_inc(to_act, 1)
            dve.wait_ge(from_act, 1)
            link(nc.vector.reciprocal(small[:, 3, :], small[:, 2, :]))
            gs = small[:, 3, :].unsqueeze(2).to_broadcast([P, B, NTILE])
            link(nc.vector.tensor_tensor(a[:, :, :], a[:, :, :], gs, ALU.mult))
            link(nc.vector.reduce_sum(tl[:, 0, :], a[:, :, :].rearrange("p b n -> p n b"), axis=AX.X))
            nc.vector.tensor_scalar(tl[:, 0, :], tl[:, 0, :], 1.0 / B, None, ALU.mult).then_inc(to_pe, 1)
            dve.wait_ge(from_pe, 3)
            link(nc.vector.tensor_copy(tl[:, 1, :], ps[:, 2, 0:NTILE]))
            tm = tl[:, 1, :].unsqueeze(1).to_broadcast([P, B, NTILE])
            link(nc.vector.tensor_tensor(a[:, :, :], a[:, :, :], tm, ALU.subtract))
            link(nc.vector.tensor_tensor(a[:, :, :], a[:, :, :], a[:, :, :], ALU.mult))
            link(nc.vector.tensor_tensor(b2[:, :, :], var, gs, ALU.mult))
            link(nc.vector.tensor_tensor(b2[:, :, :], b2[:, :, :], gs, ALU.mult))
            link(nc.vector.tensor_tensor(a[:, :, :], a[:, :, :], b2[:, :, :], ALU.add))
            link(nc.vector.reduce_sum(tl[:, 2, :], a[:, :, :].rearrange("p b n -> p n b"), axis=AX.X))
            nc.vector.tensor_scalar(tl[:, 2, :], tl[:, 2, :], 1.0 / B, None, ALU.mult).then_inc(to_pe, 1)
            dve.wait_ge(from_pe, 4)
            nc.vector.tensor_scalar(tl[:, 2, :], ps[:, 3, 0:NTILE], EPS, None, ALU.add).then_inc(to_act, 1)
            dve.wait_ge(from_act, 2)
            link(nc.vector.reciprocal(tl[:, 3, :], tl[:, 2, :]))
            link(nc.vector.tensor_scalar(tl[:, 3, :], tl[:, 3, :], keep["cols"][:, COL_GAMMA:COL_GAMMA + 1], None, ALU.mult))
            link(nc.vector.tensor_tensor(tl[:, 1, :], tl[:, 1, :], tl[:, 3, :], ALU.mult))
            link(nc.vector.tensor_scalar(tl[:, 1, :], tl[:, 1, :], -1.0, keep["cols"][:, COL_BETA:COL_BETA + 1],
                                         ALU.mult, ALU.add))
            link(nc.vector.tensor_tensor(tile_scale[:, :, :], gs,
                                         tl[:, 3, :].unsqueeze(1).to_broadcast([P, B, NTILE]), ALU.mult))
            link(nc.vector.tensor_tensor(b2[:, :, :], tile_scale[:, :, :], gm, ALU.mult))
            link(nc.vector.tensor_tensor(tile_bias[:, :, :], tl[:, 1, :].unsqueeze(1).to_broadcast([P, B, NTILE]),
                                         b2[:, :, :], ALU.subtract))

        @block.tensor
        def _(pe):
            for n, (lhs, rhs, cnt) in enumerate(((keep["gavg"], small[:, 0, :], B), (keep["gavg"], small[:, 2, :], B),
                                                 (keep["cavg"], tl[:, 0, :], NTILE), (keep["cavg"], tl[:, 2, :], NTILE))):
                pe.wait_ge(to_pe, n + 1)
                nc.tensor.matmul(ps[:, n, 0:cnt], lhs[:, :], rhs, start=True, stop=True).then_inc(from_pe, 1)

        @block.scalar
        def _(act):
            act.wait_ge(to_act, 1)
            nc.scalar.activation(small[:, 2, :], small[:, 2, :], ACT.Sqrt).then_inc(from_act, 1)
            act.wait_ge(to_act, 2)
            nc.scalar.activation(tl[:, 2, :], tl[:, 2, :], ACT.Sqrt).then_inc(from_act, 1)


def group_scalars(nc, B, keep, tag, padded):
    with ExitStack() as ctx:
        sb = lambda name, shape: ctx.enter_context(nc.sbuf_tensor(f"{tag}_{name}", shape, FP32))
        a, b2, m0 = sb("a", [P, B]), sb("b2", [P, B]), sb("m0", [P, B])
        rows = sb("rows", [P, B, W])
        ps = ctx.enter_context(nc.psum_tensor(f"{tag}_ps", [P, 2, 512], FP32))
        sem = lambda name: ctx.enter_context(nc.semaphore(f"{tag}_{name}"))
        chain, to_pe, from_pe, to_act, from_act, mean_ready, rows_out = (
            sem("chain"), sem("to_pe"), sem("from_pe"), sem("to_act"), sem("from_act"), sem("mean_ready"), sem("rows_out"))
        block = ctx.enter_context(nc.Block())
        mu, var = keep["stats"][:, :, 0], keep["stats"][:, :, 1]

        @block.vector
        def _(dve):
            link = Chain(dve, chain)
            nc.vector.tensor_copy(m0[:, :], mu).then_inc(to_pe, 1)
            dve.wait_ge(from_pe, 1)
            link(nc.vector.tensor_copy(keep["mean"][:, :], ps[:, 0, 0:B]))
            if padded is not None:
                nc.vector.tensor_copy(rows[:, :, :], keep["mean"][:, :].unsqueeze(2).to_broadcast([P, B, W])) \
                    .then_inc(mean_ready, 1)
            link(nc.vector.tensor_tensor(a[:, :], mu, keep["mean"][:, :], ALU.subtract))
            link(nc.vector.tensor_tensor(a[:, :], a[:, :], a[:, :], ALU.mult))
            nc.vector.tensor_tensor(b2[:, :], a[:, :], var, ALU.add).then_inc(to_pe, 1)
            dve.wait_ge(from_pe, 2)
            nc.vector.tensor_scalar(a[:, :], ps[:, 1, 0:B], EPS, None, ALU.add).then_inc(to_act, 1)
            dve.wait_ge(from_act, 1)
            link(nc.vector.reciprocal(keep["scale"][:, :], a[:, :]))
            link(nc.vector.tensor_tensor(b2[:, :], keep["mean"][:, :], keep["scale"][:, :], ALU.mult))
            link(nc.vector.tensor_scalar(keep["bias"][:, :], b2[:, :], -1.0, None, ALU.mult))

        @block.tensor
        def _(pe):
            pe.wait_ge(to_pe, 1)
            nc.tensor.matmul(ps[:, 0, 0:B], keep["gavg"][:, :], m0[:, :], start=True, stop=True).then_inc(from_pe, 1)
            pe.wait_ge(to_pe, 2)
            nc.tensor.matmul(ps[:, 1, 0:B], keep["gavg"][:, :], b2[:, :], start=True, stop=True).then_inc(from_pe, 1)

        @block.scalar
        def _(act):
            act.wait_ge(to_act, 1)
            nc.scalar.activation(a[:, :], a[:, :], ACT.Sqrt).then_inc(from_act, 1)

        if padded is not None:
            @block.sync
            def _(sp):
                sp.wait_ge(mean_ready, 1)
                for g in (0, G + 1):
                    sp.dma_start(padded[:, :, g, :].rearrange("b p w -> p b w"), rows[:, :, :]).then_inc(rows_out, 16)
                sp.wait_ge(rows_out, 32)


def conv_phase(nc, B, t, keep, tag, src, dst, w_main, w_edge, bias_col, tile_scale=None, tile_bias=None):
    tiled = tag == "l0"
    fused = tag == "l3"
    PW = TC * (TW + 2) if tiled else W + 2
    EK = 2 * C + 6 if fused else 2 * C
    with ExitStack() as ctx:
        def sb(name, shape):
            return ctx.enter_context(nc.sbuf_tensor(f"{tag}_{name}", shape, FP32))

        def sem(name):
            return ctx.enter_context(nc.semaphore(f"{tag}_{name}"))

        wm, we = sb("wm", [P, 3, P]), sb("we", [EK, 3, P])
        if fused:
            fm, fe = sb("fm", [P, 3, P]), sb("fe", [EK, 3, P])
        raw = [sb(f"raw{k}", [P, GS, W]) for k in range(2)]
        eraw = [sb(f"eraw{k}", [2 * C, GS, W]) for k in range(2)]
        pad = [sb(f"pad{k}", [P, GS, PW]) for k in range(2)]
        epad = [sb(f"epad{k}", [EK, GS, PW]) for k in range(2)]
        res = [sb(f"res{k}", [P, GS * W]) for k in range(2)]
        strip_stats = [sb(f"sst{k}", [P, NT, 6]) for k in range(2)]
        all_stats = sb("all_stats", [P, B * STRIPS, NT * 6])
        if tiled:
            neg_scale, neg_bias = sb("nsc", [P, B * PAIRS * TC]), sb("nbi", [P, B * PAIRS * TC])
            neg_slope = sb("nslope", [P, 1])
            low = [sb(f"low{k}", [P, GS, W]) for k in range(2)]
            elow = [sb(f"elow{k}", [2 * C, GS, W]) for k in range(2)]
            high = [sb(f"high{k}", [P, GS, W]) for k in range(2)]
            ehigh = [sb(f"ehigh{k}", [2 * C, GS, W]) for k in range(2)]
        ps = ctx.enter_context(nc.psum_tensor(f"{tag}_ps", [P, 2, NT, 512], FP32))
        w_in, w_ready = sem("w_in"), sem("w_ready")
        loaded = [sem(f"loaded{k}") for k in range(2)]
        split = [sem(f"split{k}") for k in range(2)]
        pad_ready = [sem(f"pad_ready{k}") for k in range(2)]
        tile_done = [sem(f"tile_done{k}") for k in range(2)]
        res_ready = [sem(f"res_ready{k}") for k in range(2)]
        stored = [sem(f"stored{k}") for k in range(2)]
        stat_w = [sem(f"stat_w{k}") for k in range(2)]
        stat_c, setup, act_passed = sem("stat_c"), sem("setup"), sem("act_passed")
        block = ctx.enter_context(nc.Block())

        if tiled:
            tile_scale2 = tile_scale[:, :, :].rearrange("p b n -> p (b n)")
            tile_bias2 = tile_bias[:, :, :].rearrange("p b n -> p (b n)")

        loads = 4 if fused else 3
        store_inc = 16 * (R if tag == "l1" else 1)

        def padded_cols(tile, part, gs, c=None):
            if tiled:
                lo = c * (TW + 2) + 1
                return tile[part, gs, lo:lo + TW]
            return tile[part, gs, 1:W + 1]

        @block.sync
        def _(sp):
            if fused:
                for dst_t, src_t in ((wm, w_main[0]), (we, w_edge[0]), (fm, w_main[1]), (fe, w_edge[1])):
                    sp.dma_start(dst_t[:, :, :], src_t).then_inc(w_in, 16)
            else:
                sp.dma_start(wm[:, :, :], w_main).then_inc(w_in, 16)
                sp.dma_start(we[:, :, :], w_edge).then_inc(w_in, 16)

            def load(b, g0, k):
                at = lambda parts, off: (src[bass.ds(b, 1), parts, bass.ds(g0 + off, GS), :]
                                         .rearrange("a p g w -> (a p) g w"))
                sp.dma_start(raw[k][:, :, :], at(slice(0, P), 1)).then_inc(loaded[k], 16)
                sp.dma_start(eraw[k][0:C, :, :], at(slice(P - C, P), 0)).then_inc(loaded[k], 16)
                sp.dma_start(eraw[k][C:2 * C, :, :], at(slice(0, C), 2)).then_inc(loaded[k], 16)
                if fused:
                    sp.dma_start(epad[k][2 * C:EK, :, :], t["ind"][:, bass.ds(g0, GS), :]).then_inc(loaded[k], 16)

            def store(b, g0, k):
                if tag == "l1":
                    for r in range(R):
                        o = dst[r, bass.ds(b * C, C), bass.ds(g0, GS), :].rearrange("c g w -> c (g w)")
                        sp.dma_start(o, res[k][r * C:(r + 1) * C, :]).then_inc(stored[k], 16)
                else:
                    o = (dst[bass.ds(b, 1), :, bass.ds(g0 + (0 if fused else 1), GS), :]
                         .rearrange("a p g w -> (a p) (g w)"))
                    sp.dma_start(o, res[k][:, :]).then_inc(stored[k], 16)

            if fused:
                sp.wait_ge(w_ready, 1)
            for k in range(2):
                load(0, k * GS, k)
            with sp.Fori(1, B * PAIRS) as m:
                b, g0 = sp.snap(m // PAIRS), sp.snap(m % PAIRS * (2 * GS))
                old_b, old_g0 = sp.snap((m - 1) // PAIRS), sp.snap((m - 1) % PAIRS * (2 * GS))
                for k in range(2):
                    sp.wait_ge(res_ready[k], m * NT + 1)
                    store(old_b, old_g0 + k * GS, k)
                    load(b, g0 + k * GS, k)
            for k in range(2):
                sp.wait_ge(res_ready[k], B * PAIRS * NT + 1)
                store(B - 1, (STRIPS - 2 + k) * GS, k)
                sp.wait_ge(stored[k], B * PAIRS * store_inc + 1)

        @block.scalar
        def _(act):
            act.wait_ge(w_ready, 1)
            with act.Fori(0, B * PAIRS) as m:
                b, s = act.snap(m // PAIRS), act.snap(m % PAIRS)
                for k in range(2):
                    act.wait_ge(loaded[k], (m + 1) * (16 * loads))
                    if tiled:
                        act.wait_ge(pad_ready[k], m + 1)
                        act.sem_inc(act_passed, 1)
                        for c in range(TC):
                            n = m * TC + c
                            cs = slice(c * TW, (c + 1) * TW)
                            for (o, i) in ((high, raw), (ehigh, eraw)):
                                q = P if i is raw else 2 * C
                                nc.scalar.activation(o[k][0:q, :, cs], i[k][0:q, :, cs], ACT.Relu,
                                                     bias=tile_bias2[0:q, bass.ds(n, 1)],
                                                     scale=tile_scale2[0:q, bass.ds(n, 1)])
                            for (o, i) in ((low, raw), (elow, eraw)):
                                q = P if i is raw else 2 * C
                                ins = nc.scalar.activation(o[k][0:q, :, cs], i[k][0:q, :, cs], ACT.Relu,
                                                           bias=neg_bias[0:q, bass.ds(n, 1)],
                                                           scale=neg_scale[0:q, bass.ds(n, 1)])
                        ins.then_inc(split[k], 1)
                    else:
                        act.wait_ge(tile_done[k], m * NT + 1)
                        act.sem_inc(act_passed, 1)
                        nc.scalar.activation(pad[k][:, :, 1:W + 1], raw[k][:, :, :], ACT.Identity,
                                             bias=keep["bias"][:, bass.ds(b, 1)],
                                             scale=keep["scale"][:, bass.ds(b, 1)])
                        nc.scalar.activation(epad[k][0:2 * C, :, 1:W + 1], eraw[k][:, :, :], ACT.Identity,
                                             bias=keep["bias"][0:2 * C, bass.ds(b, 1)],
                                             scale=keep["scale"][0:2 * C, bass.ds(b, 1)]) \
                            .then_inc(pad_ready[k], 1)

        def window(tile, rows, j, kx):
            if tiled:
                return tile[0:rows, 2 * j:2 * j + 2, :].rearrange("p g (c w) -> p (g c) w", c=TC)[:, :, kx:kx + TW]
            return tile[0:rows, 2 * j:2 * j + 2, kx:kx + W]

        @block.tensor
        def _(pe):
            pe.wait_ge(w_ready, 1)
            with pe.Fori(0, B * PAIRS) as m:
                for k in range(2):
                    pe.wait_ge(pad_ready[k], m + 2)
                    pe.wait_ge(res_ready[k], m * NT + 1)
                    for j in range(NT):
                        for kx in range(3):
                            nc.tensor.matmul(ps[:, k, j, :], wm[:, kx, :], window(pad[k], P, j, kx),
                                             start=(kx == 0), stop=False)
                        for kx in range(3):
                            ins = nc.tensor.matmul(ps[:, k, j, :], we[:, kx, :], window(epad[k], EK, j, kx),
                                                   start=False, stop=(kx == 2))
                        ins.then_inc(tile_done[k], 1)

        @block.vector
        def _(dve):
            link = Chain(dve, setup)
            for k in range(2):
                link(nc.vector.memset(pad[k][:, :, :], 0.0))
                link(nc.vector.memset(epad[k][:, :, :], 0.0))
            if tiled:
                link(nc.vector.tensor_scalar(neg_scale[:, :], tile_scale2, -1.0, None, ALU.mult))
                link(nc.vector.tensor_scalar(neg_bias[:, :], tile_bias2, -1.0, None, ALU.mult))
                link(nc.vector.tensor_scalar(neg_slope[:, :], keep["cols"][:, COL_PRELU:COL_PRELU + 1], -1.0, None, ALU.mult))
            if fused:
                dve.wait_ge(w_in, 64)
                link(nc.vector.tensor_tensor(wm[:, :, :], wm[:, :, :], fm[:, :, :], ALU.mult))
                link(nc.vector.tensor_tensor(we[:, :, :], we[:, :, :], fe[:, :, :], ALU.mult))
            else:
                dve.wait_ge(w_in, 32)
            for k in range(2):
                for x in (pad_ready[k], tile_done[k], res_ready[k], stored[k]):
                    dve.sem_inc(x, 1)
            dve.sem_inc(w_ready, 1)

            def combine(m, k):
                dve.wait_ge(split[k], m + 1)
                dve.wait_ge(tile_done[k], m * NT + 1)
                for c in range(TC):
                    cs = slice(c * TW, (c + 1) * TW)
                    for (o, hi, lo, part, gs) in (
                            (pad, high, low, slice(0, P), slice(0, GS)),
                            (epad, ehigh, elow, slice(0, C), slice(1 - k, GS)),
                            (epad, ehigh, elow, slice(C, 2 * C), slice(0, GS - k))):
                        ins = nc.vector.scalar_tensor_tensor(
                            padded_cols(o[k], part, gs, c), lo[k][part, gs, cs], neg_slope[part, :],
                            hi[k][part, gs, cs], ALU.mult, ALU.add)
                ins.then_inc(pad_ready[k], 1)

            def finish(m, k):
                dve.wait_ge(stored[k], m * store_inc + 1)
                for j in range(NT):
                    dve.wait_ge(tile_done[k], m * NT + (j + 2))
                    o = res[k][:, j * 512:(j + 1) * 512]
                    if fused:
                        ins = nc.vector.tensor_scalar(o, ps[:, k, j, :], keep["cols"][:, bias_col:bias_col + 1],
                                                      None, ALU.add)
                    else:
                        ins = nc.vector.scalar_tensor_tensor(
                            o, ps[:, k, j, :], keep["cols"][:, bias_col:bias_col + 1],
                            raw[k][:, 2 * j:2 * j + 2, :].rearrange("p g w -> p (g w)"), ALU.add, ALU.add)
                    ins.then_inc(res_ready[k], 1)
                dve.wait_ge(res_ready[k], (m + 1) * NT + 1)
                for j in range(NT):
                    ins = nc.vector.bn_stats(strip_stats[k][:, j, :], res[k][:, j * 512:(j + 1) * 512])
                ins.then_inc(stat_w[k], 1)
                dve.wait_ge(stat_w[k], m + 1)
                nc.vector.tensor_scalar(
                    all_stats[:, bass.ds(m * 2 + k, 1), :].rearrange("p n v -> p (n v)"),
                    strip_stats[k][:, :, :].rearrange("p n v -> p (n v)"), 1.0, None, ALU.mult).then_inc(stat_c, 1)

            def pair(m, last):
                if tiled:
                    combine(m, 1)
                finish(m, 0)
                if tiled and not last:
                    combine(m + 1, 0)
                finish(m, 1)

            if tiled:
                combine(0, 0)
            with dve.Fori(0, B * PAIRS - 1) as m:
                pair(m, False)
            pair(B * PAIRS - 1, True)
            dve.wait_ge(stat_c, B * STRIPS)
            for b in range(B):
                ins = nc.vector.bn_aggr(keep["stats"][:, b, :], all_stats[:, b * STRIPS:(b + 1) * STRIPS, :]
                                        .rearrange("p n v -> p (n v)"))


def mix_phase(nc, B, t, keep, x2, mag, ang, x3):
    with ExitStack() as ctx:
        sb = lambda name, shape: ctx.enter_context(nc.sbuf_tensor("mx_" + name, shape, FP32))
        sem = lambda name: ctx.enter_context(nc.semaphore("mx_" + name))
        wmag, wang = sb("wmag", [P, P]), sb("wang", [P, P])
        raw = [sb(f"raw{k}", [P, GS * W]) for k in range(2)]
        mg = [sb(f"mg{k}", [P, GS * W]) for k in range(2)]
        an = [sb(f"an{k}", [P, GS * W]) for k in range(2)]
        res = [sb(f"res{k}", [P, GS * W]) for k in range(2)]
        strip_stats = [sb(f"sst{k}", [P, NT, 6]) for k in range(2)]
        all_stats = sb("all_stats", [P, B * STRIPS, NT * 6])
        ps = ctx.enter_context(nc.psum_tensor("mx_ps", [P, 2, NT, 512], FP32))
        w_in, w_ready, stat_c, setup = sem("w_in"), sem("w_ready"), sem("stat_c"), sem("setup")
        loaded = [sem(f"loaded{k}") for k in range(2)]
        tile_done = [sem(f"tile_done{k}") for k in range(2)]
        res_ready = [sem(f"res_ready{k}") for k in range(2)]
        stored = [sem(f"stored{k}") for k in range(2)]
        stat_w = [sem(f"stat_w{k}") for k in range(2)]
        block = ctx.enter_context(nc.Block())

        @block.sync
        def _(sp):
            sp.dma_start(wmag[:, :], t["wmag"]).then_inc(w_in, 16)
            sp.dma_start(wang[:, :], t["wang"]).then_inc(w_in, 16)

            def load(b, g0, k):
                for buf, src in ((mg, mag), (an, ang), (raw, x2)):
                    for r in range(R):
                        o = src[r, bass.ds(b * C, C), bass.ds(g0, GS), :].rearrange("c g w -> c (g w)")
                        sp.dma_start(buf[k][r * C:(r + 1) * C, :], o).then_inc(loaded[k], 16)

            def store(b, g0, k):
                o = x3[bass.ds(b, 1), :, bass.ds(g0 + 1, GS), :].rearrange("a p g w -> (a p) (g w)")
                sp.dma_start(o, res[k][:, :]).then_inc(stored[k], 16)

            for k in range(2):
                load(0, k * GS, k)
            with sp.Fori(1, B * PAIRS) as m:
                b, g0 = sp.snap(m // PAIRS), sp.snap(m % PAIRS * (2 * GS))
                old_b, old_g0 = sp.snap((m - 1) // PAIRS), sp.snap((m - 1) % PAIRS * (2 * GS))
                for k in range(2):
                    sp.wait_ge(res_ready[k], m * NT + 1)
                    store(old_b, old_g0 + k * GS, k)
                    load(b, g0 + k * GS, k)
            for k in range(2):
                sp.wait_ge(res_ready[k], B * PAIRS * NT + 1)
                store(B - 1, (STRIPS - 2 + k) * GS, k)
                sp.wait_ge(stored[k], B * PAIRS * 16 + 1)

        @block.tensor
        def _(pe):
            pe.wait_ge(w_ready, 1)
            with pe.Fori(0, B * PAIRS) as m:
                for k in range(2):
                    pe.wait_ge(loaded[k], (m + 1) * (16 * 3 * R))
                    pe.wait_ge(res_ready[k], m * NT + 1)
                    for j in range(NT):
                        cs = slice(j * 512, (j + 1) * 512)
                        nc.tensor.matmul(ps[:, k, j, :], wmag[:, :], mg[k][:, cs], start=True, stop=False)
                        nc.tensor.matmul(ps[:, k, j, :], wang[:, :], an[k][:, cs], start=False, stop=True) \
                            .then_inc(tile_done[k], 1)

        @block.vector
        def _(dve):
            link = Chain(dve, setup)
            dve.wait_ge(w_in, 32)
            link(nc.vector.tensor_scalar(wang[:, :], wang[:, :], 2.0, None, ALU.mult))
            for k in range(2):
                for x in (tile_done[k], res_ready[k], stored[k]):
                    dve.sem_inc(x, 1)
            dve.sem_inc(w_ready, 1)
            with dve.Fori(0, B * PAIRS) as m:
                for k in range(2):
                    dve.wait_ge(stored[k], m * 16 + 1)
                    for j in range(NT):
                        cs = slice(j * 512, (j + 1) * 512)
                        dve.wait_ge(tile_done[k], m * NT + (j + 2))
                        nc.vector.tensor_tensor(res[k][:, cs], ps[:, k, j, :], raw[k][:, cs], ALU.add) \
                            .then_inc(res_ready[k], 1)
                    dve.wait_ge(res_ready[k], (m + 1) * NT + 1)
                    for j in range(NT):
                        ins = nc.vector.bn_stats(strip_stats[k][:, j, :], res[k][:, j * 512:(j + 1) * 512])
                    ins.then_inc(stat_w[k], 1)
                    dve.wait_ge(stat_w[k], m + 1)
                    nc.vector.tensor_scalar(
                        all_stats[:, bass.ds(m * 2 + k, 1), :].rearrange("p n v -> p (n v)"),
                        strip_stats[k][:, :, :].rearrange("p n v -> p (n v)"), 1.0, None, ALU.mult).then_inc(stat_c, 1)
            dve.wait_ge(stat_c, B * STRIPS)
            for b in range(B):
                nc.vector.bn_aggr(keep["stats"][:, b, :], all_stats[:, b * STRIPS:(b + 1) * STRIPS, :]
                                  .rearrange("p n v -> p (n v)"))


def sample_phase(nc, B, t, keep, x3, h, out):
    with ExitStack() as ctx:
        sb = lambda name, shape: ctx.enter_context(nc.sbuf_tensor("sp_" + name, shape, FP32))
        sem = lambda name: ctx.enter_context(nc.semaphore("sp_" + name))
        woff = sb("woff", [P, 2, P])
        x0 = [sb(f"x0{k}", [P, GS, W + 1]) for k in range(2)]
        x1 = [sb(f"x1{k}", [P, GS, W + 1]) for k in range(2)]
        hb = [sb(f"h{k}", [P, GS * W]) for k in range(2)]
        th = [sb(f"th{k}", [P, 2, GS, W]) for k in range(2)]
        base = [sb(f"base{k}", [P, GS, W]) for k in range(2)]
        dy = [sb(f"dy{k}", [P, GS, W + 1]) for k in range(2)]
        dx = [sb(f"dx{k}", [P, GS, W]) for k in range(2)]
        dxy = [sb(f"dxy{k}", [P, GS, W]) for k in range(2)]
        u, v = sb("u", [P, GS, W]), sb("v", [P, GS, W])
        res = [sb(f"res{k}", [P, GS, W]) for k in range(2)]
        half_scale, one_scale = sb("half_scale", [P, B]), sb("one_scale", [P, B])
        bn = sb("bn", [P, 8])
        bs = sb("bs", [P, B])
        ps = ctx.enter_context(nc.psum_tensor("sp_ps", [P, 2, NT, 512], FP32))
        act_passed = sem("act_passed")
        w_in, chain, to_pe, from_pe, to_act, from_act, bn_ready = (
            sem("w_in"), sem("chain"), sem("to_pe"), sem("from_pe"), sem("to_act"), sem("from_act"), sem("bn_ready"))
        h_loaded = [sem(f"h_loaded{k}") for k in range(2)]
        x_loaded = [sem(f"x_loaded{k}") for k in range(2)]
        gelu_done = [sem(f"gelu_done{k}") for k in range(2)]
        off_done = [sem(f"off_done{k}") for k in range(2)]
        th_ready = [sem(f"th_ready{k}") for k in range(2)]
        edge_ready = [sem(f"edge_ready{k}") for k in range(2)]
        res_ready = [sem(f"res_ready{k}") for k in range(2)]
        stored = [sem(f"stored{k}") for k in range(2)]
        diff, base_ready, dve_step = sem("diff"), sem("base_ready"), sem("dve_step")
        block = ctx.enter_context(nc.Block())

        @block.sync
        def _(sp):
            sp.dma_start(woff[:, :, :], t["woff"]).then_inc(w_in, 16)

            def load(b, s, k):
                g0 = s * (2 * GS) + k * GS
                at = lambda parts, off: (x3[bass.ds(b, 1), parts, bass.ds(g0 + off, GS), :]
                                         .rearrange("a p g w -> (a p) g w"))
                sp.dma_start(hb[k][:, :], h[bass.ds(b, 1), :, bass.ds(g0, GS), :]
                             .rearrange("a p g w -> (a p) (g w)")).then_inc(h_loaded[k], 16)
                sp.dma_start(x0[k][:, :, 0:W], at(slice(0, P), 1)).then_inc(x_loaded[k], 16)
                sp.dma_start(x1[k][0:P - C, :, 0:W], at(slice(C, P), 1)).then_inc(x_loaded[k], 16)
                sp.dma_start(x1[k][P - C:P, :, 0:W], at(slice(0, C), 2)).then_inc(x_loaded[k], 16)

            def store(n, k):
                sp.dma_start(out[bass.ds(n, 1), :, :].rearrange("n p v -> (n p) v"),
                             res[k][:, :, :].rearrange("p g w -> p (g w)")).then_inc(stored[k], 16)

            for k in range(2):
                load(0, 0, k)
            with sp.Fori(1, B * PAIRS) as m:
                b, s, n = sp.snap(m // PAIRS), sp.snap(m % PAIRS), sp.snap(m * 2)
                for k in range(2):
                    sp.wait_ge(res_ready[k], m)
                    store(n + (k - 2), k)
                    load(b, s, k)
            for k in range(2):
                sp.wait_ge(res_ready[k], B * PAIRS)
                store(B * STRIPS - 2 + k, k)
                sp.wait_ge(stored[k], B * PAIRS * 16 + 1)

        @block.gpsimd
        def _(pool):
            with pool.Fori(0, B * PAIRS) as m:
                b, s = pool.snap(m // PAIRS), pool.snap(m % PAIRS)
                for k in range(2):
                    n = m * 2 + k
                    pool.wait_ge(x_loaded[k], (m + 1) * 48)
                    pool.wait_ge(edge_ready[k], m + 1)
                    nc.gpsimd.tensor_tensor(dy[k][:, :, :], x1[k][:, :, :], x0[k][:, :, :], ALU.subtract).then_inc(diff, 1)
                    nc.gpsimd.tensor_tensor(dx[k][:, :, :], x0[k][:, :, 1:W + 1], x0[k][:, :, 0:W], ALU.subtract) \
                        .then_inc(diff, 1)
                    pool.wait_ge(diff, n * 3 + 1)
                    nc.gpsimd.tensor_tensor(dxy[k][:, :, :], dy[k][:, :, 1:W + 1], dy[k][:, :, 0:W], ALU.subtract) \
                        .then_inc(diff, 1)

        @block.scalar
        def _(act):
            act.wait_ge(to_act, 1)
            nc.scalar.activation(bn[:, 4:5], bn[:, 4:5], ACT.Sqrt).then_inc(from_act, 1)
            act.wait_ge(bn_ready, 1)
            with act.Fori(0, B * PAIRS) as m:
                b, s = act.snap(m // PAIRS), act.snap(m % PAIRS)
                for k in range(2):
                    n = m * 2 + k
                    act.wait_ge(h_loaded[k], (m + 1) * 16)
                    nc.scalar.activation(hb[k][:, :], hb[k][:, :], ACT.Gelu, bias=bn[:, 6:7], scale=bn[:, 5:6]) \
                        .then_inc(gelu_done[k], 1)
                    act.wait_ge(x_loaded[k], (m + 1) * 48)
                    act.sem_inc(act_passed, 1)
                    nc.scalar.activation(base[k][:, :, :], x0[k][:, :, 0:W], ACT.Identity,
                                         bias=keep["bias"][:, bass.ds(b, 1)],
                                         scale=one_scale[:, bass.ds(b, 1)]).then_inc(base_ready, 1)
                    act.wait_ge(off_done[k], m + 1)
                    nc.scalar.activation(th[k][:, :, :, :].rearrange("p a g w -> p (a g w)"),
                                         ps[:, :, :, :].rearrange("p a j n -> p (a j n)"), ACT.Tanh) \
                        .then_inc(th_ready[k], 1)

        @block.tensor
        def _(pe):
            pe.wait_ge(to_pe, 1)
            nc.tensor.matmul(ps[:, 0, 0, 0:1], keep["cavg"][:, :], bn[:, 0:1], start=True, stop=True).then_inc(from_pe, 1)
            pe.wait_ge(to_pe, 2)
            nc.tensor.matmul(ps[:, 0, 1, 0:1], keep["cavg"][:, :], bn[:, 2:3], start=True, stop=True).then_inc(from_pe, 1)
            pe.wait_ge(bn_ready, 1)
            pe.wait_ge(w_in, 16)
            with pe.Fori(0, B * PAIRS) as m:
                for k in range(2):
                    pe.wait_ge(gelu_done[k], m + 1)
                    pe.wait_ge(th_ready[1 - k], m + 1)
                    for a in range(2):
                        for j in range(NT):
                            ins = nc.tensor.matmul(ps[:, a, j, :], woff[:, a, :], hb[k][:, j * 512:(j + 1) * 512],
                                                   start=True, stop=True)
                    ins.then_inc(off_done[k], 1)

        @block.vector
        def _(dve):
            link = Chain(dve, chain)
            mu, var = keep["stats"][:, :, 0], keep["stats"][:, :, 1]
            link(nc.vector.reduce_sum(bn[:, 1:2], mu, axis=AX.X))
            nc.vector.tensor_scalar(bn[:, 0:1], bn[:, 1:2], 1.0 / B, None, ALU.mult).then_inc(to_pe, 1)
            dve.wait_ge(from_pe, 1)
            link(nc.vector.tensor_copy(bn[:, 3:4], ps[:, 0, 0, 0:1]))
            link(nc.vector.tensor_scalar(bs[:, :], mu, bn[:, 3:4], None, ALU.subtract))
            link(nc.vector.tensor_tensor(bs[:, :], bs[:, :], bs[:, :], ALU.mult))
            link(nc.vector.tensor_tensor(bs[:, :], bs[:, :], var, ALU.add))
            link(nc.vector.reduce_sum(bn[:, 1:2], bs[:, :], axis=AX.X))
            nc.vector.tensor_scalar(bn[:, 2:3], bn[:, 1:2], 1.0 / B, None, ALU.mult).then_inc(to_pe, 1)
            dve.wait_ge(from_pe, 2)
            nc.vector.tensor_scalar(bn[:, 4:5], ps[:, 0, 1, 0:1], EPS, None, ALU.add).then_inc(to_act, 1)
            dve.wait_ge(from_act, 1)
            link(nc.vector.reciprocal(bn[:, 7:8], bn[:, 4:5]))
            link(nc.vector.tensor_scalar(bn[:, 5:6], bn[:, 7:8], keep["cols"][:, COL_BNG:COL_BNG + 1], None, ALU.mult))
            link(nc.vector.tensor_tensor(bn[:, 7:8], bn[:, 3:4], bn[:, 5:6], ALU.mult))
            link(nc.vector.tensor_tensor(bn[:, 6:7], keep["cols"][:, COL_BNB:COL_BNB + 1], bn[:, 7:8], ALU.subtract))
            link(nc.vector.tensor_scalar(half_scale[:, :], keep["scale"][:, :], 0.5, None, ALU.mult))
            link(nc.vector.tensor_scalar(one_scale[:, :], keep["scale"][:, :], 1.0, None, ALU.add))
            for k in range(2):
                dve.sem_inc(stored[k], 1)
            dve.sem_inc(th_ready[1], 1)
            dve.sem_inc(bn_ready, 1)

            def edges(b, m, k):
                dve.wait_ge(x_loaded[k], (m + 1) * 48)
                for tile in (x0, x1):
                    ins = nc.vector.tensor_scalar(tile[k][:, :, W:W + 1], tile[k][:, :, 0:1], 0.0,
                                                  keep["mean"][:, bass.ds(b, 1)], ALU.mult, ALU.add)
                ins.then_inc(edge_ready[k], 1)

            with dve.Fori(0, B * PAIRS) as m:
                b, s = dve.snap(m // PAIRS), dve.snap(m % PAIRS)
                for k in range(2):
                    n = m * 2 + k
                    edges(b, m, k)
                    ty, tx = th[k][:, 0, :, :], th[k][:, 1, :, :]
                    dve.wait_ge(diff, (n + 1) * 3)
                    dve.wait_ge(th_ready[k], m + (1 + k))
                    nc.vector.scalar_tensor_tensor(u[:, :, :], ty, 1.0, dxy[k][:, :, :], ALU.add, ALU.mult) \
                        .then_inc(dve_step, 1)
                    nc.vector.scalar_tensor_tensor(v[:, :, :], ty, 1.0, dy[k][:, :, 0:W], ALU.add, ALU.mult) \
                        .then_inc(dve_step, 1)
                    dve.wait_ge(dve_step, n * 5 + 1)
                    nc.vector.scalar_tensor_tensor(u[:, :, :], u[:, :, :], 0.5, dx[k][:, :, :], ALU.mult, ALU.add) \
                        .then_inc(dve_step, 1)
                    dve.wait_ge(dve_step, n * 5 + 3)
                    nc.vector.scalar_tensor_tensor(u[:, :, :], tx, 1.0, u[:, :, :], ALU.add, ALU.mult) \
                        .then_inc(dve_step, 1)
                    dve.wait_ge(dve_step, n * 5 + 4)
                    nc.vector.tensor_tensor(u[:, :, :], u[:, :, :], v[:, :, :], ALU.add).then_inc(dve_step, 1)
                    dve.wait_ge(dve_step, n * 5 + 5)
                    dve.wait_ge(base_ready, n + 1)
                    dve.wait_ge(stored[k], m * 16 + 1)
                    nc.vector.scalar_tensor_tensor(
                        res[k][:, :, :], u[:, :, :], half_scale[:, bass.ds(b, 1)], base[k][:, :, :],
                        ALU.mult, ALU.add).then_inc(res_ready[k], 1)


def fourier_phase(nc, B, t, keep, x2, mag, ang):
    NG = B * C // CI
    K2 = 2 * W
    NPH = 2 * W + 6
    with ExitStack() as ctx:
        def sb(name, shape):
            return ctx.enter_context(nc.sbuf_tensor("ft_" + name, shape, FP32))

        def sem(name):
            return ctx.enter_context(nc.semaphore("ft_" + name))

        row_m = sb("row_m", [P, 2, 2, W])
        col_m = sb("col_m", [P, 2, 3, W])
        img_scale, img_bias = sb("img_scale", [P, B * C]), sb("img_bias", [P, B * C])
        fourier_tables(nc, B, t, keep, row_m, col_m, img_scale, img_bias, NPH)
        raw = [sb(f"raw{k}", [P, 2, CI, W]) for k in range(2)]
        xn = [sb(f"xn{k}", [P, 2, CI, W]) for k in range(2)]
        zt = [sb(f"zt{k}", [P, 2, K2]) for k in range(2)]
        y = [sb(f"y{k}", [P, CI, 2, K2]) for k in range(2)]
        sq = sb("sq", [P, CI, 2, K2])
        d = sb("d", [P, CI * 2, W])
        e = sb("e", [P, CI * 2, W])
        turn = sb("turn", [P, CI * 2, W])
        mg = [sb(f"mg{k}", [P, CI, 2, W]) for k in range(2)]
        an = [sb(f"an{k}", [P, CI, 2, W]) for k in range(2)]
        ps_a = ctx.enter_context(nc.psum_tensor("ft_psa", [P, 2, 2, 512], FP32))
        ps_b = ctx.enter_context(nc.psum_tensor("ft_psb", [P, 2, 2, 512], FP32))
        loaded = [sem(f"loaded{k}") for k in range(2)]
        stored = [sem(f"stored{k}") for k in range(2)]
        xn_ready, a_done, z_done, b_done, y_done = (
            sem("xn_ready"), sem("a_done"), sem("z_done"), sem("b_done"), sem("y_done"))
        sq_done, sum_done, mag_done, ratio_done, atan_done, post_done, step = (
            sem("sq_done"), sem("sum_done"), sem("mag_done"), sem("ratio_done"), sem("atan_done"), sem("post_done"),
            sem("step"))
        block = ctx.enter_context(nc.Block())

        def groups(eng, part):
            part(0, 0, 0, True, False)
            with eng.Fori(0, NG // 2 - 1) as v:
                part(v * 2 + 1, 1, v, False, False)
                part(v * 2 + 2, 0, v + 1, False, False)
            part(NG - 1, 1, NG // 2 - 1, False, True)

        @block.sync
        def _(sp):
            def load(c0, k):
                for r in range(R):
                    sp.dma_start(raw[k][64 * (r % 2):64 * (r % 2) + 64, r // 2, :, :],
                                 x2[r, bass.ds(c0, CI), :, :].rearrange("c g w -> g c w")).then_inc(loaded[k], 16)


            def store(c0, k):
                for buf, dst in ((mg, mag), (an, ang)):
                    for r in range(R):
                        sp.dma_start(dst[r, bass.ds(c0, CI), :, :].rearrange("c g w -> g c w"),
                                     buf[k][64 * (r % 2):64 * (r % 2) + 64, :, r // 2, :]).then_inc(stored[k], 16)

            load(0, 0)
            load(CI, 1)
            sp.wait_ge(xn_ready, 1)
            load(2 * CI, 0)
            with sp.Fori(0, NG // 2 - 2) as v:
                c0 = sp.snap(v * (2 * CI))
                sp.wait_ge(xn_ready, v * 2 + 2)
                load(c0 + 3 * CI, 1)
                sp.wait_ge(post_done, v * 2 + 3)
                store(c0, 0)
                sp.wait_ge(xn_ready, v * 2 + 3)
                load(c0 + 4 * CI, 0)
                sp.wait_ge(post_done, v * 2 + 4)
                store(c0 + CI, 1)
            sp.wait_ge(xn_ready, NG - 2)
            load((NG - 1) * CI, 1)
            for q in range(NG - 4, NG):
                sp.wait_ge(post_done, q + 3)
                store(q * CI, q % 2)
            for k in range(2):
                sp.wait_ge(stored[k], NG // 2 * (16 * 2 * R) + 1)

        @block.tensor
        def _(pe):
            def rows(k, i):
                for wc in range(2):
                    for hc in range(2):
                        ins = nc.tensor.matmul(ps_a[:, i % 2, wc, :], xn[k][:, hc, i, wc * P:(wc + 1) * P],
                                               row_m[:, hc, :, :].rearrange("p a w -> p (a w)"),
                                               start=(hc == 0), stop=(hc == 1))
                ins.then_inc(a_done, 1)

            def part(q, k, u, first, last):
                for i in range(CI):
                    n = q * CI + i
                    if not (last and i == CI - 1):
                        if i == CI - 1:
                            pe.wait_ge(xn_ready, q + 2)
                        pe.wait_ge(z_done, n + 1)
                        rows(k if i < CI - 1 else 1 - k, (i + 1) % CI)
                    pe.wait_ge(z_done, n + 2)
                    pe.wait_ge(y_done, n + 1)
                    for pc in range(2):
                        for wc in range(2):
                            for im in range(2):
                                ins = nc.tensor.matmul(
                                    ps_b[:, i % 2, pc, :], zt[i % 2][:, wc, im * W + pc * P:im * W + (pc + 1) * P],
                                    col_m[:, wc, 1 - im:3 - im, :].rearrange("p a w -> p (a w)"),
                                    start=(wc == 0 and im == 0), stop=(wc == 1 and im == 1))
                    ins.then_inc(b_done, 1)

            pe.wait_ge(xn_ready, 1)
            rows(0, 0)
            groups(pe, part)

        def whole(ap):
            return ap.rearrange("p a w -> p (a w)")

        def halves(ap, part):
            return ap.rearrange("p i c w -> p (i c) w")[:, :, part * W:(part + 1) * W]

        @block.scalar
        def _(act):
            for x, credit in ((z_done, 1), (y_done, 2)):
                act.sem_inc(x, credit)

            def take_z(n, i):
                act.wait_ge(a_done, n + 1)
                act.wait_ge(b_done, n + 1)
                nc.scalar.activation(whole(zt[i % 2][:, :, :]), whole(ps_a[:, i % 2, :, :]), ACT.Identity) \
                    .then_inc(z_done, 1)

            def take_y(n, i, k, q):
                act.wait_ge(b_done, n + 3)
                if i == 0:
                    act.wait_ge(post_done, q + 1)
                nc.scalar.activation(whole(y[k][:, i, :, :]), whole(ps_b[:, i % 2, :, :]), ACT.Identity) \
                    .then_inc(y_done, 1)

            def squares(q, k):
                act.wait_ge(y_done, (q + 1) * CI + 2)
                nc.scalar.activation(sq[:, :, :, :].rearrange("p i c w -> p (i c w)"),
                                     y[k][:, :, :, :].rearrange("p i c w -> p (i c w)"), ACT.Square).then_inc(sq_done, 1)

            def root(q, k, u):
                act.wait_ge(stored[k], u * (16 * 2 * R) + 1)
                act.wait_ge(sum_done, q + 1)
                nc.scalar.activation(mg[k][:, :, :, :].rearrange("p i c w -> p (i c) w"), d[:, :, :], ACT.Sqrt) \
                    .then_inc(mag_done, 1)

            def arctan(q):
                act.wait_ge(ratio_done, q + 1)
                nc.scalar.activation(e[:, :, :], d[:, :, :], ACT.Arctan).then_inc(atan_done, 1)

            def part(q, k, u, first, last):
                for i in range(CI):
                    n = q * CI + i
                    take_z(n, i)
                    if i:
                        take_y(n - 1, i - 1, k, q)
                    elif not first:
                        take_y(n - 1, CI - 1, 1 - k, q - 1)
                        squares(q - 1, 1 - k)
                    if i == 1 and not first:
                        root(q - 1, 1 - k, u - (1 - k))
                    if i == 3 and not first:
                        arctan(q - 1)

            groups(act, part)
            take_y(NG * CI - 1, CI - 1, 1, NG - 1)
            squares(NG - 1, 1)
            root(NG - 1, 1, NG // 2 - 1)
            arctan(NG - 1)

        @block.vector
        def _(dve):
            for k in range(2):
                dve.sem_inc(stored[k], 1)
            dve.sem_inc(b_done, 2)
            dve.sem_inc(post_done, 2)
            STEPS = 5

            def normalise(q, k, u):
                dve.wait_ge(loaded[k], (u + 1) * (16 * R))
                for i in range(CI):
                    ins = nc.vector.tensor_scalar(xn[k][:, :, i, :], raw[k][:, :, i, :],
                                                  img_scale[:, bass.ds(q * CI + i, 1)],
                                                  img_bias[:, bass.ds(q * CI + i, 1)], ALU.mult, ALU.add)
                ins.then_inc(xn_ready, 1)

            def angles(q, k, u):
                re, im = halves(y[k][:, :, :, :], 0), halves(y[k][:, :, :, :], 1)
                did = [0]

                def link(ins, more=None):
                    did[0] += 1
                    ins.then_inc(step, 1)
                    dve.wait_ge(step, q * STEPS + did[0])

                dve.wait_ge(post_done, q + 2)
                dve.wait_ge(sq_done, q + 1)
                nc.vector.scalar_tensor_tensor(d[:, :, :], halves(sq[:, :, :, :], 0), 1.5e-35,
                                               halves(sq[:, :, :, :], 1), ALU.add, ALU.add).then_inc(sum_done, 1)
                link(nc.vector.tensor_scalar(turn[:, :, :], im, 0.0, 0.5, ALU.is_ge, ALU.subtract))
                link(nc.vector.scalar_tensor_tensor(turn[:, :, :], re, 0.0, turn[:, :, :], ALU.is_lt, ALU.mult))
                dve.wait_ge(mag_done, q + 1)
                link(nc.vector.scalar_tensor_tensor(
                    d[:, :, :].bitcast(U32), re.bitcast(U32), 0x80000000,
                    mg[k][:, :, :, :].rearrange("p i c w -> p (i c) w").bitcast(U32), ALU.bitwise_and, ALU.bitwise_or))
                link(nc.vector.tensor_tensor(d[:, :, :], d[:, :, :], re, ALU.add))
                link(nc.vector.reciprocal(d[:, :, :], d[:, :, :]))
                nc.vector.tensor_tensor(d[:, :, :], d[:, :, :], im, ALU.mult).then_inc(ratio_done, 1)
                dve.wait_ge(ratio_done, q + 1)
                dve.wait_ge(stored[k], u * (16 * 2 * R) + 1)
                dve.wait_ge(atan_done, q + 1)
                nc.vector.scalar_tensor_tensor(an[k][:, :, :, :].rearrange("p i c w -> p (i c) w"), e[:, :, :],
                                               1.0 / np.pi, turn[:, :, :], ALU.mult, ALU.add).then_inc(post_done, 1)
                assert did[0] == STEPS


            def part(q, k, u, first, last):
                if not first:
                    angles(q - 1, 1 - k, u - (1 - k))
                if first:
                    dve.wait_ge(a_done, CI)
                    if NG > 2:
                        normalise(2, 0, 1)
                elif not last:
                    more_part(q, k, u)

            def more_part(q, k, u):
                dve.wait_ge(a_done, q * CI + CI)
                normalise(q + 2, k, u + 1)

            normalise(0, 0, 0)
            normalise(1, 1, 0)
            part(0, 0, 0, True, False)
            with dve.Fori(0, NG // 2 - 2) as v:
                part(v * 2 + 1, 1, v, False, False)
                part(v * 2 + 2, 0, v + 1, False, False)
            part(NG - 3, 1, NG // 2 - 2, False, False)
            part(NG - 2, 0, NG // 2 - 1, False, True)
            part(NG - 1, 1, NG // 2 - 1, False, True)
            angles(NG - 1, 1, NG // 2 - 1)


def fourier_tables(nc, B, t, keep, row_m, col_m, img_scale, img_bias, NPH):
    K2 = 2 * W
    with ExitStack() as ctx:
        sb = lambda name, shape: ctx.enter_context(nc.sbuf_tensor("fm_" + name, shape, FP32))
        sem = lambda name: ctx.enter_context(nc.semaphore("fm_" + name))
        dft = sb("dft", [P, 2, 4, W])
        nsq = sb("nsq", [P, NPH])
        ident = sb("ident", [C, C])
        ones = sb("ones", [C, P])
        spread = sb("spread", [C, 2, B, C])
        ph, turns, co, si = sb("ph", [P, NPH]), sb("turns", [P, NPH]), sb("co", [P, NPH]), sb("si", [P, NPH])
        rhs = sb("rhs", [P, 2, 4, 2, W])
        circ = sb("circ", [P, 2, 2, 2, W])
        dd = sb("dd", [P, 2, 2, 2, W])
        tmp = sb("tmp", [P, 2, W])
        a = sb("a", [P, 16])
        c2 = sb("c2", [P, 2, 2])
        ps = ctx.enter_context(nc.psum_tensor("fm_ps", [P, 8, 512], FP32))
        const_in, chain, to_pe, from_pe, to_act, from_act = (
            sem("const_in"), sem("chain"), sem("to_pe"), sem("from_pe"), sem("to_act"), sem("from_act"))
        block = ctx.enter_context(nc.Block())
        col = lambda n: a[:, n:n + 1]

        @block.sync
        def _(sp):
            sp.dma_start(dft[:, :, :, :], t["dft"]).then_inc(const_in, 16)
            sp.dma_start(nsq[:, :], t["nsq"]).then_inc(const_in, 16)
            sp.dma_start(ident[:, :], t["ident"]).then_inc(const_in, 16)

        @block.scalar
        def _(act):
            act.wait_ge(to_act, 1)
            nc.scalar.activation(a[:, 4:7], a[:, 1:4], ACT.Sin).then_inc(from_act, 1)
            act.wait_ge(to_act, 2)
            nc.scalar.activation(si[:, :], ph[:, :], ACT.Sin).then_inc(from_act, 1)
            nc.scalar.activation(co[:, :], ph[:, :], ACT.Sin, scale=0.5).then_inc(from_act, 1)
            act.wait_ge(to_act, 3)
            nc.scalar.activation(col(11), col(10), ACT.Sqrt).then_inc(from_act, 1)

        @block.tensor
        def _(pe):
            pe.wait_ge(to_pe, 1)
            for n in range(2):
                ins = nc.tensor.matmul(ps[:, n, 0:B * C], ones[:, :], spread[:, n, :, :].rearrange("p b c -> p (b c)"),
                                       start=True, stop=True)
            ins.then_inc(from_pe, 1)
            pe.wait_ge(to_pe, 2)
            for v in range(2):
                for pc in range(2):
                    for kk in range(4):
                        ins = nc.tensor.matmul(ps[:, 4 + 2 * v + pc, :], dft[:, v, kk, pc * P:(pc + 1) * P],
                                               rhs[:, v, kk, :, :].rearrange("p a w -> p (a w)"),
                                               start=(kk == 0), stop=(kk == 3))
            ins.then_inc(from_pe, 1)

        @block.vector
        def _(dve):
            link = Chain(dve, chain)
            dve.wait_ge(const_in, 48)
            link(nc.vector.memset(ones[:, :], 1.0))
            for n, src in enumerate((keep["scale"], keep["bias"])):
                link(nc.vector.tensor_tensor(spread[:, n, :, :], src[0:C, :].unsqueeze(2).to_broadcast([C, B, C]),
                                             ident[:, :].unsqueeze(1).to_broadcast([C, B, C]), ALU.mult))
            dve.sem_inc(to_pe, 1)
            alpha = keep["cols"][:, COL_ALPHA:COL_ALPHA + 1]
            link(nc.vector.tensor_scalar(col(0), alpha, 1e-4, float(np.float32(2.0 - 1e-4)), ALU.max, ALU.min))
            link(nc.vector.tensor_scalar(col(1), col(0), float(np.pi / 4), None, ALU.mult))
            link(nc.vector.tensor_scalar(col(2), col(1), -1.0, float(np.pi / 2), ALU.mult, ALU.add))
            link(nc.vector.tensor_scalar(col(3), col(0), float(np.pi / 2), None, ALU.mult))
            dve.sem_inc(to_act, 1)
            dve.wait_ge(from_act, 1)
            link(nc.vector.reciprocal(a[:, 8:10], a[:, 5:7]))
            link(nc.vector.tensor_tensor(col(7), col(4), col(8), ALU.mult))
            link(nc.vector.tensor_scalar(ph[:, :], nsq[:, :], float(np.pi), None, ALU.mult))
            link(nc.vector.tensor_scalar(ph[:, 0:NPH - 2], ph[:, 0:NPH - 2], col(7), 1.0 / W, ALU.mult, ALU.mult))
            link(nc.vector.tensor_scalar(ph[:, NPH - 2:NPH], ph[:, NPH - 2:NPH], col(9), 1.0 / W, ALU.mult, ALU.mult))
            link(nc.vector.tensor_scalar(turns[:, :], ph[:, :], float(0.5 / np.pi), BIG, ALU.mult, ALU.add))
            link(nc.vector.tensor_scalar(turns[:, :], turns[:, :], BIG, None, ALU.subtract))
            for part in (6.28125, float(2 * np.pi - 6.28125)):
                link(nc.vector.scalar_tensor_tensor(ph[:, :], turns[:, :], -part, ph[:, :], ALU.mult, ALU.add))
            link(nc.vector.tensor_scalar(ph[:, :], ph[:, :], 3.1415925, -3.1415925, ALU.min, ALU.max))
            dve.sem_inc(to_act, 1)
            link(nc.vector.tensor_scalar(col(13), col(6), -1.0, None, ALU.mult))
            link(nc.vector.tensor_tensor(col(10), col(6), col(13), ALU.max))
            link(nc.vector.tensor_scalar(col(10), col(10), 1e-12, None, ALU.add))
            dve.sem_inc(to_act, 1)
            dve.wait_ge(from_act, 4)
            link(nc.vector.reciprocal(col(12), col(11)))
            link(nc.vector.tensor_tensor(co[:, :], co[:, :], co[:, :], ALU.mult))
            link(nc.vector.tensor_scalar(co[:, :], co[:, :], -2.0, 1.0, ALU.mult, ALU.add))
            link(nc.vector.tensor_scalar(c2[:, 0, :], co[:, NPH - 2:NPH], 1.0 / W, None, ALU.mult))
            link(nc.vector.tensor_scalar(c2[:, 1, :], si[:, NPH - 2:NPH], -1.0 / W, None, ALU.mult))
            for v in range(2):
                for kk in range(4):
                    for im in range(2):
                        link(nc.vector.tensor_scalar(rhs[:, v, kk, im, :], dft[:, v, kk, :], c2[:, im, kk % 2:kk % 2 + 1],
                                                     None, ALU.mult))
            dve.sem_inc(to_pe, 1)
            dve.wait_ge(from_pe, 1)
            link(nc.vector.tensor_copy(img_scale[:, :], ps[:, 0, 0:B * C]))
            link(nc.vector.tensor_copy(img_bias[:, :], ps[:, 1, 0:B * C]))
            dve.wait_ge(from_pe, 2)
            for v in range(2):
                link(nc.vector.tensor_copy(circ[:, v, :, :, :].rearrange("p c a w -> p c (a w)"),
                                           ps[:, 4 + 2 * v:6 + 2 * v, :]))
            link(nc.vector.tensor_scalar(co[:, K2:K2 + 4], co[:, K2:K2 + 4], col(12), None, ALU.mult))
            link(nc.vector.tensor_scalar(si[:, K2:K2 + 4], si[:, K2:K2 + 4], col(12), None, ALU.mult))
            for v in range(2):
                cr = co[:, v * W:(v + 1) * W].unsqueeze(1).to_broadcast([P, 2, W])
                sr = si[:, v * W:(v + 1) * W].unsqueeze(1).to_broadcast([P, 2, W])
                re, im = circ[:, v, :, 0, :], circ[:, v, :, 1, :]
                link(nc.vector.tensor_tensor(dd[:, v, :, 0, :], re, cr, ALU.mult))
                link(nc.vector.tensor_tensor(tmp[:, :, :], im, sr, ALU.mult))
                link(nc.vector.tensor_tensor(dd[:, v, :, 0, :], dd[:, v, :, 0, :], tmp[:, :, :], ALU.add))
                link(nc.vector.tensor_tensor(dd[:, v, :, 1, :], im, cr, ALU.mult))
                link(nc.vector.tensor_tensor(tmp[:, :, :], re, sr, ALU.mult))
                link(nc.vector.tensor_tensor(dd[:, v, :, 1, :], dd[:, v, :, 1, :], tmp[:, :, :], ALU.subtract))
                for pc in range(2):
                    cc, sc = co[:, K2 + 2 * v + pc:K2 + 2 * v + pc + 1], si[:, K2 + 2 * v + pc:K2 + 2 * v + pc + 1]
                    o_re, o_im = ((col_m[:, pc, 1, :], col_m[:, pc, 2, :]) if v == 0 else
                                  (row_m[:, pc, 0, :], row_m[:, pc, 1, :]))
                    link(nc.vector.tensor_scalar(tmp[:, 0, :], dd[:, v, pc, 1, :], sc, None, ALU.mult))
                    link(nc.vector.scalar_tensor_tensor(o_re, dd[:, v, pc, 0, :], cc, tmp[:, 0, :], ALU.mult, ALU.add))
                    link(nc.vector.tensor_scalar(tmp[:, 1, :], dd[:, v, pc, 0, :], sc, None, ALU.mult))
                    link(nc.vector.scalar_tensor_tensor(o_im, dd[:, v, pc, 1, :], cc, tmp[:, 1, :], ALU.mult, ALU.subtract))
            link(nc.vector.tensor_scalar(col_m[:, :, 0, :], col_m[:, :, 2, :], -1.0, None, ALU.mult))


_COLS = ("L0_conv_gamma", "L0_conv_beta", "L0_conv_prelu_a", "L0_conv_conv_b", "L1_conv_b", "L3_conv_dw_b",
         "L3_conv_bn_g", "L3_conv_bn_b", "L2_conv_alpha")


def _band(w):
    main = np.zeros((R, C, 3, R, C), w.dtype)
    edge = np.zeros((2, C, 3, R, C), w.dtype)
    for r in range(R):
        for q in range(R):
            if abs(r - q) <= 1:
                main[r, :, :, q, :] = w[:, :, r - q + 1, :].transpose(1, 2, 0)
    edge[0, :, :, 0, :] = w[:, :, 0, :].transpose(1, 2, 0)
    edge[1, :, :, R - 1, :] = w[:, :, 2, :].transpose(1, 2, 0)
    return main.reshape(P, 3, P), edge.reshape(2 * C, 3, P)


def _block_diagonal(w):
    m = np.zeros((R, C, R, C), w.dtype)
    for r in range(R):
        m[r, :, r, :] = w.T
    return m.reshape(P, P)


def _constants():
    c = np.arange(P) % C
    gavg = ((c[:, None] // 2 == c[None, :] // 2) / (2.0 * R)).astype(np.float32)
    cavg = ((c[:, None] == c[None, :]) / float(R)).astype(np.float32)
    perm = np.array([R * (p % G) + p // G for p in range(H)])
    j = np.arange(W)
    dft = np.zeros((P, 2, 4, W), np.float32)
    for v, rows in enumerate((j, perm)):
        x = 2 * np.pi * ((j[:, None] * rows[None, :]) % W) / W
        dft[:, v] = np.concatenate([np.cos(x).reshape(2, P, W), np.sin(x).reshape(2, P, W)]).transpose(1, 0, 2)
    n2 = (((j + W // 2) % W) - W // 2) ** 2
    nsq = np.zeros((P, 2 * W + 6), np.float32)
    nsq[:, 0:W] = n2
    nsq[:, W:2 * W] = n2[perm]
    nsq[:, 2 * W:2 * W + 2] = n2.reshape(2, P).T
    nsq[:, 2 * W + 2:2 * W + 4] = n2[perm].reshape(2, P).T
    nsq[:, 2 * W + 4:] = ((j - W // 2) ** 2).reshape(2, P).T
    ind = np.zeros((6, G, W + 2), np.float32)
    for q in range(6):
        h = R * np.arange(G) - 1 + q
        ind[q, :, 1:W + 1] = ((h >= 0) & (h < H))[:, None]
    return dict(gavg=gavg, cavg=cavg, dft=dft, nsq=nsq, ident=np.eye(C, dtype=np.float32), ind=ind)


def layout(inputs):
    x = np.asarray(inputs["x"])
    B = x.shape[0]
    a = _constants()
    xr = np.zeros((B, R, C, G + 2, W), x.dtype)
    xr[:, :, :, 1:G + 1] = x.reshape(B, C, G, R, W).transpose(0, 3, 1, 2, 4)
    a["xr"] = xr.reshape(B, P, G + 2, W)
    cols = np.zeros((P, NCOL), np.float32)
    for n, name in enumerate(_COLS):
        v = np.asarray(inputs[name]).reshape(-1)
        cols[:, n] = np.tile(v, R) if v.size == C else v[0]
    a["cols"] = cols
    a["w0m"], a["w0e"] = _band(np.asarray(inputs["L0_conv_conv_w"]))
    a["w1m"], a["w1e"] = _band(np.asarray(inputs["L1_conv_W"]))
    pw = np.asarray(inputs["L3_conv_proj_w"])[:, :, 0, 0]
    dw = np.asarray(inputs["L3_conv_dw_w"])[:, 0]
    pb = np.asarray(inputs["L3_conv_proj_b"])
    fac_p = _band(np.broadcast_to(pw[:, :, None, None], (C, C, 3, 3)))
    fac_d = _band(np.broadcast_to(dw[:, None, :, :], (C, C, 3, 3)))
    ind_d = np.zeros((6, 3, R, C), np.float32)
    for q in range(6):
        for r in range(R):
            if 0 <= q - r <= 2:
                ind_d[q, :, r, :] = dw[:, q - r, :].T
    ind_p = np.broadcast_to(np.tile(pb, R), (6, 3, P))
    a["w3m_p"], a["w3m_d"] = fac_p[0], fac_d[0]
    a["w3e_p"] = np.concatenate([fac_p[1], ind_p])
    a["w3e_d"] = np.concatenate([fac_d[1], ind_d.reshape(6, 3, P)])
    w = np.asarray(inputs["L2_conv_w"])
    a["wmag"], a["wang"] = _block_diagonal(w[:, :C]), _block_diagonal(w[:, C:])
    off = np.asarray(inputs["L3_conv_off_w"])[:, :, 0, 0]
    a["woff"] = np.stack([_block_diagonal(np.broadcast_to(off[n], (C, C))) for n in range(2)], axis=1)
    return {k: np.ascontiguousarray(v) for k, v in a.items()}, B


def program(nc, arrays, B):
    t = {k: nc.dram_tensor("in_" + k, v.shape, mybir.dt.from_np(v.dtype), kind="ExternalInput").ap()
         for k, v in arrays.items()}
    t["w3m"], t["w3e"] = (t["w3m_p"], t["w3m_d"]), (t["w3e_p"], t["w3e_d"])
    t["out"] = nc.dram_tensor("out_0", [B * STRIPS, P, GS * W], FP32, kind="ExternalOutput").ap()
    build(nc, B, t)


def unlay(o, B):
    return np.ascontiguousarray(o.reshape(B, STRIPS, R, C, GS, W).transpose(0, 3, 1, 4, 2, 5)).reshape(B, C, H, W)


def kernel(**inputs):
    import concourse.bacc as _bacc
    from concourse.bass_utils import run_bass_kernel_spmd as _run

    arrays, B = layout(inputs)
    nc = _bacc.Bacc("TRN2", target_bir_lowering=False, num_devices=1)
    program(nc, arrays, B)
    r = _run(nc, [{"in_" + k: v for k, v in arrays.items()}], core_ids=[0])
    return unlay(r.results[0]["out_0"], B)
```

```python
from contextlib import ExitStack

import numpy as np
import concourse.bass as bass
from concourse import mybir

FP32 = mybir.dt.float32
BF16 = mybir.dt.bfloat16
U32 = mybir.dt.uint32
U16 = mybir.dt.uint16
ALU = mybir.AluOpType
ACT = mybir.ActivationFunctionType
AX = mybir.AxisListType

C = 32
H = W = 256
R = 4
G = H // R
P = R * C
GS = 8
STRIPS = G // GS
PAIRS = STRIPS // 2
NT = 4
TC = 4
TW = W // TC
CI = 4
EPS = 1e-5
BIG = 12582912.0

(COL_GAMMA, COL_BETA, COL_PRELU, COL_B0, COL_B1, COL_DWB, COL_BNG, COL_BNB, COL_ALPHA, NCOL) = range(10)


class Chain:

    def __init__(self, eng, sem, n=0):
        self.eng, self.sem, self.n = eng, sem, n

    def __call__(self, ins):
        self.n += 1
        ins.then_inc(self.sem, 1)
        self.eng.wait_ge(self.sem, self.n)


def build(nc, B, t):
    with ExitStack() as ctx:
        def sb(name, shape, dt=FP32):
            return ctx.enter_context(nc.sbuf_tensor(name, shape, dt))

        cols = sb("cols", [P, NCOL])
        gavg = sb("gavg", [P, P])
        cavg = sb("cavg", [P, P])
        scale = sb("scale", [P, B])
        bias = sb("bias", [P, B])
        mean = sb("mean", [P, B])
        stats = sb("stats", [P, B, 2])
        dram = {}
        for name, shape in (("x1", [B, P, G + 2, W]), ("x2", [R, B * C, G, W]), ("mag", [R, B * C, G, W]),
                            ("ang", [R, B * C, G, W]), ("x3", [B, P, G + 2, W]), ("h", [B, P, G, W])):
            dram[name] = nc.dram_tensor(name + "_dram", shape, FP32, kind="Internal").ap()
        keep = dict(cols=cols, gavg=gavg, cavg=cavg, scale=scale, bias=bias, mean=mean, stats=stats)
        keep["group_sems"] = [ctx.enter_context(nc.semaphore("group_" + name)) for name in
                              ("chain", "to_pe", "from_pe", "to_act", "from_act", "mean_ready", "rows_out")]
        keep["padded_turns"] = 0
        with ExitStack() as tiles:
            tile_scale = tiles.enter_context(nc.sbuf_tensor("tile_scale", [P, B, PAIRS * TC], FP32))
            tile_bias = tiles.enter_context(nc.sbuf_tensor("tile_bias", [P, B, PAIRS * TC], FP32))
            x_stats(nc, B, t, keep, tile_scale, tile_bias)
            conv_phase(nc, B, t, keep, "l0", t["xr"], dram["x1"], (t["w0"],), COL_B0, tile_scale, tile_bias)
        group_scalars(nc, B, keep, 0, dram["x1"])
        conv_phase(nc, B, t, keep, "l1", dram["x1"], dram["x2"], (t["w1"],), COL_B1)
        group_scalars(nc, B, keep, 1, None)
        fourier_phase(nc, B, t, keep, dram["x2"], dram["mag"], dram["ang"])
        mix_phase(nc, B, t, keep, dram["x2"], dram["mag"], dram["ang"], dram["x3"])
        group_scalars(nc, B, keep, 2, dram["x3"])
        conv_phase(nc, B, t, keep, "l3", dram["x3"], dram["h"], (t["w3_p"], t["w3_d"]), COL_DWB)
        sample_phase(nc, B, t, keep, dram["x3"], dram["h"], t["out"])


def x_stats(nc, B, t, keep, tile_scale, tile_bias):
    NTILE = PAIRS * TC
    with ExitStack() as ctx:
        sb = lambda name, shape: ctx.enter_context(nc.sbuf_tensor("xs_" + name, shape, FP32))
        raw = [sb(f"raw{k}", [P, GS, W]) for k in range(2)]
        st = [sb(f"st{k}", [P, TC, 6]) for k in range(2)]
        raw_stats = sb("raw_stats", [P, B * PAIRS * 2, TC, 6])
        tile_stats = sb("tile_stats", [P, B, NTILE, 2])
        a = sb("a", [P, B, NTILE])
        b2 = sb("b2", [P, B, NTILE])
        small = sb("small", [P, 4, B])
        tl = sb("tl", [P, 4, NTILE])
        ps = ctx.enter_context(nc.psum_tensor("xs_ps", [P, 4, 512], FP32))
        sem = lambda name: ctx.enter_context(nc.semaphore("xs_" + name))
        const_in, chain, to_pe, from_pe, to_act, from_act = (
            sem("const_in"), sem("chain"), sem("to_pe"), sem("from_pe"), sem("to_act"), sem("from_act"))
        loaded = [sem(f"loaded{k}") for k in range(2)]
        freed = [sem(f"freed{k}") for k in range(2)]
        stat_done = sem("stat_done")
        block = ctx.enter_context(nc.Block())

        @block.sync
        def _(sp):
            sp.dma_start(keep["cols"][:, :], t["cols"]).then_inc(const_in, 16)
            sp.dma_start(keep["gavg"][:, :], t["gavg"]).then_inc(const_in, 16)
            sp.dma_start(keep["cavg"][:, :], t["cavg"]).then_inc(const_in, 16)
            with sp.Fori(0, B * PAIRS) as m:
                b, s = sp.snap(m // PAIRS), sp.snap(m % PAIRS)
                for k in range(2):
                    sp.wait_ge(freed[k], m + 1)
                    sp.dma_start(raw[k][:, :, :],
                                 t["xr"][bass.ds(b, 1), :, bass.ds(s * (2 * GS) + (1 + k * GS), GS), :]
                                 .rearrange("a p g w -> (a p) g w")).then_inc(loaded[k], 16)

        @block.vector
        def _(dve):
            for k in range(2):
                dve.sem_inc(freed[k], 1)
            with dve.Fori(0, B * PAIRS) as m:
                for k in range(2):
                    dve.wait_ge(loaded[k], (m + 1) * 16)
                    for c in range(TC):
                        ins = nc.vector.bn_stats(st[k][:, c, :], raw[k][:, :, c * TW:(c + 1) * TW])
                    ins.then_inc(freed[k], 1)
                    dve.wait_ge(freed[k], m + 2)
                    nc.vector.tensor_scalar(
                        raw_stats[:, bass.ds(m * 2 + k, 1), :, :]
                        .rearrange("p n c v -> p (n c) v"),
                        st[k][:, :, :], 1.0, None, ALU.mult).then_inc(stat_done, 1)
            dve.wait_ge(stat_done, B * PAIRS * 2)
            link = Chain(dve, chain)
            for b in range(B):
                for n in range(NTILE):
                    ins = nc.vector.bn_aggr(tile_stats[:, b, n, :],
                                            raw_stats[:, 2 * (b * PAIRS + n // TC):2 * (b * PAIRS + n // TC) + 2, n % TC, :])
            link(ins)
            mu, var = tile_stats[:, :, :, 0], tile_stats[:, :, :, 1]
            link(nc.vector.reduce_sum(small[:, 0, :], mu, axis=AX.X))
            dve.wait_ge(const_in, 48)
            nc.vector.tensor_scalar(small[:, 0, :], small[:, 0, :], 1.0 / NTILE, None, ALU.mult).then_inc(to_pe, 1)
            dve.wait_ge(from_pe, 1)
            link(nc.vector.tensor_copy(small[:, 1, :], ps[:, 0, 0:B]))
            gm = small[:, 1, :].unsqueeze(2).to_broadcast([P, B, NTILE])
            link(nc.vector.tensor_tensor(a[:, :, :], mu, gm, ALU.subtract))
            link(nc.vector.tensor_tensor(b2[:, :, :], a[:, :, :], a[:, :, :], ALU.mult))
            link(nc.vector.tensor_tensor(b2[:, :, :], b2[:, :, :], var, ALU.add))
            link(nc.vector.reduce_sum(small[:, 2, :], b2[:, :, :], axis=AX.X))
            nc.vector.tensor_scalar(small[:, 2, :], small[:, 2, :], 1.0 / NTILE, None, ALU.mult).then_inc(to_pe, 1)
            dve.wait_ge(from_pe, 2)
            nc.vector.tensor_scalar(small[:, 2, :], ps[:, 1, 0:B], EPS, None, ALU.add).then_inc(to_act, 1)
            dve.wait_ge(from_act, 1)
            link(nc.vector.reciprocal(small[:, 3, :], small[:, 2, :]))
            gs = small[:, 3, :].unsqueeze(2).to_broadcast([P, B, NTILE])
            link(nc.vector.tensor_tensor(a[:, :, :], a[:, :, :], gs, ALU.mult))
            link(nc.vector.reduce_sum(tl[:, 0, :], a[:, :, :].rearrange("p b n -> p n b"), axis=AX.X))
            nc.vector.tensor_scalar(tl[:, 0, :], tl[:, 0, :], 1.0 / B, None, ALU.mult).then_inc(to_pe, 1)
            dve.wait_ge(from_pe, 3)
            link(nc.vector.tensor_copy(tl[:, 1, :], ps[:, 2, 0:NTILE]))
            tm = tl[:, 1, :].unsqueeze(1).to_broadcast([P, B, NTILE])
            link(nc.vector.tensor_tensor(a[:, :, :], a[:, :, :], tm, ALU.subtract))
            link(nc.vector.tensor_tensor(a[:, :, :], a[:, :, :], a[:, :, :], ALU.mult))
            link(nc.vector.tensor_tensor(b2[:, :, :], var, gs, ALU.mult))
            link(nc.vector.tensor_tensor(b2[:, :, :], b2[:, :, :], gs, ALU.mult))
            link(nc.vector.tensor_tensor(a[:, :, :], a[:, :, :], b2[:, :, :], ALU.add))
            link(nc.vector.reduce_sum(tl[:, 2, :], a[:, :, :].rearrange("p b n -> p n b"), axis=AX.X))
            nc.vector.tensor_scalar(tl[:, 2, :], tl[:, 2, :], 1.0 / B, None, ALU.mult).then_inc(to_pe, 1)
            dve.wait_ge(from_pe, 4)
            nc.vector.tensor_scalar(tl[:, 2, :], ps[:, 3, 0:NTILE], EPS, None, ALU.add).then_inc(to_act, 1)
            dve.wait_ge(from_act, 2)
            link(nc.vector.reciprocal(tl[:, 3, :], tl[:, 2, :]))
            link(nc.vector.tensor_scalar(tl[:, 3, :], tl[:, 3, :], keep["cols"][:, COL_GAMMA:COL_GAMMA + 1], None, ALU.mult))
            link(nc.vector.tensor_tensor(tl[:, 1, :], tl[:, 1, :], tl[:, 3, :], ALU.mult))
            link(nc.vector.tensor_scalar(tl[:, 1, :], tl[:, 1, :], -1.0, keep["cols"][:, COL_BETA:COL_BETA + 1],
                                         ALU.mult, ALU.add))
            link(nc.vector.tensor_tensor(tile_scale[:, :, :], gs,
                                         tl[:, 3, :].unsqueeze(1).to_broadcast([P, B, NTILE]), ALU.mult))
            link(nc.vector.tensor_tensor(b2[:, :, :], tile_scale[:, :, :], gm, ALU.mult))
            link(nc.vector.tensor_tensor(tile_bias[:, :, :], tl[:, 1, :].unsqueeze(1).to_broadcast([P, B, NTILE]),
                                         b2[:, :, :], ALU.subtract))

        @block.tensor
        def _(pe):
            for n, (lhs, rhs, cnt) in enumerate(((keep["gavg"], small[:, 0, :], B), (keep["gavg"], small[:, 2, :], B),
                                                 (keep["cavg"], tl[:, 0, :], NTILE), (keep["cavg"], tl[:, 2, :], NTILE))):
                pe.wait_ge(to_pe, n + 1)
                nc.tensor.matmul(ps[:, n, 0:cnt], lhs[:, :], rhs, start=True, stop=True).then_inc(from_pe, 1)

        @block.scalar
        def _(act):
            act.wait_ge(to_act, 1)
            nc.scalar.activation(small[:, 2, :], small[:, 2, :], ACT.Sqrt).then_inc(from_act, 1)
            act.wait_ge(to_act, 2)
            nc.scalar.activation(tl[:, 2, :], tl[:, 2, :], ACT.Sqrt).then_inc(from_act, 1)


def group_scalars(nc, B, keep, turn, padded):
    CHAIN = 6
    with ExitStack() as ctx:
        sb = lambda name, shape: ctx.enter_context(nc.sbuf_tensor(f"n{turn}_{name}", shape, FP32))
        a, b2, m0 = sb("a", [P, B]), sb("b2", [P, B]), sb("m0", [P, B])
        rows = sb("rows", [P, B, W])
        ps = ctx.enter_context(nc.psum_tensor(f"n{turn}_ps", [P, 2, 512], FP32))
        chain, to_pe, from_pe, to_act, from_act, mean_ready, rows_out = keep["group_sems"]
        padded_turn = keep["padded_turns"]
        if padded is not None:
            keep["padded_turns"] += 1
        block = ctx.enter_context(nc.Block())
        mu, var = keep["stats"][:, :, 0], keep["stats"][:, :, 1]

        @block.vector
        def _(dve):
            link = Chain(dve, chain, CHAIN * turn)
            nc.vector.tensor_copy(m0[:, :], mu).then_inc(to_pe, 1)
            dve.wait_ge(from_pe, 2 * turn + 1)
            link(nc.vector.tensor_copy(keep["mean"][:, :], ps[:, 0, 0:B]))
            if padded is not None:
                nc.vector.tensor_copy(rows[:, :, :], keep["mean"][:, :].unsqueeze(2).to_broadcast([P, B, W])) \
                    .then_inc(mean_ready, 1)
            link(nc.vector.tensor_tensor(a[:, :], mu, keep["mean"][:, :], ALU.subtract))
            link(nc.vector.tensor_tensor(a[:, :], a[:, :], a[:, :], ALU.mult))
            nc.vector.tensor_tensor(b2[:, :], a[:, :], var, ALU.add).then_inc(to_pe, 1)
            dve.wait_ge(from_pe, 2 * turn + 2)
            nc.vector.tensor_scalar(a[:, :], ps[:, 1, 0:B], EPS, None, ALU.add).then_inc(to_act, 1)
            dve.wait_ge(from_act, turn + 1)
            link(nc.vector.reciprocal(keep["scale"][:, :], a[:, :]))
            link(nc.vector.tensor_tensor(b2[:, :], keep["mean"][:, :], keep["scale"][:, :], ALU.mult))
            link(nc.vector.tensor_scalar(keep["bias"][:, :], b2[:, :], -1.0, None, ALU.mult))
            assert link.n == CHAIN * (turn + 1)

        @block.tensor
        def _(pe):
            pe.wait_ge(to_pe, 2 * turn + 1)
            nc.tensor.matmul(ps[:, 0, 0:B], keep["gavg"][:, :], m0[:, :], start=True, stop=True).then_inc(from_pe, 1)
            pe.wait_ge(to_pe, 2 * turn + 2)
            nc.tensor.matmul(ps[:, 1, 0:B], keep["gavg"][:, :], b2[:, :], start=True, stop=True).then_inc(from_pe, 1)

        @block.scalar
        def _(act):
            act.wait_ge(to_act, turn + 1)
            nc.scalar.activation(a[:, :], a[:, :], ACT.Sqrt).then_inc(from_act, 1)

        if padded is not None:
            @block.sync
            def _(sp):
                sp.wait_ge(mean_ready, padded_turn + 1)
                for g in (0, G + 1):
                    sp.dma_start(padded[:, :, g, :].rearrange("b p w -> p b w"), rows[:, :, :]).then_inc(rows_out, 16)
                sp.wait_ge(rows_out, 32 * (padded_turn + 1))


def conv_phase(nc, B, t, keep, tag, src, dst, weights, bias_col, tile_scale=None, tile_bias=None):
    tiled = tag == "l0"
    fused = tag == "l3"
    PW = TC * (TW + 2) if tiled else W + 2
    HALF = P // 2
    LB = 4
    BODIES = B * STRIPS // LB
    with ExitStack() as ctx:
        def sb(name, shape, dt=FP32):
            return ctx.enter_context(nc.sbuf_tensor(f"{tag}_{name}", shape, dt))

        def sem(name):
            return ctx.enter_context(nc.semaphore(f"{tag}_{name}"))

        wt = sb("wt", [P, 2, 3, HALF])
        raw = [sb(f"raw{k}", [P, 2, GS, W]) for k in range(LB)]
        pad = [sb(f"pad{k}", [P, 2, GS, PW]) for k in range(2)]
        res = [sb(f"res{k}", [P, GS * W]) for k in range(2)]
        strip_stats = [sb(f"sst{k}", [P, NT, 6]) for k in range(2)]
        all_stats = sb("all_stats", [P, B * STRIPS, NT * 6])
        if fused:
            factor = sb("factor", [P, 2, 3, HALF])
            ind = sb("ind", [P, G, W], U16)
            ind_w, ind_f, ind_r = sb("ind_w", [P, P]), sb("ind_f", [P, P]), sb("ind_r", [P, P])
            ind_wb = sb("ind_wb", [P, P], BF16)
        if tiled:
            neg_scale, neg_bias = sb("nsc", [P, B * PAIRS * TC]), sb("nbi", [P, B * PAIRS * TC])
            neg_slope = sb("nslope", [P, 1])
            low = [sb(f"low{k}", [P, 2, GS, W]) for k in range(2)]
            high = [sb(f"high{k}", [P, 2, GS, W]) for k in range(2)]
            tile_scale2 = tile_scale[:, :, :].rearrange("p b n -> p (b n)")
            tile_bias2 = tile_bias[:, :, :].rearrange("p b n -> p (b n)")
        ps = ctx.enter_context(nc.psum_tensor(f"{tag}_ps", [P, 2, NT, 512], FP32))
        w_in, w_ready, stat_c, setup, act_passed = (
            sem("w_in"), sem("w_ready"), sem("stat_c"), sem("setup"), sem("act_passed"))
        loaded = [sem(f"loaded{k}") for k in range(LB)]
        if tiled:
            split = [sem(f"split{k}") for k in range(2)]
            combined = [sem(f"combined{k}") for k in range(2)]
        pad_ready = [sem(f"pad_ready{k}") for k in range(2)]
        tile_done = [sem(f"tile_done{k}") for k in range(2)]
        res_ready = [sem(f"res_ready{k}") for k in range(2)]
        stored = [sem(f"stored{k}") for k in range(2)]
        stat_w = [sem(f"stat_w{k}") for k in range(2)]
        block = ctx.enter_context(nc.Block())
        LOAD_INC = 16 * 6
        STORE_INC = 16 * (R if tag == "l1" else 1)

        @block.sync
        def _(sp):
            sp.dma_start(wt[:, :, :, :], weights[0]).then_inc(w_in, 16)
            if fused:
                sp.dma_start(factor[:, :, :, :], weights[1]).then_inc(w_in, 16)
                sp.dma_start(ind[:, :, :], t["ind"]).then_inc(w_in, 16)
                sp.dma_start(ind_w[:, :], t["ind_p"]).then_inc(w_in, 16)
                sp.dma_start(ind_f[:, :], t["ind_d"]).then_inc(w_in, 16)

            def load(b, g0, k):
                def rows(half, first, last, quarter, off):
                    n = last - first + 1
                    sp.dma_start(raw[k][first * C:(last + 1) * C, half, :, :],
                                 src[bass.ds(b, 1), quarter * C:(quarter + n) * C, bass.ds(g0 + off, GS), :]
                                 .rearrange("a p g w -> (a p) g w")).then_inc(loaded[k], 16)

                rows(0, 0, 1, 0, 1)
                rows(0, 2, 2, 3, 0)
                rows(0, 3, 3, 2, 1)
                rows(1, 0, 0, 1, 1)
                rows(1, 1, 1, 0, 2)
                rows(1, 2, 3, 2, 1)

            def store(b, g0, k):
                if tag == "l1":
                    for r in range(R):
                        o = dst[r, bass.ds(b * C, C), bass.ds(g0, GS), :].rearrange("c g w -> c (g w)")
                        sp.dma_start(o, res[k][r * C:(r + 1) * C, :]).then_inc(stored[k], 16)
                else:
                    o = (dst[bass.ds(b, 1), :, bass.ds(g0 + (0 if fused else 1), GS), :]
                         .rearrange("a p g w -> (a p) (g w)"))
                    sp.dma_start(o, res[k][:, :]).then_inc(stored[k], 16)

            for k in range(LB):
                load(0, k * GS, k)
            per = STRIPS // LB
            with sp.Fori(0, BODIES - 1) as m:
                b, g0 = sp.snap(m // per), sp.snap(m % per * (LB * GS))
                next_b, next_g0 = sp.snap((m + 1) // per), sp.snap((m + 1) % per * (LB * GS))
                for k in range(LB):
                    sp.wait_ge(res_ready[k % 2], (2 * m + (k // 2 + 1)) * NT + 1)
                    store(b, g0 + k * GS, k % 2)
                    load(next_b, next_g0 + k * GS, k)
            for k in range(LB):
                sp.wait_ge(res_ready[k % 2], (2 * (BODIES - 1) + k // 2 + 1) * NT + 1)
                store(B - 1, (STRIPS - LB + k) * GS, k % 2)
            for k in range(2):
                sp.wait_ge(stored[k], 2 * BODIES * STORE_INC + 1)

        def bodies(eng, strip):
            with eng.Fori(0, BODIES) as m:
                for k in range(LB):
                    strip(m * LB + k, m * 2 + k // 2, k, m)

        @block.scalar
        def _(act):
            def strip(n, u, k, m):
                h = k % 2
                act.wait_ge(loaded[k], (m + 1) * LOAD_INC)
                if tiled:
                    act.wait_ge(pad_ready[h], u + 1)
                    act.sem_inc(act_passed, 1)
                    tile = m * (2 * TC) + k // 2 * TC
                    for c in range(TC):
                        cs = slice(c * TW, (c + 1) * TW)
                        for o, bias, scale in ((high, tile_bias2, tile_scale2), (low, neg_bias, neg_scale)):
                            ins = nc.scalar.activation(
                                o[h][:, :, :, cs].rearrange("p a g w -> p (a g) w"),
                                raw[k][:, :, :, cs].rearrange("p a g w -> p (a g) w"), ACT.Relu,
                                bias=bias[:, bass.ds(tile + c, 1)], scale=scale[:, bass.ds(tile + c, 1)])
                    ins.then_inc(split[h], 1)
                else:
                    act.wait_ge(tile_done[h], u * NT + 1)
                    act.sem_inc(act_passed, 1)
                    b = act.snap(m // (STRIPS // LB))
                    nc.scalar.activation(pad[h][:, :, :, 1:W + 1].rearrange("p a g w -> p (a g) w"),
                                         raw[k][:, :, :, :].rearrange("p a g w -> p (a g) w"), ACT.Identity,
                                         bias=keep["bias"][:, bass.ds(b, 1)],
                                         scale=keep["scale"][:, bass.ds(b, 1)]).then_inc(pad_ready[h], 1)

            act.wait_ge(w_ready, 1)
            bodies(act, strip)

        def window(tile, half, j, kx):
            rows = tile[:, half, 2 * j:2 * j + 2, :]
            if tiled:
                return rows.rearrange("p g (c w) -> p (g c) w", c=TC)[:, :, kx:kx + TW]
            return rows[:, :, kx:kx + W]

        @block.tensor
        def _(pe):
            def strip(n, u, k, m):
                h = k % 2
                pe.wait_ge(pad_ready[h], u + 2)
                pe.wait_ge(res_ready[h], u * NT + 1)
                for j in range(NT):
                    if fused:
                        g0 = m % (STRIPS // LB) * (LB * GS) + (k * GS + 2 * j)
                        nc.tensor.matmul(ps[:, h, j, :], ind_wb[:, :],
                                         ind[:, bass.ds(g0, 2), :].rearrange("p g w -> p (g w)").bitcast(BF16),
                                         start=True, stop=False)
                    for kx in range(3):
                        for half in range(2):
                            ins = nc.tensor.matmul(ps[half * HALF:(half + 1) * HALF, h, j, :], wt[:, half, kx, :],
                                                   window(pad[h], half, j, kx),
                                                   start=(kx == 0 and not fused), stop=(kx == 2))
                    ins.then_inc(tile_done[h], 1)

            pe.wait_ge(w_ready, 1)
            bodies(pe, strip)

        @block.vector
        def _(dve):
            link = Chain(dve, setup)
            for k in range(2):
                link(nc.vector.memset(pad[k][:, :, :, :], 0.0))
            if tiled:
                link(nc.vector.tensor_scalar(neg_scale[:, :], tile_scale2, -1.0, None, ALU.mult))
                link(nc.vector.tensor_scalar(neg_bias[:, :], tile_bias2, -1.0, None, ALU.mult))
                link(nc.vector.tensor_scalar(neg_slope[:, :], keep["cols"][:, COL_PRELU:COL_PRELU + 1], -1.0, None, ALU.mult))
            if fused:
                dve.wait_ge(w_in, 16 * 5)
                link(nc.vector.tensor_tensor(wt[:, :, :, :], wt[:, :, :, :], factor[:, :, :, :], ALU.mult))
                link(nc.vector.memset(ind_wb[:, :], 0.0))
                link(nc.vector.tensor_tensor(ind_w[:, :], ind_w[:, :], ind_f[:, :], ALU.mult))
                for q in range(3):
                    part = slice(q * C, (q + 1) * C)
                    for _ in range(q):
                        link(nc.vector.tensor_copy(ind_wb[part, :], ind_w[part, :]))
                        link(nc.vector.tensor_tensor(ind_r[part, :], ind_w[part, :], ind_wb[part, :], ALU.subtract))
                        link(nc.vector.tensor_copy(ind_w[part, :], ind_r[part, :]))
                    link(nc.vector.tensor_copy(ind_wb[part, :], ind_w[part, :]))
            else:
                dve.wait_ge(w_in, 16)
            for k in range(2):
                for x in (pad_ready[k], tile_done[k], res_ready[k], stored[k]):
                    dve.sem_inc(x, 1)
            dve.sem_inc(w_ready, 1)

            def combine(u, h):
                dve.wait_ge(split[h], u + 1)
                dve.wait_ge(tile_done[h], u * NT + 1)
                for half in range(2):
                    nc.vector.scalar_tensor_tensor(
                        pad[h][:, half, :, :].rearrange("p g (c w) -> p (g c) w", c=TC)[:, :, 1:TW + 1],
                        low[h][:, half, :, :].rearrange("p g (c w) -> p (g c) w", c=TC), neg_slope[:, :],
                        high[h][:, half, :, :].rearrange("p g (c w) -> p (g c) w", c=TC),
                        ALU.mult, ALU.add).then_inc(combined[h], 1)
                dve.wait_ge(combined[h], (u + 1) * 2)
                edge = pad[h][2 * C:3 * C, 0, 0, :] if h == 0 else pad[h][C:2 * C, 1, GS - 1, :]
                nc.vector.memset(edge, 0.0).then_inc(pad_ready[h], 1)

            def finish(n, u, k):
                h = k % 2
                dve.wait_ge(stored[h], u * STORE_INC + 1)
                for j in range(NT):
                    dve.wait_ge(tile_done[h], u * NT + (j + 2))
                    o = res[h][:, j * 512:(j + 1) * 512]
                    if fused:
                        ins = nc.vector.tensor_scalar(o, ps[:, h, j, :], keep["cols"][:, bias_col:bias_col + 1],
                                                      None, ALU.add)
                    else:
                        for half in range(2):
                            part = slice(half * HALF, (half + 1) * HALF)
                            ins = nc.vector.scalar_tensor_tensor(
                                o[part, :], ps[part, h, j, :], keep["cols"][part, bias_col:bias_col + 1],
                                raw[k][part, half, 2 * j:2 * j + 2, :].rearrange("p g w -> p (g w)"),
                                ALU.add, ALU.add)
                    ins.then_inc(res_ready[h], 1)
                dve.wait_ge(res_ready[h], (u + 1) * NT + 1)
                for j in range(NT):
                    ins = nc.vector.bn_stats(strip_stats[h][:, j, :], res[h][:, j * 512:(j + 1) * 512])
                ins.then_inc(stat_w[h], 1)
                dve.wait_ge(stat_w[h], u + 1)
                nc.vector.tensor_scalar(
                    all_stats[:, bass.ds(n, 1), :].rearrange("p n v -> p (n v)"),
                    strip_stats[h][:, :, :].rearrange("p n v -> p (n v)"), 1.0, None, ALU.mult).then_inc(stat_c, 1)

            def body(m, last):
                for k in range(LB):
                    if tiled and not (last and k == LB - 1):
                        combine(m * 2 + (k + 1) // 2, (k + 1) % 2)
                    finish(m * LB + k, m * 2 + k // 2, k)

            if tiled:
                combine(0, 0)
            with dve.Fori(0, BODIES - 1) as m:
                body(m, False)
            body(BODIES - 1, True)
            dve.wait_ge(stat_c, B * STRIPS)
            for b in range(B):
                nc.vector.bn_aggr(keep["stats"][:, b, :], all_stats[:, b * STRIPS:(b + 1) * STRIPS, :]
                                  .rearrange("p n v -> p (n v)"))


def mix_phase(nc, B, t, keep, x2, mag, ang, x3):
    with ExitStack() as ctx:
        sb = lambda name, shape: ctx.enter_context(nc.sbuf_tensor("mx_" + name, shape, FP32))
        sem = lambda name: ctx.enter_context(nc.semaphore("mx_" + name))
        wmag, wang = sb("wmag", [P, P]), sb("wang", [P, P])
        raw = [sb(f"raw{k}", [P, GS * W]) for k in range(2)]
        mg = [sb(f"mg{k}", [P, GS * W]) for k in range(2)]
        an = [sb(f"an{k}", [P, GS * W]) for k in range(2)]
        res = [sb(f"res{k}", [P, GS * W]) for k in range(2)]
        strip_stats = [sb(f"sst{k}", [P, NT, 6]) for k in range(2)]
        all_stats = sb("all_stats", [P, B * STRIPS, NT * 6])
        ps = ctx.enter_context(nc.psum_tensor("mx_ps", [P, 2, NT, 512], FP32))
        w_in, w_ready, stat_c, setup = sem("w_in"), sem("w_ready"), sem("stat_c"), sem("setup")
        loaded = [sem(f"loaded{k}") for k in range(2)]
        tile_done = [sem(f"tile_done{k}") for k in range(2)]
        res_ready = [sem(f"res_ready{k}") for k in range(2)]
        stored = [sem(f"stored{k}") for k in range(2)]
        stat_w = [sem(f"stat_w{k}") for k in range(2)]
        block = ctx.enter_context(nc.Block())

        @block.sync
        def _(sp):
            sp.dma_start(wmag[:, :], t["wmag"]).then_inc(w_in, 16)
            sp.dma_start(wang[:, :], t["wang"]).then_inc(w_in, 16)

            def load(b, g0, k):
                for buf, src in ((mg, mag), (an, ang), (raw, x2)):
                    for r in range(R):
                        o = src[r, bass.ds(b * C, C), bass.ds(g0, GS), :].rearrange("c g w -> c (g w)")
                        sp.dma_start(buf[k][r * C:(r + 1) * C, :], o).then_inc(loaded[k], 16)

            def store(b, g0, k):
                o = x3[bass.ds(b, 1), :, bass.ds(g0 + 1, GS), :].rearrange("a p g w -> (a p) (g w)")
                sp.dma_start(o, res[k][:, :]).then_inc(stored[k], 16)

            for k in range(2):
                load(0, k * GS, k)
            with sp.Fori(1, B * PAIRS) as m:
                b, g0 = sp.snap(m // PAIRS), sp.snap(m % PAIRS * (2 * GS))
                old_b, old_g0 = sp.snap((m - 1) // PAIRS), sp.snap((m - 1) % PAIRS * (2 * GS))
                for k in range(2):
                    sp.wait_ge(res_ready[k], m * NT + 1)
                    store(old_b, old_g0 + k * GS, k)
                    load(b, g0 + k * GS, k)
            for k in range(2):
                sp.wait_ge(res_ready[k], B * PAIRS * NT + 1)
                store(B - 1, (STRIPS - 2 + k) * GS, k)
                sp.wait_ge(stored[k], B * PAIRS * 16 + 1)

        @block.tensor
        def _(pe):
            pe.wait_ge(w_ready, 1)
            with pe.Fori(0, B * PAIRS) as m:
                for k in range(2):
                    pe.wait_ge(loaded[k], (m + 1) * (16 * 3 * R))
                    pe.wait_ge(res_ready[k], m * NT + 1)
                    for j in range(NT):
                        cs = slice(j * 512, (j + 1) * 512)
                        nc.tensor.matmul(ps[:, k, j, :], wmag[:, :], mg[k][:, cs], start=True, stop=False)
                        nc.tensor.matmul(ps[:, k, j, :], wang[:, :], an[k][:, cs], start=False, stop=True) \
                            .then_inc(tile_done[k], 1)

        @block.vector
        def _(dve):
            link = Chain(dve, setup)
            dve.wait_ge(w_in, 32)
            link(nc.vector.tensor_scalar(wang[:, :], wang[:, :], 2.0, None, ALU.mult))
            for k in range(2):
                for x in (tile_done[k], res_ready[k], stored[k]):
                    dve.sem_inc(x, 1)
            dve.sem_inc(w_ready, 1)
            with dve.Fori(0, B * PAIRS) as m:
                for k in range(2):
                    dve.wait_ge(stored[k], m * 16 + 1)
                    for j in range(NT):
                        cs = slice(j * 512, (j + 1) * 512)
                        dve.wait_ge(tile_done[k], m * NT + (j + 2))
                        nc.vector.tensor_tensor(res[k][:, cs], ps[:, k, j, :], raw[k][:, cs], ALU.add) \
                            .then_inc(res_ready[k], 1)
                    dve.wait_ge(res_ready[k], (m + 1) * NT + 1)
                    for j in range(NT):
                        ins = nc.vector.bn_stats(strip_stats[k][:, j, :], res[k][:, j * 512:(j + 1) * 512])
                    ins.then_inc(stat_w[k], 1)
                    dve.wait_ge(stat_w[k], m + 1)
                    nc.vector.tensor_scalar(
                        all_stats[:, bass.ds(m * 2 + k, 1), :].rearrange("p n v -> p (n v)"),
                        strip_stats[k][:, :, :].rearrange("p n v -> p (n v)"), 1.0, None, ALU.mult).then_inc(stat_c, 1)
            dve.wait_ge(stat_c, B * STRIPS)
            for b in range(B):
                nc.vector.bn_aggr(keep["stats"][:, b, :], all_stats[:, b * STRIPS:(b + 1) * STRIPS, :]
                                  .rearrange("p n v -> p (n v)"))


def sample_phase(nc, B, t, keep, x3, h, out):
    with ExitStack() as ctx:
        sb = lambda name, shape: ctx.enter_context(nc.sbuf_tensor("sp_" + name, shape, FP32))
        sem = lambda name: ctx.enter_context(nc.semaphore("sp_" + name))
        woff = sb("woff", [P, 2, P])
        x0 = [sb(f"x0{k}", [P, GS, W + 1]) for k in range(2)]
        x1 = [sb(f"x1{k}", [P, GS, W + 1]) for k in range(2)]
        hb = [sb(f"h{k}", [P, GS * W]) for k in range(2)]
        th = [sb(f"th{k}", [P, 2, GS, W]) for k in range(2)]
        base = [sb(f"base{k}", [P, GS, W]) for k in range(2)]
        dy = [sb(f"dy{k}", [P, GS, W + 1]) for k in range(2)]
        dx = [sb(f"dx{k}", [P, GS, W]) for k in range(2)]
        dxy = [sb(f"dxy{k}", [P, GS, W]) for k in range(2)]
        u = [sb(f"u{k}", [P, GS, W]) for k in range(2)]
        v = sb("v", [P, GS, W])
        res = [sb(f"res{k}", [P, GS, W]) for k in range(2)]
        half_scale, one_scale = sb("half_scale", [P, B]), sb("one_scale", [P, B])
        bn = sb("bn", [P, 8])
        bs = sb("bs", [P, B])
        ps = ctx.enter_context(nc.psum_tensor("sp_ps", [P, 2, NT, 512], FP32))
        act_passed = sem("act_passed")
        w_in, chain, to_pe, from_pe, to_act, from_act, bn_ready = (
            sem("w_in"), sem("chain"), sem("to_pe"), sem("from_pe"), sem("to_act"), sem("from_act"), sem("bn_ready"))
        h_loaded = [sem(f"h_loaded{k}") for k in range(2)]
        x_loaded = [sem(f"x_loaded{k}") for k in range(2)]
        gelu_done = [sem(f"gelu_done{k}") for k in range(2)]
        off_done = [sem(f"off_done{k}") for k in range(2)]
        th_ready = [sem(f"th_ready{k}") for k in range(2)]
        edge_ready = [sem(f"edge_ready{k}") for k in range(2)]
        res_ready = [sem(f"res_ready{k}") for k in range(2)]
        stored = [sem(f"stored{k}") for k in range(2)]
        diff, base_ready, dve_step = sem("diff"), sem("base_ready"), sem("dve_step")
        block = ctx.enter_context(nc.Block())

        @block.sync
        def _(sp):
            sp.dma_start(woff[:, :, :], t["woff"]).then_inc(w_in, 16)

            def load(b, s, k):
                g0 = s * (2 * GS) + k * GS
                at = lambda parts, off: (x3[bass.ds(b, 1), parts, bass.ds(g0 + off, GS), :]
                                         .rearrange("a p g w -> (a p) g w"))
                sp.dma_start(hb[k][:, :], h[bass.ds(b, 1), :, bass.ds(g0, GS), :]
                             .rearrange("a p g w -> (a p) (g w)")).then_inc(h_loaded[k], 16)
                sp.dma_start(x0[k][:, :, 0:W], at(slice(0, P), 1)).then_inc(x_loaded[k], 16)
                sp.dma_start(x1[k][0:P - C, :, 0:W], at(slice(C, P), 1)).then_inc(x_loaded[k], 16)
                sp.dma_start(x1[k][P - C:P, :, 0:W], at(slice(0, C), 2)).then_inc(x_loaded[k], 16)

            def store(n, k):
                sp.dma_start(out[bass.ds(n, 1), :, :].rearrange("n p v -> (n p) v"),
                             res[k][:, :, :].rearrange("p g w -> p (g w)")).then_inc(stored[k], 16)

            for k in range(2):
                load(0, 0, k)
            with sp.Fori(1, B * PAIRS) as m:
                b, s, n = sp.snap(m // PAIRS), sp.snap(m % PAIRS), sp.snap(m * 2)
                for k in range(2):
                    sp.wait_ge(res_ready[k], m)
                    store(n + (k - 2), k)
                    load(b, s, k)
            for k in range(2):
                sp.wait_ge(res_ready[k], B * PAIRS)
                store(B * STRIPS - 2 + k, k)
                sp.wait_ge(stored[k], B * PAIRS * 16 + 1)

        @block.gpsimd
        def _(pool):
            with pool.Fori(0, B * PAIRS) as m:
                b, s = pool.snap(m // PAIRS), pool.snap(m % PAIRS)
                for k in range(2):
                    n = m * 2 + k
                    pool.wait_ge(x_loaded[k], (m + 1) * 48)
                    pool.wait_ge(edge_ready[k], m + 1)
                    nc.gpsimd.tensor_tensor(dy[k][:, :, :], x1[k][:, :, :], x0[k][:, :, :], ALU.subtract).then_inc(diff, 1)
                    nc.gpsimd.tensor_tensor(dx[k][:, :, :], x0[k][:, :, 1:W + 1], x0[k][:, :, 0:W], ALU.subtract) \
                        .then_inc(diff, 1)
                    pool.wait_ge(diff, n * 3 + 1)
                    nc.gpsimd.tensor_tensor(dxy[k][:, :, :], dy[k][:, :, 1:W + 1], dy[k][:, :, 0:W], ALU.subtract) \
                        .then_inc(diff, 1)

        @block.scalar
        def _(act):
            act.wait_ge(to_act, 1)
            nc.scalar.activation(bn[:, 4:5], bn[:, 4:5], ACT.Sqrt).then_inc(from_act, 1)
            act.wait_ge(bn_ready, 1)
            with act.Fori(0, B * PAIRS) as m:
                b, s = act.snap(m // PAIRS), act.snap(m % PAIRS)
                for k in range(2):
                    n = m * 2 + k
                    act.wait_ge(h_loaded[k], (m + 1) * 16)
                    nc.scalar.activation(hb[k][:, :], hb[k][:, :], ACT.Gelu, bias=bn[:, 6:7], scale=bn[:, 5:6]) \
                        .then_inc(gelu_done[k], 1)
                    act.wait_ge(x_loaded[k], (m + 1) * 48)
                    act.sem_inc(act_passed, 1)
                    for tile in (x0, x1):
                        ins = nc.scalar.activation(tile[k][:, :, W:W + 1], tile[k][:, :, 0:1], ACT.Identity,
                                                   bias=keep["mean"][:, bass.ds(b, 1)], scale=0.0)
                    ins.then_inc(edge_ready[k], 1)
                    nc.scalar.activation(base[k][:, :, :], x0[k][:, :, 0:W], ACT.Identity,
                                         bias=keep["bias"][:, bass.ds(b, 1)],
                                         scale=one_scale[:, bass.ds(b, 1)]).then_inc(base_ready, 1)
                    act.wait_ge(off_done[k], m + 1)
                    nc.scalar.activation(th[k][:, :, :, :].rearrange("p a g w -> p (a g w)"),
                                         ps[:, :, :, :].rearrange("p a j n -> p (a j n)"), ACT.Tanh) \
                        .then_inc(th_ready[k], 1)

        @block.tensor
        def _(pe):
            pe.wait_ge(to_pe, 1)
            nc.tensor.matmul(ps[:, 0, 0, 0:1], keep["cavg"][:, :], bn[:, 0:1], start=True, stop=True).then_inc(from_pe, 1)
            pe.wait_ge(to_pe, 2)
            nc.tensor.matmul(ps[:, 0, 1, 0:1], keep["cavg"][:, :], bn[:, 2:3], start=True, stop=True).then_inc(from_pe, 1)
            pe.wait_ge(bn_ready, 1)
            pe.wait_ge(w_in, 16)
            with pe.Fori(0, B * PAIRS) as m:
                for k in range(2):
                    pe.wait_ge(gelu_done[k], m + 1)
                    pe.wait_ge(th_ready[1 - k], m + 1)
                    for a in range(2):
                        for j in range(NT):
                            ins = nc.tensor.matmul(ps[:, a, j, :], woff[:, a, :], hb[k][:, j * 512:(j + 1) * 512],
                                                   start=True, stop=True)
                    ins.then_inc(off_done[k], 1)

        @block.vector
        def _(dve):
            link = Chain(dve, chain)
            mu, var = keep["stats"][:, :, 0], keep["stats"][:, :, 1]
            link(nc.vector.reduce_sum(bn[:, 1:2], mu, axis=AX.X))
            nc.vector.tensor_scalar(bn[:, 0:1], bn[:, 1:2], 1.0 / B, None, ALU.mult).then_inc(to_pe, 1)
            dve.wait_ge(from_pe, 1)
            link(nc.vector.tensor_copy(bn[:, 3:4], ps[:, 0, 0, 0:1]))
            link(nc.vector.tensor_scalar(bs[:, :], mu, bn[:, 3:4], None, ALU.subtract))
            link(nc.vector.tensor_tensor(bs[:, :], bs[:, :], bs[:, :], ALU.mult))
            link(nc.vector.tensor_tensor(bs[:, :], bs[:, :], var, ALU.add))
            link(nc.vector.reduce_sum(bn[:, 1:2], bs[:, :], axis=AX.X))
            nc.vector.tensor_scalar(bn[:, 2:3], bn[:, 1:2], 1.0 / B, None, ALU.mult).then_inc(to_pe, 1)
            dve.wait_ge(from_pe, 2)
            nc.vector.tensor_scalar(bn[:, 4:5], ps[:, 0, 1, 0:1], EPS, None, ALU.add).then_inc(to_act, 1)
            dve.wait_ge(from_act, 1)
            link(nc.vector.reciprocal(bn[:, 7:8], bn[:, 4:5]))
            link(nc.vector.tensor_scalar(bn[:, 5:6], bn[:, 7:8], keep["cols"][:, COL_BNG:COL_BNG + 1], None, ALU.mult))
            link(nc.vector.tensor_tensor(bn[:, 7:8], bn[:, 3:4], bn[:, 5:6], ALU.mult))
            link(nc.vector.tensor_tensor(bn[:, 6:7], keep["cols"][:, COL_BNB:COL_BNB + 1], bn[:, 7:8], ALU.subtract))
            link(nc.vector.tensor_scalar(half_scale[:, :], keep["scale"][:, :], 0.5, None, ALU.mult))
            link(nc.vector.tensor_scalar(one_scale[:, :], keep["scale"][:, :], 1.0, None, ALU.add))
            for k in range(2):
                dve.sem_inc(stored[k], 1)
            dve.sem_inc(th_ready[1], 1)
            dve.sem_inc(bn_ready, 1)

            with dve.Fori(0, B * PAIRS) as m:
                b, s = dve.snap(m // PAIRS), dve.snap(m % PAIRS)
                for k in range(2):
                    n = m * 2 + k
                    ty, tx = th[k][:, 0, :, :], th[k][:, 1, :, :]
                    dve.wait_ge(diff, (n + 1) * 3)
                    dve.wait_ge(th_ready[k], m + (1 + k))
                    nc.vector.scalar_tensor_tensor(u[k][:, :, :], ty, 1.0, dxy[k][:, :, :], ALU.add, ALU.mult) \
                        .then_inc(dve_step, 1)
                    nc.vector.scalar_tensor_tensor(v[:, :, :], ty, 1.0, dy[k][:, :, 0:W], ALU.add, ALU.mult) \
                        .then_inc(dve_step, 1)
                    dve.wait_ge(dve_step, n * 5 + 1)
                    nc.vector.scalar_tensor_tensor(u[k][:, :, :], u[k][:, :, :], 0.5, dx[k][:, :, :], ALU.mult, ALU.add) \
                        .then_inc(dve_step, 1)
                    dve.wait_ge(dve_step, n * 5 + 3)
                    nc.vector.scalar_tensor_tensor(u[k][:, :, :], tx, 1.0, u[k][:, :, :], ALU.add, ALU.mult) \
                        .then_inc(dve_step, 1)
                    dve.wait_ge(dve_step, n * 5 + 4)
                    nc.vector.tensor_tensor(u[k][:, :, :], u[k][:, :, :], v[:, :, :], ALU.add).then_inc(dve_step, 1)
                    dve.wait_ge(dve_step, n * 5 + 5)
                    dve.wait_ge(base_ready, n + 1)
                    dve.wait_ge(stored[k], m * 16 + 1)
                    nc.vector.scalar_tensor_tensor(
                        res[k][:, :, :], u[k][:, :, :], half_scale[:, bass.ds(b, 1)], base[k][:, :, :],
                        ALU.mult, ALU.add).then_inc(res_ready[k], 1)


def fourier_phase(nc, B, t, keep, x2, mag, ang):
    NG = B * C // CI
    K2 = 2 * W
    NPH = 2 * W + 6
    with ExitStack() as ctx:
        def sb(name, shape):
            return ctx.enter_context(nc.sbuf_tensor("ft_" + name, shape, FP32))

        def sem(name):
            return ctx.enter_context(nc.semaphore("ft_" + name))

        row_m = sb("row_m", [P, 2, 2, W])
        col_m = sb("col_m", [P, 2, 3, W])
        img_scale, img_bias = sb("img_scale", [P, B * C]), sb("img_bias", [P, B * C])
        fourier_tables(nc, B, t, keep, row_m, col_m, img_scale, img_bias, NPH)
        raw = [sb(f"raw{k}", [P, 2, CI, W]) for k in range(2)]
        xn = [sb(f"xn{k}", [P, 2, CI, W]) for k in range(2)]
        zt = [sb(f"zt{k}", [P, 2, K2]) for k in range(2)]
        y = [sb(f"y{k}", [P, CI, 2, K2]) for k in range(2)]
        sq = sb("sq", [P, CI, 2, K2])
        d = sb("d", [P, CI * 2, W])
        e = sb("e", [P, CI * 2, W])
        turn = sb("turn", [P, CI * 2, W])
        mg = [sb(f"mg{k}", [P, CI, 2, W]) for k in range(2)]
        an = [sb(f"an{k}", [P, CI, 2, W]) for k in range(2)]
        ps_a = ctx.enter_context(nc.psum_tensor("ft_psa", [P, 2, 2, 512], FP32))
        ps_b = ctx.enter_context(nc.psum_tensor("ft_psb", [P, 2, 2, 512], FP32))
        loaded = [sem(f"loaded{k}") for k in range(2)]
        stored = [sem(f"stored{k}") for k in range(2)]
        xn_ready, a_done, z_done, b_done, y_done = (
            sem("xn_ready"), sem("a_done"), sem("z_done"), sem("b_done"), sem("y_done"))
        sq_done, sum_done, mag_done, ratio_done, atan_done, post_done, step = (
            sem("sq_done"), sem("sum_done"), sem("mag_done"), sem("ratio_done"), sem("atan_done"), sem("post_done"),
            sem("step"))
        block = ctx.enter_context(nc.Block())

        def groups(eng, part):
            part(0, 0, 0, True, False)
            with eng.Fori(0, NG // 2 - 1) as v:
                part(v * 2 + 1, 1, v, False, False)
                part(v * 2 + 2, 0, v + 1, False, False)
            part(NG - 1, 1, NG // 2 - 1, False, True)

        @block.sync
        def _(sp):
            def load(c0, k):
                for r in range(R):
                    sp.dma_start(raw[k][64 * (r % 2):64 * (r % 2) + 64, r // 2, :, :],
                                 x2[r, bass.ds(c0, CI), :, :].rearrange("c g w -> g c w")).then_inc(loaded[k], 16)


            def store(c0, k):
                for buf, dst in ((mg, mag), (an, ang)):
                    for r in range(R):
                        sp.dma_start(dst[r, bass.ds(c0, CI), :, :].rearrange("c g w -> g c w"),
                                     buf[k][64 * (r % 2):64 * (r % 2) + 64, :, r // 2, :]).then_inc(stored[k], 16)

            load(0, 0)
            load(CI, 1)
            sp.wait_ge(xn_ready, 1)
            load(2 * CI, 0)
            with sp.Fori(0, NG // 2 - 2) as v:
                c0 = sp.snap(v * (2 * CI))
                sp.wait_ge(xn_ready, v * 2 + 2)
                load(c0 + 3 * CI, 1)
                sp.wait_ge(post_done, v * 2 + 3)
                store(c0, 0)
                sp.wait_ge(xn_ready, v * 2 + 3)
                load(c0 + 4 * CI, 0)
                sp.wait_ge(post_done, v * 2 + 4)
                store(c0 + CI, 1)
            sp.wait_ge(xn_ready, NG - 2)
            load((NG - 1) * CI, 1)
            for q in range(NG - 4, NG):
                sp.wait_ge(post_done, q + 3)
                store(q * CI, q % 2)
            for k in range(2):
                sp.wait_ge(stored[k], NG // 2 * (16 * 2 * R) + 1)

        @block.tensor
        def _(pe):
            def rows(k, i):
                for wc in range(2):
                    for hc in range(2):
                        ins = nc.tensor.matmul(ps_a[:, i % 2, wc, :], xn[k][:, hc, i, wc * P:(wc + 1) * P],
                                               row_m[:, hc, :, :].rearrange("p a w -> p (a w)"),
                                               start=(hc == 0), stop=(hc == 1))
                ins.then_inc(a_done, 1)

            def part(q, k, u, first, last):
                for i in range(CI):
                    n = q * CI + i
                    if not (last and i == CI - 1):
                        if i == CI - 1:
                            pe.wait_ge(xn_ready, q + 2)
                        pe.wait_ge(z_done, n + 1)
                        rows(k if i < CI - 1 else 1 - k, (i + 1) % CI)
                    pe.wait_ge(z_done, n + 2)
                    pe.wait_ge(y_done, n + 1)
                    for pc in range(2):
                        for wc in range(2):
                            for im in range(2):
                                ins = nc.tensor.matmul(
                                    ps_b[:, i % 2, pc, :], zt[i % 2][:, wc, im * W + pc * P:im * W + (pc + 1) * P],
                                    col_m[:, wc, 1 - im:3 - im, :].rearrange("p a w -> p (a w)"),
                                    start=(wc == 0 and im == 0), stop=(wc == 1 and im == 1))
                    ins.then_inc(b_done, 1)

            pe.wait_ge(xn_ready, 1)
            rows(0, 0)
            groups(pe, part)

        def whole(ap):
            return ap.rearrange("p a w -> p (a w)")

        def halves(ap, part):
            return ap.rearrange("p i c w -> p (i c) w")[:, :, part * W:(part + 1) * W]

        @block.scalar
        def _(act):
            for x, credit in ((z_done, 1), (y_done, 2)):
                act.sem_inc(x, credit)

            def take_z(n, i):
                act.wait_ge(a_done, n + 1)
                act.wait_ge(b_done, n + 1)
                nc.scalar.activation(whole(zt[i % 2][:, :, :]), whole(ps_a[:, i % 2, :, :]), ACT.Identity) \
                    .then_inc(z_done, 1)

            def take_y(n, i, k, q):
                act.wait_ge(b_done, n + 3)
                if i == 0:
                    act.wait_ge(post_done, q + 1)
                nc.scalar.activation(whole(y[k][:, i, :, :]), whole(ps_b[:, i % 2, :, :]), ACT.Identity) \
                    .then_inc(y_done, 1)

            def squares(q, k):
                act.wait_ge(y_done, (q + 1) * CI + 2)
                nc.scalar.activation(sq[:, :, :, :].rearrange("p i c w -> p (i c w)"),
                                     y[k][:, :, :, :].rearrange("p i c w -> p (i c w)"), ACT.Square).then_inc(sq_done, 1)

            def root(q, k, u):
                act.wait_ge(stored[k], u * (16 * 2 * R) + 1)
                act.wait_ge(sum_done, q + 1)
                nc.scalar.activation(mg[k][:, :, :, :].rearrange("p i c w -> p (i c) w"), d[:, :, :], ACT.Sqrt) \
                    .then_inc(mag_done, 1)

            def arctan(q):
                act.wait_ge(ratio_done, q + 1)
                nc.scalar.activation(e[:, :, :], d[:, :, :], ACT.Arctan).then_inc(atan_done, 1)

            def part(q, k, u, first, last):
                for i in range(CI):
                    n = q * CI + i
                    take_z(n, i)
                    if i:
                        take_y(n - 1, i - 1, k, q)
                    elif not first:
                        take_y(n - 1, CI - 1, 1 - k, q - 1)
                        squares(q - 1, 1 - k)
                    if i == 1 and not first:
                        root(q - 1, 1 - k, u - (1 - k))
                    if i == 3 and not first:
                        arctan(q - 1)

            groups(act, part)
            take_y(NG * CI - 1, CI - 1, 1, NG - 1)
            squares(NG - 1, 1)
            root(NG - 1, 1, NG // 2 - 1)
            arctan(NG - 1)

        @block.vector
        def _(dve):
            for k in range(2):
                dve.sem_inc(stored[k], 1)
            dve.sem_inc(b_done, 2)
            dve.sem_inc(post_done, 2)
            STEPS = 5

            def normalise(q, k, u):
                dve.wait_ge(loaded[k], (u + 1) * (16 * R))
                for i in range(CI):
                    ins = nc.vector.tensor_scalar(xn[k][:, :, i, :], raw[k][:, :, i, :],
                                                  img_scale[:, bass.ds(q * CI + i, 1)],
                                                  img_bias[:, bass.ds(q * CI + i, 1)], ALU.mult, ALU.add)
                ins.then_inc(xn_ready, 1)

            def angles(q, k, u):
                re, im = halves(y[k][:, :, :, :], 0), halves(y[k][:, :, :, :], 1)
                did = [0]

                def link(ins, more=None):
                    did[0] += 1
                    ins.then_inc(step, 1)
                    dve.wait_ge(step, q * STEPS + did[0])

                dve.wait_ge(post_done, q + 2)
                dve.wait_ge(sq_done, q + 1)
                nc.vector.scalar_tensor_tensor(d[:, :, :], halves(sq[:, :, :, :], 0), 1.5e-35,
                                               halves(sq[:, :, :, :], 1), ALU.add, ALU.add).then_inc(sum_done, 1)
                link(nc.vector.tensor_scalar(turn[:, :, :], im, 0.0, 0.5, ALU.is_ge, ALU.subtract))
                link(nc.vector.scalar_tensor_tensor(turn[:, :, :], re, 0.0, turn[:, :, :], ALU.is_lt, ALU.mult))
                dve.wait_ge(mag_done, q + 1)
                link(nc.vector.scalar_tensor_tensor(
                    d[:, :, :].bitcast(U32), re.bitcast(U32), 0x80000000,
                    mg[k][:, :, :, :].rearrange("p i c w -> p (i c) w").bitcast(U32), ALU.bitwise_and, ALU.bitwise_or))
                link(nc.vector.tensor_tensor(d[:, :, :], d[:, :, :], re, ALU.add))
                link(nc.vector.reciprocal(d[:, :, :], d[:, :, :]))
                nc.vector.tensor_tensor(d[:, :, :], d[:, :, :], im, ALU.mult).then_inc(ratio_done, 1)
                dve.wait_ge(ratio_done, q + 1)
                dve.wait_ge(stored[k], u * (16 * 2 * R) + 1)
                dve.wait_ge(atan_done, q + 1)
                nc.vector.scalar_tensor_tensor(an[k][:, :, :, :].rearrange("p i c w -> p (i c) w"), e[:, :, :],
                                               1.0 / np.pi, turn[:, :, :], ALU.mult, ALU.add).then_inc(post_done, 1)
                assert did[0] == STEPS


            def part(q, k, u, first, last):
                if not first:
                    angles(q - 1, 1 - k, u - (1 - k))
                if first:
                    dve.wait_ge(a_done, CI)
                    if NG > 2:
                        normalise(2, 0, 1)
                elif not last:
                    more_part(q, k, u)

            def more_part(q, k, u):
                dve.wait_ge(a_done, q * CI + CI)
                normalise(q + 2, k, u + 1)

            normalise(0, 0, 0)
            normalise(1, 1, 0)
            part(0, 0, 0, True, False)
            with dve.Fori(0, NG // 2 - 2) as v:
                part(v * 2 + 1, 1, v, False, False)
                part(v * 2 + 2, 0, v + 1, False, False)
            part(NG - 3, 1, NG // 2 - 2, False, False)
            part(NG - 2, 0, NG // 2 - 1, False, True)
            part(NG - 1, 1, NG // 2 - 1, False, True)
            angles(NG - 1, 1, NG // 2 - 1)


def fourier_tables(nc, B, t, keep, row_m, col_m, img_scale, img_bias, NPH):
    K2 = 2 * W
    with ExitStack() as ctx:
        sb = lambda name, shape: ctx.enter_context(nc.sbuf_tensor("fm_" + name, shape, FP32))
        sem = lambda name: ctx.enter_context(nc.semaphore("fm_" + name))
        dft = sb("dft", [P, 2, 4, W])
        nsq = sb("nsq", [P, NPH])
        ident = sb("ident", [C, C])
        ones = sb("ones", [C, P])
        spread = sb("spread", [C, 2, B, C])
        ph, turns, co, si = sb("ph", [P, NPH]), sb("turns", [P, NPH]), sb("co", [P, NPH]), sb("si", [P, NPH])
        rhs = sb("rhs", [P, 2, 4, 2, W])
        circ = sb("circ", [P, 2, 2, 2, W])
        dd = sb("dd", [P, 2, 2, 2, W])
        tmp = sb("tmp", [P, 2, W])
        a = sb("a", [P, 16])
        c2 = sb("c2", [P, 2, 2])
        ps = ctx.enter_context(nc.psum_tensor("fm_ps", [P, 8, 512], FP32))
        const_in, chain, to_pe, from_pe, to_act, from_act = (
            sem("const_in"), sem("chain"), sem("to_pe"), sem("from_pe"), sem("to_act"), sem("from_act"))
        block = ctx.enter_context(nc.Block())
        col = lambda n: a[:, n:n + 1]

        @block.sync
        def _(sp):
            sp.dma_start(dft[:, :, :, :], t["dft"]).then_inc(const_in, 16)
            sp.dma_start(nsq[:, :], t["nsq"]).then_inc(const_in, 16)
            sp.dma_start(ident[:, :], t["ident"]).then_inc(const_in, 16)

        @block.scalar
        def _(act):
            act.wait_ge(to_act, 1)
            nc.scalar.activation(a[:, 4:7], a[:, 1:4], ACT.Sin).then_inc(from_act, 1)
            act.wait_ge(to_act, 2)
            nc.scalar.activation(si[:, :], ph[:, :], ACT.Sin).then_inc(from_act, 1)
            nc.scalar.activation(co[:, :], ph[:, :], ACT.Sin, scale=0.5).then_inc(from_act, 1)
            act.wait_ge(to_act, 3)
            nc.scalar.activation(col(11), col(10), ACT.Sqrt).then_inc(from_act, 1)

        @block.tensor
        def _(pe):
            pe.wait_ge(to_pe, 1)
            for n in range(2):
                ins = nc.tensor.matmul(ps[:, n, 0:B * C], ones[:, :], spread[:, n, :, :].rearrange("p b c -> p (b c)"),
                                       start=True, stop=True)
            ins.then_inc(from_pe, 1)
            pe.wait_ge(to_pe, 2)
            for v in range(2):
                for pc in range(2):
                    for kk in range(4):
                        ins = nc.tensor.matmul(ps[:, 4 + 2 * v + pc, :], dft[:, v, kk, pc * P:(pc + 1) * P],
                                               rhs[:, v, kk, :, :].rearrange("p a w -> p (a w)"),
                                               start=(kk == 0), stop=(kk == 3))
            ins.then_inc(from_pe, 1)

        @block.vector
        def _(dve):
            link = Chain(dve, chain)
            dve.wait_ge(const_in, 48)
            link(nc.vector.memset(ones[:, :], 1.0))
            for n, src in enumerate((keep["scale"], keep["bias"])):
                link(nc.vector.tensor_tensor(spread[:, n, :, :], src[0:C, :].unsqueeze(2).to_broadcast([C, B, C]),
                                             ident[:, :].unsqueeze(1).to_broadcast([C, B, C]), ALU.mult))
            dve.sem_inc(to_pe, 1)
            alpha = keep["cols"][:, COL_ALPHA:COL_ALPHA + 1]
            link(nc.vector.tensor_scalar(col(0), alpha, 1e-4, float(np.float32(2.0 - 1e-4)), ALU.max, ALU.min))
            link(nc.vector.tensor_scalar(col(1), col(0), float(np.pi / 4), None, ALU.mult))
            link(nc.vector.tensor_scalar(col(2), col(1), -1.0, float(np.pi / 2), ALU.mult, ALU.add))
            link(nc.vector.tensor_scalar(col(3), col(0), float(np.pi / 2), None, ALU.mult))
            dve.sem_inc(to_act, 1)
            dve.wait_ge(from_act, 1)
            link(nc.vector.reciprocal(a[:, 8:10], a[:, 5:7]))
            link(nc.vector.tensor_tensor(col(7), col(4), col(8), ALU.mult))
            link(nc.vector.tensor_scalar(ph[:, :], nsq[:, :], float(np.pi), None, ALU.mult))
            link(nc.vector.tensor_scalar(ph[:, 0:NPH - 2], ph[:, 0:NPH - 2], col(7), 1.0 / W, ALU.mult, ALU.mult))
            link(nc.vector.tensor_scalar(ph[:, NPH - 2:NPH], ph[:, NPH - 2:NPH], col(9), 1.0 / W, ALU.mult, ALU.mult))
            link(nc.vector.tensor_scalar(turns[:, :], ph[:, :], float(0.5 / np.pi), BIG, ALU.mult, ALU.add))
            link(nc.vector.tensor_scalar(turns[:, :], turns[:, :], BIG, None, ALU.subtract))
            for part in (6.28125, float(2 * np.pi - 6.28125)):
                link(nc.vector.scalar_tensor_tensor(ph[:, :], turns[:, :], -part, ph[:, :], ALU.mult, ALU.add))
            link(nc.vector.tensor_scalar(ph[:, :], ph[:, :], 3.1415925, -3.1415925, ALU.min, ALU.max))
            dve.sem_inc(to_act, 1)
            link(nc.vector.tensor_scalar(col(13), col(6), -1.0, None, ALU.mult))
            link(nc.vector.tensor_tensor(col(10), col(6), col(13), ALU.max))
            link(nc.vector.tensor_scalar(col(10), col(10), 1e-12, None, ALU.add))
            dve.sem_inc(to_act, 1)
            dve.wait_ge(from_act, 4)
            link(nc.vector.reciprocal(col(12), col(11)))
            link(nc.vector.tensor_tensor(co[:, :], co[:, :], co[:, :], ALU.mult))
            link(nc.vector.tensor_scalar(co[:, :], co[:, :], -2.0, 1.0, ALU.mult, ALU.add))
            link(nc.vector.tensor_scalar(c2[:, 0, :], co[:, NPH - 2:NPH], 1.0 / W, None, ALU.mult))
            link(nc.vector.tensor_scalar(c2[:, 1, :], si[:, NPH - 2:NPH], -1.0 / W, None, ALU.mult))
            for v in range(2):
                for kk in range(4):
                    for im in range(2):
                        link(nc.vector.tensor_scalar(rhs[:, v, kk, im, :], dft[:, v, kk, :], c2[:, im, kk % 2:kk % 2 + 1],
                                                     None, ALU.mult))
            dve.sem_inc(to_pe, 1)
            dve.wait_ge(from_pe, 1)
            link(nc.vector.tensor_copy(img_scale[:, :], ps[:, 0, 0:B * C]))
            link(nc.vector.tensor_copy(img_bias[:, :], ps[:, 1, 0:B * C]))
            dve.wait_ge(from_pe, 2)
            for v in range(2):
                link(nc.vector.tensor_copy(circ[:, v, :, :, :].rearrange("p c a w -> p c (a w)"),
                                           ps[:, 4 + 2 * v:6 + 2 * v, :]))
            link(nc.vector.tensor_scalar(co[:, K2:K2 + 4], co[:, K2:K2 + 4], col(12), None, ALU.mult))
            link(nc.vector.tensor_scalar(si[:, K2:K2 + 4], si[:, K2:K2 + 4], col(12), None, ALU.mult))
            for v in range(2):
                cr = co[:, v * W:(v + 1) * W].unsqueeze(1).to_broadcast([P, 2, W])
                sr = si[:, v * W:(v + 1) * W].unsqueeze(1).to_broadcast([P, 2, W])
                re, im = circ[:, v, :, 0, :], circ[:, v, :, 1, :]
                link(nc.vector.tensor_tensor(dd[:, v, :, 0, :], re, cr, ALU.mult))
                link(nc.vector.tensor_tensor(tmp[:, :, :], im, sr, ALU.mult))
                link(nc.vector.tensor_tensor(dd[:, v, :, 0, :], dd[:, v, :, 0, :], tmp[:, :, :], ALU.add))
                link(nc.vector.tensor_tensor(dd[:, v, :, 1, :], im, cr, ALU.mult))
                link(nc.vector.tensor_tensor(tmp[:, :, :], re, sr, ALU.mult))
                link(nc.vector.tensor_tensor(dd[:, v, :, 1, :], dd[:, v, :, 1, :], tmp[:, :, :], ALU.subtract))
                for pc in range(2):
                    cc, sc = co[:, K2 + 2 * v + pc:K2 + 2 * v + pc + 1], si[:, K2 + 2 * v + pc:K2 + 2 * v + pc + 1]
                    o_re, o_im = ((col_m[:, pc, 1, :], col_m[:, pc, 2, :]) if v == 0 else
                                  (row_m[:, pc, 0, :], row_m[:, pc, 1, :]))
                    link(nc.vector.tensor_scalar(tmp[:, 0, :], dd[:, v, pc, 1, :], sc, None, ALU.mult))
                    link(nc.vector.scalar_tensor_tensor(o_re, dd[:, v, pc, 0, :], cc, tmp[:, 0, :], ALU.mult, ALU.add))
                    link(nc.vector.tensor_scalar(tmp[:, 1, :], dd[:, v, pc, 0, :], sc, None, ALU.mult))
                    link(nc.vector.scalar_tensor_tensor(o_im, dd[:, v, pc, 1, :], cc, tmp[:, 1, :], ALU.mult, ALU.subtract))
            link(nc.vector.tensor_scalar(col_m[:, :, 0, :], col_m[:, :, 2, :], -1.0, None, ALU.mult))


_COLS = ("L0_conv_gamma", "L0_conv_beta", "L0_conv_prelu_a", "L0_conv_conv_b", "L1_conv_b", "L3_conv_dw_b",
         "L3_conv_bn_g", "L3_conv_bn_b", "L2_conv_alpha")


HALF_ROWS = ((0, 1, -1, 2), (1, 4, 2, 3))


def _band(w):
    m = np.zeros((R, C, 2, 3, 2, C), w.dtype)
    for half, rows in enumerate(HALF_ROWS):
        for a, row in enumerate(rows):
            for q in range(2):
                ky = row - (2 * half + q) + 1
                if 0 <= ky <= 2:
                    m[a, :, half, :, q, :] = w[:, :, ky, :].transpose(1, 2, 0)
    return m.reshape(P, 2, 3, 2 * C)


def _block_diagonal(w):
    m = np.zeros((R, C, R, C), w.dtype)
    for r in range(R):
        m[r, :, r, :] = w.T
    return m.reshape(P, P)


BF16_ONE = 0x3F80


def _constants():
    c = np.arange(P) % C
    gavg = ((c[:, None] // 2 == c[None, :] // 2) / (2.0 * R)).astype(np.float32)
    cavg = ((c[:, None] == c[None, :]) / float(R)).astype(np.float32)
    perm = np.array([R * (p % G) + p // G for p in range(H)])
    j = np.arange(W)
    dft = np.zeros((P, 2, 4, W), np.float32)
    for v, rows in enumerate((j, perm)):
        x = 2 * np.pi * ((j[:, None] * rows[None, :]) % W) / W
        dft[:, v] = np.concatenate([np.cos(x).reshape(2, P, W), np.sin(x).reshape(2, P, W)]).transpose(1, 0, 2)
    n2 = (((j + W // 2) % W) - W // 2) ** 2
    nsq = np.zeros((P, 2 * W + 6), np.float32)
    nsq[:, 0:W] = n2
    nsq[:, W:2 * W] = n2[perm]
    nsq[:, 2 * W:2 * W + 2] = n2.reshape(2, P).T
    nsq[:, 2 * W + 2:2 * W + 4] = n2[perm].reshape(2, P).T
    nsq[:, 2 * W + 4:] = ((j - W // 2) ** 2).reshape(2, P).T
    ind = np.zeros((R, C, G, W), np.uint16)
    for q in range(6):
        h = R * np.arange(G) - 1 + q
        for kx in range(3):
            c = j + kx - 1
            inside = ((h >= 0) & (h < H))[:, None] & ((c >= 0) & (c < W))[None, :]
            ind[0:3, q * 3 + kx] = np.where(inside, BF16_ONE, 0)
    ind = ind.reshape(P, G, W)
    return dict(gavg=gavg, cavg=cavg, dft=dft, nsq=nsq, ident=np.eye(C, dtype=np.float32), ind=ind)


def layout(inputs):
    x = np.asarray(inputs["x"])
    B = x.shape[0]
    a = _constants()
    xr = np.zeros((B, R, C, G + 2, W), x.dtype)
    xr[:, :, :, 1:G + 1] = x.reshape(B, C, G, R, W).transpose(0, 3, 1, 2, 4)
    a["xr"] = xr.reshape(B, P, G + 2, W)
    cols = np.zeros((P, NCOL), np.float32)
    for n, name in enumerate(_COLS):
        v = np.asarray(inputs[name]).reshape(-1)
        cols[:, n] = np.tile(v, R) if v.size == C else v[0]
    a["cols"] = cols
    a["w0"] = _band(np.asarray(inputs["L0_conv_conv_w"]))
    a["w1"] = _band(np.asarray(inputs["L1_conv_W"]))
    pw = np.asarray(inputs["L3_conv_proj_w"])[:, :, 0, 0]
    dw = np.asarray(inputs["L3_conv_dw_w"])[:, 0]
    pb = np.asarray(inputs["L3_conv_proj_b"])
    a["w3_p"] = _band(np.broadcast_to(pw[:, :, None, None], (C, C, 3, 3)))
    a["w3_d"] = _band(np.broadcast_to(dw[:, None, :, :], (C, C, 3, 3)))
    ind_d = np.zeros((R, C, R, C), np.float32)
    for q in range(6):
        for r in range(R):
            if 0 <= q - r <= 2:
                for kx in range(3):
                    ind_d[0:3, q * 3 + kx, r, :] = dw[:, q - r, kx]
    a["ind_d"] = ind_d.reshape(P, P)
    a["ind_p"] = np.broadcast_to(np.tile(pb, R), (P, P))
    w = np.asarray(inputs["L2_conv_w"])
    a["wmag"], a["wang"] = _block_diagonal(w[:, :C]), _block_diagonal(w[:, C:])
    off = np.asarray(inputs["L3_conv_off_w"])[:, :, 0, 0]
    a["woff"] = np.stack([_block_diagonal(np.broadcast_to(off[n], (C, C))) for n in range(2)], axis=1)
    return {k: np.ascontiguousarray(v) for k, v in a.items()}, B


def program(nc, arrays, B):
    t = {k: nc.dram_tensor("in_" + k, v.shape, mybir.dt.from_np(v.dtype), kind="ExternalInput").ap()
         for k, v in arrays.items()}
    t["out"] = nc.dram_tensor("out_0", [B * STRIPS, P, GS * W], FP32, kind="ExternalOutput").ap()
    build(nc, B, t)


def unlay(o, B):
    return np.ascontiguousarray(o.reshape(B, STRIPS, R, C, GS, W).transpose(0, 3, 1, 4, 2, 5)).reshape(B, C, H, W)


def kernel(**inputs):
    import concourse.bacc as _bacc
    from concourse.bass_utils import run_bass_kernel_spmd as _run

    arrays, B = layout(inputs)
    nc = _bacc.Bacc("TRN2", target_bir_lowering=False, num_devices=1)
    program(nc, arrays, B)
    r = _run(nc, [{"in_" + k: v for k, v in arrays.items()}], core_ids=[0])
    return unlay(r.results[0]["out_0"], B)
```

```python
from contextlib import ExitStack

import numpy as np
import concourse.bass as bass
from concourse import mybir

FP32 = mybir.dt.float32
BF16 = mybir.dt.bfloat16
FP16 = mybir.dt.float16
U32 = mybir.dt.uint32
U16 = mybir.dt.uint16
ALU = mybir.AluOpType
ACT = mybir.ActivationFunctionType
AX = mybir.AxisListType

C = 32
H = W = 256
R = 4
G = H // R
P = R * C
GS = 8
STRIPS = G // GS
PAIRS = STRIPS // 2
NT = 4
TC = 4
TW = W // TC
CI = 4
EPS = 1e-5
UP = 64.0
BIG = 12582912.0

(COL_GAMMA, COL_BETA, COL_PRELU, COL_B0, COL_B1, COL_DWB, COL_BNG, COL_BNB, COL_ALPHA, NCOL) = range(10)


class Chain:

    def __init__(self, eng, sem, n=0):
        self.eng, self.sem, self.n = eng, sem, n

    def __call__(self, ins):
        self.n += 1
        ins.then_inc(self.sem, 1)
        self.eng.wait_ge(self.sem, self.n)


def build(nc, B, t):
    with ExitStack() as ctx:
        def sb(name, shape, dt=FP32):
            return ctx.enter_context(nc.sbuf_tensor(name, shape, dt))

        cols = sb("cols", [P, NCOL])
        gavg = sb("gavg", [P, P])
        cavg = sb("cavg", [P, P])
        scale = sb("scale", [P, B])
        bias = sb("bias", [P, B])
        mean = sb("mean", [P, B])
        stats = sb("stats", [P, B, 2])
        dram = {}
        for name, shape in (("x1", [B, P, G + 2, W]), ("x2", [B, P, G, W]), ("mag", [B, P, G, W]),
                            ("ang", [B, P, G, W]), ("x3", [B, P, G + 2, W]), ("h", [B, P, G, W])):
            dram[name] = nc.dram_tensor(name + "_dram", shape, FP32, kind="Internal").ap()
        keep = dict(cols=cols, gavg=gavg, cavg=cavg, scale=scale, bias=bias, mean=mean, stats=stats)
        keep["group_sems"] = [ctx.enter_context(nc.semaphore("group_" + name)) for name in
                              ("chain", "to_pe", "from_pe", "to_act", "from_act", "mean_ready", "rows_out")]
        keep["padded_turns"] = 0
        with ExitStack() as tiles:
            tile_scale = tiles.enter_context(nc.sbuf_tensor("tile_scale", [P, B, PAIRS * TC], FP32))
            tile_bias = tiles.enter_context(nc.sbuf_tensor("tile_bias", [P, B, PAIRS * TC], FP32))
            x_stats(nc, B, t, keep, tile_scale, tile_bias)
            conv_phase(nc, B, t, keep, "l0", t["xr"], dram["x1"], (t["w0"],), COL_B0, tile_scale, tile_bias)
        group_scalars(nc, B, keep, 0, dram["x1"])
        conv_phase(nc, B, t, keep, "l1", dram["x1"], dram["x2"], (t["w1"],), COL_B1)
        group_scalars(nc, B, keep, 1, None)
        fourier_phase(nc, B, t, keep, dram["x2"], dram["mag"], dram["ang"])
        mix_phase(nc, B, t, keep, dram["x2"], dram["mag"], dram["ang"], dram["x3"])
        group_scalars(nc, B, keep, 2, dram["x3"])
        conv_phase(nc, B, t, keep, "l3", dram["x3"], dram["h"], (t["w3_p"], t["w3_d"]), COL_DWB)
        sample_phase(nc, B, t, keep, dram["x3"], dram["h"], t["out"])


def x_stats(nc, B, t, keep, tile_scale, tile_bias):
    NTILE = PAIRS * TC
    LB = 4
    BODIES = B * STRIPS // LB
    with ExitStack() as ctx:
        sb = lambda name, shape: ctx.enter_context(nc.sbuf_tensor("xs_" + name, shape, FP32))
        raw = [sb(f"raw{k}", [P, GS, W]) for k in range(LB)]
        st = [sb(f"st{k}", [P, TC, 6]) for k in range(LB)]
        raw_stats = sb("raw_stats", [P, B * PAIRS * 2, TC, 6])
        tile_stats = sb("tile_stats", [P, B, NTILE, 2])
        a = sb("a", [P, B, NTILE])
        b2 = sb("b2", [P, B, NTILE])
        small = sb("small", [P, 4, B])
        tl = sb("tl", [P, 4, NTILE])
        ps = ctx.enter_context(nc.psum_tensor("xs_ps", [P, 4, 512], FP32))
        sem = lambda name: ctx.enter_context(nc.semaphore("xs_" + name))
        const_in, chain, to_pe, from_pe, to_act, from_act = (
            sem("const_in"), sem("chain"), sem("to_pe"), sem("from_pe"), sem("to_act"), sem("from_act"))
        loaded = [sem(f"loaded{k}") for k in range(LB)]
        freed = [sem(f"freed{k}") for k in range(LB)]
        stat_done = sem("stat_done")
        block = ctx.enter_context(nc.Block())

        @block.sync
        def _(sp):
            sp.dma_start(keep["cols"][:, :], t["cols"]).then_inc(const_in, 16)
            sp.dma_start(keep["gavg"][:, :], t["gavg"]).then_inc(const_in, 16)
            sp.dma_start(keep["cavg"][:, :], t["cavg"]).then_inc(const_in, 16)
            per = STRIPS // LB
            with sp.Fori(0, BODIES) as m:
                b, s = sp.snap(m // per), sp.snap(m % per)
                for k in range(LB):
                    sp.wait_ge(freed[k], m + 1)
                    sp.dma_start(raw[k][:, :, :],
                                 t["xr"][bass.ds(b, 1), :, bass.ds(s * (LB * GS) + (1 + k * GS), GS), :]
                                 .rearrange("a p g w -> (a p) g w")).then_inc(loaded[k], 16)

        @block.vector
        def _(dve):
            for k in range(LB):
                dve.sem_inc(freed[k], 1)
            with dve.Fori(0, BODIES) as m:
                for k in range(LB):
                    dve.wait_ge(loaded[k], (m + 1) * 16)
                    for c in range(TC):
                        ins = nc.vector.bn_stats(st[k][:, c, :], raw[k][:, :, c * TW:(c + 1) * TW])
                    ins.then_inc(freed[k], 1)
                    dve.wait_ge(freed[k], m + 2)
                    nc.vector.tensor_scalar(
                        raw_stats[:, bass.ds(m * LB + k, 1), :, :]
                        .rearrange("p n c v -> p (n c) v"),
                        st[k][:, :, :], 1.0, None, ALU.mult).then_inc(stat_done, 1)
            dve.wait_ge(stat_done, B * PAIRS * 2)
            link = Chain(dve, chain)
            for b in range(B):
                for n in range(NTILE):
                    ins = nc.vector.bn_aggr(tile_stats[:, b, n, :],
                                            raw_stats[:, 2 * (b * PAIRS + n // TC):2 * (b * PAIRS + n // TC) + 2, n % TC, :])
            link(ins)
            mu, var = tile_stats[:, :, :, 0], tile_stats[:, :, :, 1]
            link(nc.vector.reduce_sum(small[:, 0, :], mu, axis=AX.X))
            dve.wait_ge(const_in, 48)
            nc.vector.tensor_scalar(small[:, 0, :], small[:, 0, :], 1.0 / NTILE, None, ALU.mult).then_inc(to_pe, 1)
            dve.wait_ge(from_pe, 1)
            link(nc.vector.tensor_copy(small[:, 1, :], ps[:, 0, 0:B]))
            gm = small[:, 1, :].unsqueeze(2).to_broadcast([P, B, NTILE])
            link(nc.vector.tensor_tensor(a[:, :, :], mu, gm, ALU.subtract))
            link(nc.vector.tensor_tensor(b2[:, :, :], a[:, :, :], a[:, :, :], ALU.mult))
            link(nc.vector.tensor_tensor(b2[:, :, :], b2[:, :, :], var, ALU.add))
            link(nc.vector.reduce_sum(small[:, 2, :], b2[:, :, :], axis=AX.X))
            nc.vector.tensor_scalar(small[:, 2, :], small[:, 2, :], 1.0 / NTILE, None, ALU.mult).then_inc(to_pe, 1)
            dve.wait_ge(from_pe, 2)
            nc.vector.tensor_scalar(small[:, 2, :], ps[:, 1, 0:B], EPS, None, ALU.add).then_inc(to_act, 1)
            dve.wait_ge(from_act, 1)
            link(nc.vector.reciprocal(small[:, 3, :], small[:, 2, :]))
            gs = small[:, 3, :].unsqueeze(2).to_broadcast([P, B, NTILE])
            link(nc.vector.tensor_tensor(a[:, :, :], a[:, :, :], gs, ALU.mult))
            link(nc.vector.reduce_sum(tl[:, 0, :], a[:, :, :].rearrange("p b n -> p n b"), axis=AX.X))
            nc.vector.tensor_scalar(tl[:, 0, :], tl[:, 0, :], 1.0 / B, None, ALU.mult).then_inc(to_pe, 1)
            dve.wait_ge(from_pe, 3)
            link(nc.vector.tensor_copy(tl[:, 1, :], ps[:, 2, 0:NTILE]))
            tm = tl[:, 1, :].unsqueeze(1).to_broadcast([P, B, NTILE])
            link(nc.vector.tensor_tensor(a[:, :, :], a[:, :, :], tm, ALU.subtract))
            link(nc.vector.tensor_tensor(a[:, :, :], a[:, :, :], a[:, :, :], ALU.mult))
            link(nc.vector.tensor_tensor(b2[:, :, :], var, gs, ALU.mult))
            link(nc.vector.tensor_tensor(b2[:, :, :], b2[:, :, :], gs, ALU.mult))
            link(nc.vector.tensor_tensor(a[:, :, :], a[:, :, :], b2[:, :, :], ALU.add))
            link(nc.vector.reduce_sum(tl[:, 2, :], a[:, :, :].rearrange("p b n -> p n b"), axis=AX.X))
            nc.vector.tensor_scalar(tl[:, 2, :], tl[:, 2, :], 1.0 / B, None, ALU.mult).then_inc(to_pe, 1)
            dve.wait_ge(from_pe, 4)
            nc.vector.tensor_scalar(tl[:, 2, :], ps[:, 3, 0:NTILE], EPS, None, ALU.add).then_inc(to_act, 1)
            dve.wait_ge(from_act, 2)
            link(nc.vector.reciprocal(tl[:, 3, :], tl[:, 2, :]))
            link(nc.vector.tensor_scalar(tl[:, 3, :], tl[:, 3, :], keep["cols"][:, COL_GAMMA:COL_GAMMA + 1], None, ALU.mult))
            link(nc.vector.tensor_tensor(tl[:, 1, :], tl[:, 1, :], tl[:, 3, :], ALU.mult))
            link(nc.vector.tensor_scalar(tl[:, 1, :], tl[:, 1, :], -1.0, keep["cols"][:, COL_BETA:COL_BETA + 1],
                                         ALU.mult, ALU.add))
            link(nc.vector.tensor_tensor(tile_scale[:, :, :], gs,
                                         tl[:, 3, :].unsqueeze(1).to_broadcast([P, B, NTILE]), ALU.mult))
            link(nc.vector.tensor_tensor(b2[:, :, :], tile_scale[:, :, :], gm, ALU.mult))
            link(nc.vector.tensor_tensor(tile_bias[:, :, :], tl[:, 1, :].unsqueeze(1).to_broadcast([P, B, NTILE]),
                                         b2[:, :, :], ALU.subtract))

        @block.tensor
        def _(pe):
            for n, (lhs, rhs, cnt) in enumerate(((keep["gavg"], small[:, 0, :], B), (keep["gavg"], small[:, 2, :], B),
                                                 (keep["cavg"], tl[:, 0, :], NTILE), (keep["cavg"], tl[:, 2, :], NTILE))):
                pe.wait_ge(to_pe, n + 1)
                nc.tensor.matmul(ps[:, n, 0:cnt], lhs[:, :], rhs, start=True, stop=True).then_inc(from_pe, 1)

        @block.scalar
        def _(act):
            act.wait_ge(to_act, 1)
            nc.scalar.activation(small[:, 2, :], small[:, 2, :], ACT.Sqrt).then_inc(from_act, 1)
            act.wait_ge(to_act, 2)
            nc.scalar.activation(tl[:, 2, :], tl[:, 2, :], ACT.Sqrt).then_inc(from_act, 1)


def group_scalars(nc, B, keep, turn, padded):
    CHAIN = 6
    with ExitStack() as ctx:
        sb = lambda name, shape: ctx.enter_context(nc.sbuf_tensor(f"n{turn}_{name}", shape, FP32))
        a, b2, m0 = sb("a", [P, B]), sb("b2", [P, B]), sb("m0", [P, B])
        rows = sb("rows", [P, B, W])
        ps = ctx.enter_context(nc.psum_tensor(f"n{turn}_ps", [P, 2, 512], FP32))
        chain, to_pe, from_pe, to_act, from_act, mean_ready, rows_out = keep["group_sems"]
        padded_turn = keep["padded_turns"]
        if padded is not None:
            keep["padded_turns"] += 1
        block = ctx.enter_context(nc.Block())
        mu, var = keep["stats"][:, :, 0], keep["stats"][:, :, 1]

        @block.vector
        def _(dve):
            link = Chain(dve, chain, CHAIN * turn)
            nc.vector.tensor_copy(m0[:, :], mu).then_inc(to_pe, 1)
            dve.wait_ge(from_pe, 2 * turn + 1)
            link(nc.vector.tensor_copy(keep["mean"][:, :], ps[:, 0, 0:B]))
            if padded is not None:
                nc.vector.tensor_copy(rows[:, :, :], keep["mean"][:, :].unsqueeze(2).to_broadcast([P, B, W])) \
                    .then_inc(mean_ready, 1)
            link(nc.vector.tensor_tensor(a[:, :], mu, keep["mean"][:, :], ALU.subtract))
            link(nc.vector.tensor_tensor(a[:, :], a[:, :], a[:, :], ALU.mult))
            nc.vector.tensor_tensor(b2[:, :], a[:, :], var, ALU.add).then_inc(to_pe, 1)
            dve.wait_ge(from_pe, 2 * turn + 2)
            nc.vector.tensor_scalar(a[:, :], ps[:, 1, 0:B], EPS, None, ALU.add).then_inc(to_act, 1)
            dve.wait_ge(from_act, turn + 1)
            link(nc.vector.reciprocal(keep["scale"][:, :], a[:, :]))
            link(nc.vector.tensor_tensor(b2[:, :], keep["mean"][:, :], keep["scale"][:, :], ALU.mult))
            link(nc.vector.tensor_scalar(keep["bias"][:, :], b2[:, :], -1.0, None, ALU.mult))
            assert link.n == CHAIN * (turn + 1)

        @block.tensor
        def _(pe):
            pe.wait_ge(to_pe, 2 * turn + 1)
            nc.tensor.matmul(ps[:, 0, 0:B], keep["gavg"][:, :], m0[:, :], start=True, stop=True).then_inc(from_pe, 1)
            pe.wait_ge(to_pe, 2 * turn + 2)
            nc.tensor.matmul(ps[:, 1, 0:B], keep["gavg"][:, :], b2[:, :], start=True, stop=True).then_inc(from_pe, 1)

        @block.scalar
        def _(act):
            act.wait_ge(to_act, turn + 1)
            nc.scalar.activation(a[:, :], a[:, :], ACT.Sqrt).then_inc(from_act, 1)

        if padded is not None:
            @block.sync
            def _(sp):
                sp.wait_ge(mean_ready, padded_turn + 1)
                for g in (0, G + 1):
                    sp.dma_start(padded[:, :, g, :].rearrange("b p w -> p b w"), rows[:, :, :]).then_inc(rows_out, 16)
                sp.wait_ge(rows_out, 32 * (padded_turn + 1))


def conv_phase(nc, B, t, keep, tag, src, dst, weights, bias_col, tile_scale=None, tile_bias=None):
    tiled = tag == "l0"
    fused = tag == "l3"
    PW = TC * (TW + 2) if tiled else W + 2
    HALF = P // 2
    LB = 4
    PAD_INC = 2 if tiled else 1
    BODIES = B * STRIPS // LB
    with ExitStack() as ctx:
        def sb(name, shape, dt=FP32):
            return ctx.enter_context(nc.sbuf_tensor(f"{tag}_{name}", shape, dt))

        def sem(name):
            return ctx.enter_context(nc.semaphore(f"{tag}_{name}"))

        wt = sb("wt", [P, 2, 3, HALF])
        raw = [sb(f"raw{k}", [P, 2, GS, W]) for k in range(LB)]
        pad = [sb(f"pad{k}", [P, 2, GS, PW]) for k in range(2)]
        res = [sb(f"res{k}", [P, GS * W]) for k in range(2)]
        strip_stats = [sb(f"sst{k}", [P, NT, 6]) for k in range(2)]
        all_stats = sb("all_stats", [P, B * STRIPS, NT * 6])
        if fused:
            factor = sb("factor", [P, 2, 3, HALF])
            inner = sb("inner", [P, G, W])
            ind_w, ind_f, ind_r = sb("ind_w", [P, P]), sb("ind_f", [P, P]), sb("ind_r", [P, P])
            ind_wb = sb("ind_wb", [P, P], BF16)
        if tiled:
            neg_scale, neg_bias = sb("nsc", [P, B * PAIRS * TC]), sb("nbi", [P, B * PAIRS * TC])
            neg_slope = sb("nslope", [P, 1])
            low = [sb(f"low{k}", [P, 2, GS, W]) for k in range(2)]
            high = [sb(f"high{k}", [P, 2, GS, W]) for k in range(2)]
            tile_scale2 = tile_scale[:, :, :].rearrange("p b n -> p (b n)")
            tile_bias2 = tile_bias[:, :, :].rearrange("p b n -> p (b n)")
        ps = ctx.enter_context(nc.psum_tensor(f"{tag}_ps", [P, 2, NT, 512], FP32))
        w_in, w_ready, stat_c, setup, act_passed = (
            sem("w_in"), sem("w_ready"), sem("stat_c"), sem("setup"), sem("act_passed"))
        loaded = [sem(f"loaded{k}") for k in range(LB)]
        if tiled:
            split = [sem(f"split{k}") for k in range(2)]
            pool_passed = sem("pool_passed")
            scaled, combined = sem("scaled"), sem("combined")
        pad_ready = [sem(f"pad_ready{k}") for k in range(2)]
        tile_done = [sem(f"tile_done{k}") for k in range(2)]
        res_ready = [sem(f"res_ready{k}") for k in range(2)]
        stored = [sem(f"stored{k}") for k in range(2)]
        stat_w = sem("stat_w")
        if fused:
            inner_made, inner_moved = sem("inner_made"), sem("inner_moved")
            INNER = G // (2 * NT)

            def indicators(n):
                return raw[2 + n][:, :, :, :].rearrange("p a g w -> p (a g w)")
        block = ctx.enter_context(nc.Block())
        LOAD_INC = 16 * 6

        @block.sync
        def _(sp):
            sp.dma_start(wt[:, :, :, :], weights[0]).then_inc(w_in, 16)
            if fused:
                sp.dma_start(factor[:, :, :, :], weights[1]).then_inc(w_in, 16)
                for n in range(2):
                    sp.dma_start(indicators(n).bitcast(U16), t["ind"][:, n * (G // 2):(n + 1) * (G // 2), :]
                                 .rearrange("p g w -> p (g w)")).then_inc(w_in, 16)
                sp.dma_start(ind_w[:, :], t["ind_p"]).then_inc(w_in, 16)
                sp.dma_start(ind_f[:, :], t["ind_d"]).then_inc(w_in, 16)

            def load(b, g0, k):
                def rows(half, first, last, quarter, off):
                    n = last - first + 1
                    sp.dma_start(raw[k][first * C:(last + 1) * C, half, :, :],
                                 src[bass.ds(b, 1), quarter * C:(quarter + n) * C, bass.ds(g0 + off, GS), :]
                                 .rearrange("a p g w -> (a p) g w")).then_inc(loaded[k], 16)

                rows(0, 0, 1, 0, 1)
                rows(0, 2, 2, 3, 0)
                rows(0, 3, 3, 2, 1)
                rows(1, 0, 0, 1, 1)
                rows(1, 1, 1, 0, 2)
                rows(1, 2, 3, 2, 1)

            def store(b, g0, k):
                o = (dst[bass.ds(b, 1), :, bass.ds(g0 + (1 if tiled else 0), GS), :]
                     .rearrange("a p g w -> (a p) (g w)"))
                sp.dma_start(o, res[k][:, :]).then_inc(stored[k], 16)

            for k in range(LB):
                if fused and k == 2:
                    sp.wait_ge(inner_moved, INNER)
                load(0, k * GS, k)
            per = STRIPS // LB
            with sp.Fori(0, BODIES - 1) as m:
                b, g0 = sp.snap(m // per), sp.snap(m % per * (LB * GS))
                next_b, next_g0 = sp.snap((m + 1) // per), sp.snap((m + 1) % per * (LB * GS))
                for k in range(LB):
                    sp.wait_ge(res_ready[k % 2], (2 * m + (k // 2 + 1)) * NT + 1)
                    store(b, g0 + k * GS, k % 2)
                    load(next_b, next_g0 + k * GS, k)
            for k in range(LB):
                sp.wait_ge(res_ready[k % 2], (2 * (BODIES - 1) + k // 2 + 1) * NT + 1)
                store(B - 1, (STRIPS - LB + k) * GS, k % 2)
            for k in range(2):
                sp.wait_ge(stored[k], 2 * BODIES * 16 + 1)

        def bodies(eng, strip):
            with eng.Fori(0, BODIES) as m:
                for k in range(LB):
                    strip(m * LB + k, m * 2 + k // 2, k, m)

        def tiles_of(buf, half):
            return buf[:, half, :, :].rearrange("p g (c w) -> p (g c) w", c=TC)

        if tiled:
            @block.gpsimd
            def _(pool):
                pool.wait_ge(w_ready, 1)
                with pool.Fori(0, BODIES) as m:
                    for k in range(LB):
                        h, u = k % 2, m * 2 + k // 2
                        half = 1 - h
                        pool.wait_ge(split[h], u + 1)
                        pool.wait_ge(tile_done[h], u * NT + 1)
                        pool.sem_inc(pool_passed, 1)
                        flat = low[h][:, half, :, :].rearrange("p g w -> p (g w)")
                        nc.gpsimd.tensor_tensor(flat, flat, neg_slope[:, :].to_broadcast([P, GS * W]), ALU.mult) \
                            .then_inc(scaled, 1)
                        pool.wait_ge(scaled, m * LB + (k + 1))
                        nc.gpsimd.tensor_tensor(tiles_of(pad[h], half)[:, :, 1:TW + 1], tiles_of(low[h], half),
                                                tiles_of(high[h], half), ALU.add).then_inc(pad_ready[h], 1)

        @block.scalar
        def _(act):
            def strip(n, u, k, m):
                h = k % 2
                act.wait_ge(loaded[k], (m + 1) * LOAD_INC)
                if tiled:
                    act.wait_ge(pad_ready[h], u * PAD_INC + 1)
                    act.sem_inc(act_passed, 1)
                    tile = m * (2 * TC) + k // 2 * TC
                    for c in range(TC):
                        cs = slice(c * TW, (c + 1) * TW)
                        for o, bias, scale in ((high, tile_bias2, tile_scale2), (low, neg_bias, neg_scale)):
                            ins = nc.scalar.activation(
                                o[h][:, :, :, cs].rearrange("p a g w -> p (a g) w"),
                                raw[k][:, :, :, cs].rearrange("p a g w -> p (a g) w"), ACT.Relu,
                                bias=bias[:, bass.ds(tile + c, 1)], scale=scale[:, bass.ds(tile + c, 1)])
                    ins.then_inc(split[h], 1)
                else:
                    act.wait_ge(tile_done[h], u * NT + 1)
                    act.sem_inc(act_passed, 1)
                    b = act.snap(m // (STRIPS // LB))
                    nc.scalar.activation(pad[h][:, :, :, 1:W + 1].rearrange("p a g w -> p (a g) w"),
                                         raw[k][:, :, :, :].rearrange("p a g w -> p (a g) w"), ACT.Identity,
                                         bias=keep["bias"][:, bass.ds(b, 1)],
                                         scale=keep["scale"][:, bass.ds(b, 1)]).then_inc(pad_ready[h], 1)

            act.wait_ge(w_ready, 1)
            bodies(act, strip)

        def window(tile, half, j, kx):
            rows = tile[:, half, 2 * j:2 * j + 2, :]
            if tiled:
                return rows.rearrange("p g (c w) -> p (g c) w", c=TC)[:, :, kx:kx + TW]
            return rows[:, :, kx:kx + W]

        @block.tensor
        def _(pe):
            def strip(n, u, k, m):
                h = k % 2
                pe.wait_ge(pad_ready[h], (u + 1) * PAD_INC + 1)
                pe.wait_ge(res_ready[h], u * NT + 1)
                for j in range(NT):
                    for kx in range(3):
                        for half in range(2):
                            ins = nc.tensor.matmul(ps[half * HALF:(half + 1) * HALF, h, j, :], wt[:, half, kx, :],
                                                   window(pad[h], half, j, kx),
                                                   start=(kx == 0), stop=(kx == 2))
                    ins.then_inc(tile_done[h], 1)

            pe.wait_ge(w_ready, 1)
            if fused:
                for n in range(INNER):
                    if n >= 2:
                        pe.wait_ge(inner_moved, n - 1)
                    for j in range(NT):
                        at = (n % (INNER // 2) * NT + j) * 512
                        ins = nc.tensor.matmul(ps[:, n % 2, j, :], ind_wb[:, :],
                                               indicators(n // (INNER // 2)).bitcast(BF16)[:, at:at + 512],
                                               start=True, stop=True)
                    ins.then_inc(inner_made, 1)
                pe.wait_ge(inner_moved, INNER)
            bodies(pe, strip)

        @block.vector
        def _(dve):
            link = Chain(dve, setup)
            for k in range(2):
                link(nc.vector.memset(pad[k][:, :, :, :], 0.0))
            if tiled:
                link(nc.vector.tensor_scalar(neg_scale[:, :], tile_scale2, -1.0, None, ALU.mult))
                link(nc.vector.tensor_scalar(neg_bias[:, :], tile_bias2, -1.0, None, ALU.mult))
                link(nc.vector.tensor_scalar(neg_slope[:, :], keep["cols"][:, COL_PRELU:COL_PRELU + 1], -1.0, None, ALU.mult))
            if fused:
                dve.wait_ge(w_in, 16 * 6)
                link(nc.vector.tensor_tensor(wt[:, :, :, :], wt[:, :, :, :], factor[:, :, :, :], ALU.mult))
                link(nc.vector.memset(ind_wb[:, :], 0.0))
                link(nc.vector.tensor_tensor(ind_w[:, :], ind_w[:, :], ind_f[:, :], ALU.mult))
                for q in range(3):
                    part = slice(q * C, (q + 1) * C)
                    for _ in range(q):
                        link(nc.vector.tensor_copy(ind_wb[part, :], ind_w[part, :]))
                        link(nc.vector.tensor_tensor(ind_r[part, :], ind_w[part, :], ind_wb[part, :], ALU.subtract))
                        link(nc.vector.tensor_copy(ind_w[part, :], ind_r[part, :]))
                    link(nc.vector.tensor_copy(ind_wb[part, :], ind_w[part, :]))
            else:
                dve.wait_ge(w_in, 16)
            for k in range(2):
                for x in (pad_ready[k], tile_done[k], res_ready[k], stored[k]):
                    dve.sem_inc(x, 1)
            dve.sem_inc(w_ready, 1)
            if fused:
                for n in range(INNER):
                    dve.wait_ge(inner_made, n + 1)
                    nc.vector.tensor_scalar(
                        inner[:, n * 2 * NT:(n + 1) * 2 * NT, :].rearrange("p g w -> p (g w)"),
                        ps[:, n % 2, :, :].rearrange("p j n -> p (j n)"), keep["cols"][:, bias_col:bias_col + 1],
                        None, ALU.add).then_inc(inner_moved, 1)
                dve.wait_ge(inner_moved, INNER)

            def own_half(u, h):
                dve.wait_ge(split[h], u + 1)
                dve.wait_ge(tile_done[h], u * NT + 1)
                nc.vector.scalar_tensor_tensor(tiles_of(pad[h], h)[:, :, 1:TW + 1], tiles_of(low[h], h),
                                               neg_slope[:, :], tiles_of(high[h], h), ALU.mult, ALU.add) \
                    .then_inc(combined, 1)
                dve.wait_ge(combined, u * 2 + (h + 1))
                edge = pad[h][2 * C:3 * C, 0, 0, :] if h == 0 else pad[h][C:2 * C, 1, GS - 1, :]
                nc.vector.memset(edge, 0.0).then_inc(pad_ready[h], 1)

            def finish(n, u, k, g0):
                h = k % 2
                dve.wait_ge(stored[h], u * 16 + 1)
                for j in range(NT):
                    dve.wait_ge(tile_done[h], u * NT + (j + 2))
                    o = res[h][:, j * 512:(j + 1) * 512]
                    if fused:
                        ins = nc.vector.tensor_tensor(
                            o, ps[:, h, j, :], inner[:, bass.ds(g0 + 2 * j, 2), :].rearrange("p g w -> p (g w)"), ALU.add)
                    else:
                        for half in range(2):
                            part = slice(half * HALF, (half + 1) * HALF)
                            ins = nc.vector.scalar_tensor_tensor(
                                o[part, :], ps[part, h, j, :], keep["cols"][part, bias_col:bias_col + 1],
                                raw[k][part, half, 2 * j:2 * j + 2, :].rearrange("p g w -> p (g w)"),
                                ALU.add, ALU.add)
                    ins.then_inc(res_ready[h], 1)
                dve.wait_ge(res_ready[h], (u + 1) * NT + 1)
                for j in range(NT):
                    ins = nc.vector.bn_stats(strip_stats[h][:, j, :], res[h][:, j * 512:(j + 1) * 512])
                ins.then_inc(stat_w, 1)
                dve.wait_ge(stat_w, n + 1)
                nc.vector.tensor_scalar(
                    all_stats[:, bass.ds(n, 1), :].rearrange("p n v -> p (n v)"),
                    strip_stats[h][:, :, :].rearrange("p n v -> p (n v)"), 1.0, None, ALU.mult).then_inc(stat_c, 1)

            def body(m, last):
                for k in range(LB):
                    if tiled and not (last and k == LB - 1):
                        own_half(m * 2 + (k + 1) // 2, (k + 1) % 2)
                    finish(m * LB + k, m * 2 + k // 2, k, m % (STRIPS // LB) * (LB * GS) + k * GS)

            if tiled:
                own_half(0, 0)
            with dve.Fori(0, BODIES - 1) as m:
                body(m, False)
            body(BODIES - 1, True)
            dve.wait_ge(stat_c, B * STRIPS)
            for b in range(B):
                nc.vector.bn_aggr(keep["stats"][:, b, :], all_stats[:, b * STRIPS:(b + 1) * STRIPS, :]
                                  .rearrange("p n v -> p (n v)"))


def mix_phase(nc, B, t, keep, x2, mag, ang, x3):
    LB = 4
    BODIES = B * STRIPS // LB
    with ExitStack() as ctx:
        sb = lambda name, shape: ctx.enter_context(nc.sbuf_tensor("mx_" + name, shape, FP32))
        sem = lambda name: ctx.enter_context(nc.semaphore("mx_" + name))
        wmag, wang = sb("wmag", [P, P]), sb("wang", [P, P])
        raw = [sb(f"raw{k}", [P, GS * W]) for k in range(LB)]
        mg = [sb(f"mg{k}", [P, GS * W]) for k in range(LB)]
        an = [sb(f"an{k}", [P, GS * W]) for k in range(LB)]
        res = [sb(f"res{k}", [P, GS * W]) for k in range(2)]
        strip_stats = [sb(f"sst{k}", [P, NT, 6]) for k in range(2)]
        all_stats = sb("all_stats", [P, B * STRIPS, NT * 6])
        ps = ctx.enter_context(nc.psum_tensor("mx_ps", [P, 2, NT, 512], FP32))
        w_in, w_ready, stat_c, setup = sem("w_in"), sem("w_ready"), sem("stat_c"), sem("setup")
        loaded = [sem(f"loaded{k}") for k in range(LB)]
        tile_done = [sem(f"tile_done{k}") for k in range(2)]
        res_ready = [sem(f"res_ready{k}") for k in range(2)]
        stored = [sem(f"stored{k}") for k in range(2)]
        stat_w = [sem(f"stat_w{k}") for k in range(2)]
        block = ctx.enter_context(nc.Block())

        @block.sync
        def _(sp):
            sp.dma_start(wmag[:, :], t["wmag"]).then_inc(w_in, 16)
            sp.dma_start(wang[:, :], t["wang"]).then_inc(w_in, 16)

            def load(b, g0, k):
                for buf, src in ((mg, mag), (an, ang), (raw, x2)):
                    sp.dma_start(buf[k][:, :], src[bass.ds(b, 1), :, bass.ds(g0, GS), :]
                                 .rearrange("a p g w -> (a p) (g w)")).then_inc(loaded[k], 16)

            def store(b, g0, k):
                o = x3[bass.ds(b, 1), :, bass.ds(g0 + 1, GS), :].rearrange("a p g w -> (a p) (g w)")
                sp.dma_start(o, res[k][:, :]).then_inc(stored[k], 16)

            for k in range(LB):
                load(0, k * GS, k)
            per = STRIPS // LB
            with sp.Fori(0, BODIES - 1) as m:
                b, g0 = sp.snap(m // per), sp.snap(m % per * (LB * GS))
                next_b, next_g0 = sp.snap((m + 1) // per), sp.snap((m + 1) % per * (LB * GS))
                for k in range(LB):
                    sp.wait_ge(res_ready[k % 2], (2 * m + (k // 2 + 1)) * NT + 1)
                    store(b, g0 + k * GS, k % 2)
                    load(next_b, next_g0 + k * GS, k)
            for k in range(LB):
                sp.wait_ge(res_ready[k % 2], (2 * (BODIES - 1) + k // 2 + 1) * NT + 1)
                store(B - 1, (STRIPS - LB + k) * GS, k % 2)
            for k in range(2):
                sp.wait_ge(stored[k], B * PAIRS * 16 + 1)

        @block.tensor
        def _(pe):
            pe.wait_ge(w_ready, 1)
            with pe.Fori(0, BODIES) as m:
                for k in range(LB):
                    h, u = k % 2, m * 2 + k // 2
                    pe.wait_ge(loaded[k], (m + 1) * (16 * 3))
                    pe.wait_ge(res_ready[h], u * NT + 1)
                    for j in range(NT):
                        cs = slice(j * 512, (j + 1) * 512)
                        nc.tensor.matmul(ps[:, h, j, :], wmag[:, :], mg[k][:, cs], start=True, stop=False)
                        nc.tensor.matmul(ps[:, h, j, :], wang[:, :], an[k][:, cs], start=False, stop=True) \
                            .then_inc(tile_done[h], 1)

        @block.vector
        def _(dve):
            link = Chain(dve, setup)
            dve.wait_ge(w_in, 32)
            link(nc.vector.tensor_scalar(wang[:, :], wang[:, :], 2.0, None, ALU.mult))
            for k in range(2):
                for x in (tile_done[k], res_ready[k], stored[k]):
                    dve.sem_inc(x, 1)
            dve.sem_inc(w_ready, 1)
            with dve.Fori(0, BODIES) as m:
                for k in range(LB):
                    h, u = k % 2, m * 2 + k // 2
                    dve.wait_ge(stored[h], u * 16 + 1)
                    for j in range(NT):
                        cs = slice(j * 512, (j + 1) * 512)
                        dve.wait_ge(tile_done[h], u * NT + (j + 2))
                        nc.vector.tensor_tensor(res[h][:, cs], ps[:, h, j, :], raw[k][:, cs], ALU.add) \
                            .then_inc(res_ready[h], 1)
                    dve.wait_ge(res_ready[h], (u + 1) * NT + 1)
                    for j in range(NT):
                        ins = nc.vector.bn_stats(strip_stats[h][:, j, :], res[h][:, j * 512:(j + 1) * 512])
                    ins.then_inc(stat_w[h], 1)
                    dve.wait_ge(stat_w[h], u + 1)
                    nc.vector.tensor_scalar(
                        all_stats[:, bass.ds(m * LB + k, 1), :].rearrange("p n v -> p (n v)"),
                        strip_stats[h][:, :, :].rearrange("p n v -> p (n v)"), 1.0, None, ALU.mult).then_inc(stat_c, 1)
            dve.wait_ge(stat_c, B * STRIPS)
            for b in range(B):
                nc.vector.bn_aggr(keep["stats"][:, b, :], all_stats[:, b * STRIPS:(b + 1) * STRIPS, :]
                                  .rearrange("p n v -> p (n v)"))


def sample_phase(nc, B, t, keep, x3, h, out):
    with ExitStack() as ctx:
        sb = lambda name, shape: ctx.enter_context(nc.sbuf_tensor("sp_" + name, shape, FP32))
        sem = lambda name: ctx.enter_context(nc.semaphore("sp_" + name))
        woff = sb("woff", [P, 2, P])
        x0 = [sb(f"x0{k}", [P, GS, W + 1]) for k in range(2)]
        x1 = [sb(f"x1{k}", [P, GS, W + 1]) for k in range(2)]
        hb = [sb(f"h{k}", [P, GS * W]) for k in range(2)]
        th = [sb(f"th{k}", [P, 2, GS, W]) for k in range(2)]
        base = [sb(f"base{k}", [P, GS, W]) for k in range(2)]
        dy = [sb(f"dy{k}", [P, GS, W + 1]) for k in range(2)]
        dx = [sb(f"dx{k}", [P, GS, W]) for k in range(2)]
        dxy = [sb(f"dxy{k}", [P, GS, W]) for k in range(2)]
        u = [sb(f"u{k}", [P, GS, W]) for k in range(2)]
        v = sb("v", [P, GS, W])
        res = [sb(f"res{k}", [P, GS, W]) for k in range(2)]
        half_scale, one_scale = sb("half_scale", [P, B]), sb("one_scale", [P, B])
        bn = sb("bn", [P, 8])
        bs = sb("bs", [P, B])
        ps = ctx.enter_context(nc.psum_tensor("sp_ps", [P, 2, 2, NT // 2, 512], FP32))
        act_passed = sem("act_passed")
        w_in, chain, to_pe, from_pe, to_act, from_act, bn_ready = (
            sem("w_in"), sem("chain"), sem("to_pe"), sem("from_pe"), sem("to_act"), sem("from_act"), sem("bn_ready"))
        h_loaded = [sem(f"h_loaded{k}") for k in range(2)]
        x_loaded = [sem(f"x_loaded{k}") for k in range(2)]
        gelu_done = [sem(f"gelu_done{k}") for k in range(2)]
        off_done, th_ready = sem("off_done"), sem("th_ready")
        edge_ready = [sem(f"edge_ready{k}") for k in range(2)]
        res_ready = [sem(f"res_ready{k}") for k in range(2)]
        stored = [sem(f"stored{k}") for k in range(2)]
        diff = [sem(f"diff{k}") for k in range(2)]
        base_ready, dve_step = sem("base_ready"), sem("dve_step")
        block = ctx.enter_context(nc.Block())

        @block.sync
        def _(sp):
            sp.dma_start(woff[:, :, :], t["woff"]).then_inc(w_in, 16)

            def load_h(b, s, k):
                g0 = s * (2 * GS) + k * GS
                sp.dma_start(hb[k][:, :], h[bass.ds(b, 1), :, bass.ds(g0, GS), :]
                             .rearrange("a p g w -> (a p) (g w)")).then_inc(h_loaded[k], 16)

            def load_x(b, s, k):
                g0 = s * (2 * GS) + k * GS
                at = lambda parts, off: (x3[bass.ds(b, 1), parts, bass.ds(g0 + off, GS), :]
                                         .rearrange("a p g w -> (a p) g w"))
                sp.dma_start(x0[k][:, :, 0:W], at(slice(0, P), 1)).then_inc(x_loaded[k], 16)
                sp.dma_start(x1[k][0:P - C, :, 0:W], at(slice(C, P), 1)).then_inc(x_loaded[k], 16)
                sp.dma_start(x1[k][P - C:P, :, 0:W], at(slice(0, C), 2)).then_inc(x_loaded[k], 16)

            for k in range(2):
                load_h(0, 0, k)
                load_x(0, 0, k)
            with sp.Fori(1, B * PAIRS) as m:
                b, s = sp.snap(m // PAIRS), sp.snap(m % PAIRS)
                counts = [(sp.snap(m * 4 + (2 * k - 2)), sp.snap(m * 3), sp.snap(m * 2 + (k - 1))) for k in range(2)]
                for k in range(2):
                    offsets, differences, bases = counts[k]
                    sp.wait_ge(off_done, offsets)
                    load_h(b, s, k)
                    sp.wait_ge(diff[k], differences)
                    sp.wait_ge(base_ready, bases)
                    load_x(b, s, k)

        @block.gpsimd
        def _(pool):
            with pool.Fori(0, B * PAIRS) as m:
                for k in range(2):
                    n = m * 2 + k
                    pool.wait_ge(x_loaded[k], (m + 1) * 48)
                    pool.wait_ge(edge_ready[k], m + 1)
                    pool.wait_ge(dve_step, n * 5 + 3)
                    nc.gpsimd.tensor_tensor(dy[k][:, :, :], x1[k][:, :, :], x0[k][:, :, :], ALU.subtract) \
                        .then_inc(diff[k], 1)
                    nc.gpsimd.tensor_tensor(dx[k][:, :, :], x0[k][:, :, 1:W + 1], x0[k][:, :, 0:W], ALU.subtract) \
                        .then_inc(diff[k], 1)
                    pool.wait_ge(diff[k], m * 3 + 1)
                    nc.gpsimd.tensor_tensor(dxy[k][:, :, :], dy[k][:, :, 1:W + 1], dy[k][:, :, 0:W], ALU.subtract) \
                        .then_inc(diff[k], 1)

        @block.scalar
        def _(act):
            act.wait_ge(to_act, 1)
            nc.scalar.activation(bn[:, 4:5], bn[:, 4:5], ACT.Sqrt).then_inc(from_act, 1)
            act.wait_ge(bn_ready, 1)

            sample = lambda m: m // PAIRS if isinstance(m, int) else act.snap(m // PAIRS)

            def prepare(m, k):
                b = sample(m)
                act.wait_ge(h_loaded[k], (m + 1) * 16)
                nc.scalar.activation(hb[k][:, :], hb[k][:, :], ACT.Gelu, bias=bn[:, 6:7], scale=bn[:, 5:6]) \
                    .then_inc(gelu_done[k], 1)
                act.wait_ge(x_loaded[k], (m + 1) * 48)
                act.sem_inc(act_passed, 1)
                for tile in (x0, x1):
                    ins = nc.scalar.activation(tile[k][:, :, W:W + 1], tile[k][:, :, 0:1], ACT.Identity,
                                               bias=keep["mean"][:, bass.ds(b, 1)], scale=0.0)
                ins.then_inc(edge_ready[k], 1)

            def store(n, k):
                nc.scalar.dma_start(out[bass.ds(n, 1), :, :].rearrange("n p v -> (n p) v"),
                                    res[k][:, :, :].rearrange("p g w -> p (g w)")).then_inc(stored[k], 16)

            def turn_over(m, k, first=False):
                b = sample(m)
                act.wait_ge(res_ready[k], m + 1)
                act.sem_inc(act_passed, 1)
                if not first:
                    store(m * 2 + (k - 2), k)
                nc.scalar.activation(base[k][:, :, :], x0[k][:, :, 0:W], ACT.Identity,
                                     bias=keep["bias"][:, bass.ds(b, 1)],
                                     scale=one_scale[:, bass.ds(b, 1)]).then_inc(base_ready, 1)

            def offsets(m, k):
                for half in range(2):
                    act.wait_ge(off_done, m * 4 + (2 * k + half + 1))
                    nc.scalar.activation(
                        th[k][:, :, half * (GS // 2):(half + 1) * (GS // 2), :].rearrange("p a g w -> p a (g w)"),
                        ps[:, half, :, :, :].rearrange("p a j n -> p a (j n)"), ACT.Tanh).then_inc(th_ready, 1)

            last = B * PAIRS - 1
            prepare(0, 0)
            turn_over(0, 0, True)
            prepare(0, 1)
            offsets(0, 0)
            turn_over(0, 1, True)
            with act.Fori(1, B * PAIRS) as m:
                prepare(m, 0)
                offsets(m - 1, 1)
                turn_over(m, 0)
                prepare(m, 1)
                offsets(m, 0)
                turn_over(m, 1)
            offsets(last, 1)
            for k in range(2):
                act.wait_ge(res_ready[k], B * PAIRS + 1)
                store(B * STRIPS - 2 + k, k)
            for k in range(2):
                act.wait_ge(stored[k], B * PAIRS * 16 + 1)

        @block.tensor
        def _(pe):
            pe.wait_ge(to_pe, 1)
            nc.tensor.matmul(ps[:, 0, 0, 0, 0:1], keep["cavg"][:, :], bn[:, 0:1], start=True, stop=True).then_inc(from_pe, 1)
            pe.wait_ge(to_pe, 2)
            nc.tensor.matmul(ps[:, 0, 1, 0, 0:1], keep["cavg"][:, :], bn[:, 2:3], start=True, stop=True).then_inc(from_pe, 1)
            pe.wait_ge(bn_ready, 1)
            pe.wait_ge(w_in, 16)
            with pe.Fori(0, B * PAIRS) as m:
                for k in range(2):
                    pe.wait_ge(gelu_done[k], m + 1)
                    for half in range(2):
                        pe.wait_ge(th_ready, m * 4 + (2 * k + half + 1))
                        for a in range(2):
                            for j in range(NT // 2):
                                at = (half * (NT // 2) + j) * 512
                                ins = nc.tensor.matmul(ps[:, half, a, j, :], woff[:, a, :], hb[k][:, at:at + 512],
                                                       start=True, stop=True)
                        ins.then_inc(off_done, 1)

        @block.vector
        def _(dve):
            link = Chain(dve, chain)
            mu, var = keep["stats"][:, :, 0], keep["stats"][:, :, 1]
            link(nc.vector.reduce_sum(bn[:, 1:2], mu, axis=AX.X))
            nc.vector.tensor_scalar(bn[:, 0:1], bn[:, 1:2], 1.0 / B, None, ALU.mult).then_inc(to_pe, 1)
            dve.wait_ge(from_pe, 1)
            link(nc.vector.tensor_copy(bn[:, 3:4], ps[:, 0, 0, 0, 0:1]))
            link(nc.vector.tensor_scalar(bs[:, :], mu, bn[:, 3:4], None, ALU.subtract))
            link(nc.vector.tensor_tensor(bs[:, :], bs[:, :], bs[:, :], ALU.mult))
            link(nc.vector.tensor_tensor(bs[:, :], bs[:, :], var, ALU.add))
            link(nc.vector.reduce_sum(bn[:, 1:2], bs[:, :], axis=AX.X))
            nc.vector.tensor_scalar(bn[:, 2:3], bn[:, 1:2], 1.0 / B, None, ALU.mult).then_inc(to_pe, 1)
            dve.wait_ge(from_pe, 2)
            nc.vector.tensor_scalar(bn[:, 4:5], ps[:, 0, 1, 0, 0:1], EPS, None, ALU.add).then_inc(to_act, 1)
            dve.wait_ge(from_act, 1)
            link(nc.vector.reciprocal(bn[:, 7:8], bn[:, 4:5]))
            link(nc.vector.tensor_scalar(bn[:, 5:6], bn[:, 7:8], keep["cols"][:, COL_BNG:COL_BNG + 1], None, ALU.mult))
            link(nc.vector.tensor_tensor(bn[:, 7:8], bn[:, 3:4], bn[:, 5:6], ALU.mult))
            link(nc.vector.tensor_tensor(bn[:, 6:7], keep["cols"][:, COL_BNB:COL_BNB + 1], bn[:, 7:8], ALU.subtract))
            link(nc.vector.tensor_scalar(half_scale[:, :], keep["scale"][:, :], 0.5, None, ALU.mult))
            link(nc.vector.tensor_scalar(one_scale[:, :], keep["scale"][:, :], 1.0, None, ALU.add))
            for k in range(2):
                for x in (stored[k], res_ready[k]):
                    dve.sem_inc(x, 1)
            dve.sem_inc(th_ready, 2)
            dve.sem_inc(dve_step, 10)
            dve.sem_inc(bn_ready, 1)

            with dve.Fori(0, B * PAIRS) as m:
                b, s = dve.snap(m // PAIRS), dve.snap(m % PAIRS)
                for k in range(2):
                    n = m * 2 + k
                    ty, tx = th[k][:, 0, :, :], th[k][:, 1, :, :]
                    dve.wait_ge(diff[k], (m + 1) * 3)
                    dve.wait_ge(th_ready, n * 2 + 4)
                    nc.vector.scalar_tensor_tensor(u[k][:, :, :], ty, 1.0, dxy[k][:, :, :], ALU.add, ALU.mult) \
                        .then_inc(dve_step, 1)
                    nc.vector.scalar_tensor_tensor(v[:, :, :], ty, 1.0, dy[k][:, :, 0:W], ALU.add, ALU.mult) \
                        .then_inc(dve_step, 1)
                    dve.wait_ge(dve_step, n * 5 + 11)
                    nc.vector.scalar_tensor_tensor(u[k][:, :, :], u[k][:, :, :], 0.5, dx[k][:, :, :], ALU.mult, ALU.add) \
                        .then_inc(dve_step, 1)
                    dve.wait_ge(dve_step, n * 5 + 13)
                    nc.vector.scalar_tensor_tensor(u[k][:, :, :], tx, 1.0, u[k][:, :, :], ALU.add, ALU.mult) \
                        .then_inc(dve_step, 1)
                    dve.wait_ge(dve_step, n * 5 + 14)
                    nc.vector.tensor_tensor(u[k][:, :, :], u[k][:, :, :], v[:, :, :], ALU.add).then_inc(dve_step, 1)
                    dve.wait_ge(dve_step, n * 5 + 15)
                    dve.wait_ge(base_ready, n + 1)
                    dve.wait_ge(stored[k], m * 16 + 1)
                    nc.vector.scalar_tensor_tensor(
                        res[k][:, :, :], u[k][:, :, :], half_scale[:, bass.ds(b, 1)], base[k][:, :, :],
                        ALU.mult, ALU.add).then_inc(res_ready[k], 1)


def fourier_phase(nc, B, t, keep, x2, mag, ang):
    NG = B * C // CI
    K2 = 2 * W
    NPH = 2 * W + 6
    with ExitStack() as ctx:
        def sb(name, shape, dt=FP32):
            return ctx.enter_context(nc.sbuf_tensor("ft_" + name, shape, dt))

        def sem(name):
            return ctx.enter_context(nc.semaphore("ft_" + name))

        row_m = sb("row_m", [P, 2, 2, 2, W], FP16)
        col_m = sb("col_m", [P, 2, 2, 3, W], FP16)
        img_scale, img_bias = sb("img_scale", [P, B * C]), sb("img_bias", [P, B * C])
        fourier_tables(nc, B, t, keep, row_m, col_m, img_scale, img_bias, NPH)
        raw = [sb(f"raw{k}", [P, 2, CI, W]) for k in range(2)]
        xf = sb("xf", [P, 2, CI, W])
        xh = [sb(f"xh{k}", [P, 2, CI, W], FP16) for k in range(2)]
        xl = [sb(f"xl{k}", [P, 2, CI, W], FP16) for k in range(2)]
        zh = [sb(f"zh{k}", [P, 2, K2], FP16) for k in range(2)]
        zl = [sb(f"zl{k}", [P, 2, K2], FP16) for k in range(2)]
        y = [sb(f"y{k}", [P, CI, 2, K2]) for k in range(2)]
        sq = sb("sq", [P, CI, 2, K2])
        d = sb("d", [P, CI * 2, W])
        e = sb("e", [P, CI * 2, W])
        f = sb("f", [P, CI * 2, W])
        turn = sb("turn", [P, CI * 2, W])
        flip = sb("flip", [P, CI * 2, W])
        mg = [sb(f"mg{k}", [P, CI, 2, W]) for k in range(2)]
        an = [sb(f"an{k}", [P, CI, 2, W]) for k in range(2)]
        ps_a = ctx.enter_context(nc.psum_tensor("ft_psa", [P, 2, 2, 512], FP32))
        ps_b = ctx.enter_context(nc.psum_tensor("ft_psb", [P, 2, 2, 512], FP32))
        loaded = [sem(f"loaded{k}") for k in range(2)]
        stored = [sem(f"stored{k}") for k in range(2)]
        xf_ready, xh_ready, xn_ready, a_done, zh_done, z_done, b_done, y_done = (
            sem("xf_ready"), sem("xh_ready"), sem("xn_ready"), sem("a_done"), sem("zh_done"), sem("z_done"),
            sem("b_done"), sem("y_done"))
        sq_done, sum_done, mag_done, sized, log_done, inv_done, ratio_done, atan_done, post_done, step, newton_done = (
            sem("sq_done"), sem("sum_done"), sem("mag_done"), sem("sized"), sem("log_done"), sem("inv_done"),
            sem("ratio_done"), sem("atan_done"), sem("post_done"), sem("step"), sem("newton_done"))
        pool_passed = sem("pool_passed")
        block = ctx.enter_context(nc.Block())

        def groups(eng, part):
            part(0, 0, 0, 0, False)
            part(1, 1, 0, 1, False)
            with eng.Fori(1, NG // 2 - 1) as v:
                part(v * 2, 0, v, 2, False)
                part(v * 2 + 1, 1, v, 2, False)
            part(NG - 2, 0, NG // 2 - 1, 2, False)
            part(NG - 1, 1, NG // 2 - 1, 2, True)

        @block.sync
        def _(sp):
            PER = C // CI

            def place(q):
                return (q // PER, q % PER * CI) if isinstance(q, int) else (sp.snap(q // PER), sp.snap(q % PER * CI))

            def load(at, k):
                b, c0 = at
                for r in range(R):
                    sp.dma_start(raw[k][64 * (r % 2):64 * (r % 2) + 64, r // 2, :, :],
                                 x2[bass.ds(b, 1), bass.ds(c0 + r * C, CI), :, :]
                                 .rearrange("a c g w -> g (a c) w")).then_inc(loaded[k], 16)

            def store(at, k):
                b, c0 = at
                for buf, dst in ((mg, mag), (an, ang)):
                    for r in range(R):
                        sp.dma_start(dst[bass.ds(b, 1), bass.ds(c0 + r * C, CI), :, :]
                                     .rearrange("a c g w -> g (a c) w"),
                                     buf[k][64 * (r % 2):64 * (r % 2) + 64, :, r // 2, :]).then_inc(stored[k], 16)

            load(place(0), 0)
            load(place(1), 1)
            sp.wait_ge(xf_ready, 1)
            load(place(2), 0)
            with sp.Fori(0, NG // 2 - 2) as v:
                group = [place(v * 2 + n) for n in (0, 1, 3, 4)]
                sp.wait_ge(xf_ready, v * 2 + 2)
                load(group[2], 1)
                sp.wait_ge(post_done, v * 2 + 3)
                store(group[0], 0)
                sp.wait_ge(xf_ready, v * 2 + 3)
                load(group[3], 0)
                sp.wait_ge(post_done, v * 2 + 4)
                store(group[1], 1)
            sp.wait_ge(xf_ready, NG - 2)
            load(place(NG - 1), 1)
            for q in range(NG - 4, NG):
                sp.wait_ge(post_done, q + 3)
                store(place(q), q % 2)
            for k in range(2):
                sp.wait_ge(stored[k], NG // 2 * (16 * 2 * R) + 1)

        @block.tensor
        def _(pe):
            def rows(k, i):
                for wc in range(2):
                    for hc in range(2):
                        for x, part in ((xh, 0), (xh, 1), (xl, 0)):
                            ins = nc.tensor.matmul(ps_a[:, i % 2, wc, :], x[k][:, hc, i, wc * P:(wc + 1) * P],
                                                   row_m[:, part, hc, :, :].rearrange("p a w -> p (a w)"),
                                                   start=(hc == 0 and x is xh and part == 0),
                                                   stop=(hc == 1 and x is xl))
                ins.then_inc(a_done, 1)

            def part(q, k, u, before, last):
                for i in range(CI):
                    n = q * CI + i
                    if not (last and i == CI - 1):
                        if i == CI - 1:
                            pe.wait_ge(xn_ready, q + 2)
                        pe.wait_ge(z_done, n + 1)
                        rows(k if i < CI - 1 else 1 - k, (i + 1) % CI)
                    pe.wait_ge(z_done, n + 2)
                    pe.wait_ge(y_done, n + 1)
                    for pc in range(2):
                        for wc in range(2):
                            for im in range(2):
                                for z, half in ((zh, 0), (zh, 1), (zl, 0)):
                                    ins = nc.tensor.matmul(
                                        ps_b[:, i % 2, pc, :],
                                        z[i % 2][:, wc, im * W + pc * P:im * W + (pc + 1) * P],
                                        col_m[:, half, wc, 1 - im:3 - im, :].rearrange("p a w -> p (a w)"),
                                        start=(wc == 0 and im == 0 and z is zh and half == 0),
                                        stop=(wc == 1 and im == 1 and z is zl))
                    ins.then_inc(b_done, 1)

            pe.wait_ge(xn_ready, 1)
            rows(0, 0)
            groups(pe, part)

        def whole(ap):
            return ap.rearrange("p a w -> p (a w)")

        def flat(ap):
            return ap.rearrange("p i c w -> p (i c) w")

        def halves(ap, part):
            return flat(ap)[:, :, part * W:(part + 1) * W]

        @block.gpsimd
        def _(pool):
            with pool.Fori(0, NG // 2) as v:
                for k in range(2):
                    pool.wait_ge(xf_ready, v * 2 + (k + 1))
                    pool.sem_inc(pool_passed, 1)
                    nc.gpsimd.tensor_copy(xh[k][:, :, :, :], xf[:, :, :, :]).then_inc(xh_ready, 1)
                    pool.wait_ge(xh_ready, v * 2 + (k + 1))
                    nc.gpsimd.tensor_tensor(xl[k][:, :, :, :], xf[:, :, :, :], xh[k][:, :, :, :], ALU.subtract) \
                        .then_inc(xn_ready, 1)

        @block.scalar
        def _(act):
            act.sem_inc(y_done, 2)

            def take_z(n, i):
                act.wait_ge(a_done, n + 1)
                act.wait_ge(b_done, n + 1)
                nc.scalar.activation(whole(zh[i % 2][:, :, :]), whole(ps_a[:, i % 2, :, :]), ACT.Identity,
                                     scale=1.0 / UP).then_inc(zh_done, 1)

            def take_y(n, i, k, q):
                act.wait_ge(b_done, n + 3)
                if i == 0:
                    act.wait_ge(post_done, q + 1)
                nc.scalar.activation(whole(y[k][:, i, :, :]), whole(ps_b[:, i % 2, :, :]), ACT.Identity,
                                     scale=1.0 / UP).then_inc(y_done, 1)

            def squares(q, k, half):
                i = half * 2
                act.wait_ge(y_done, q * CI + (i + 4))
                if half == 0:
                    act.wait_ge(sum_done, q + 1)
                nc.scalar.activation(sq[:, i:i + 2, :, :].rearrange("p i c w -> p (i c w)"),
                                     y[k][:, i:i + 2, :, :].rearrange("p i c w -> p (i c w)"), ACT.Square) \
                    .then_inc(sq_done, 1)

            def root(q, k, u):
                act.wait_ge(post_done, q + 2)
                nc.scalar.activation(e[:, :, :], halves(y[k][:, :, :, :], 0), ACT.Abs).then_inc(mag_done, 1)
                act.wait_ge(stored[k], u * (16 * 2 * R) + 1)
                act.wait_ge(sum_done, q + 2)
                nc.scalar.activation(flat(mg[k][:, :, :, :]), d[:, :, :], ACT.Sqrt).then_inc(mag_done, 1)

            def inverse(q):
                act.wait_ge(sized, q + 1)
                nc.scalar.activation(f[:, :, :], d[:, :, :], ACT.Ln).then_inc(log_done, 1)
                act.wait_ge(log_done, q + 1)
                nc.scalar.activation(e[:, :, :], f[:, :, :], ACT.Exp, scale=-1.0).then_inc(inv_done, 1)

            def arctan(q):
                act.wait_ge(ratio_done, q + 1)
                nc.scalar.activation(e[:, :, :], d[:, :, :], ACT.Arctan).then_inc(atan_done, 1)

            def part(q, k, u, before, last):
                p, pk, pu = q - 1, 1 - k, u - (1 - k)
                for i in range(CI):
                    n = q * CI + i
                    take_z(n, i)
                    if i:
                        take_y(n - 1, i - 1, k, q)
                    elif before:
                        take_y(n - 1, CI - 1, pk, p)
                    if i == 0 and before == 2:
                        arctan(q - 2)
                    if i == 0 and before:
                        squares(p, pk, 1)
                    if i == 1 and before:
                        root(p, pk, pu)
                    if i == 2 and before:
                        inverse(p)
                    if i == 3:
                        squares(q, k, 0)

            groups(act, part)
            take_y(NG * CI - 1, CI - 1, 1, NG - 1)
            arctan(NG - 2)
            squares(NG - 1, 1, 1)
            root(NG - 1, 1, NG // 2 - 1)
            inverse(NG - 1)
            arctan(NG - 1)

        @block.vector
        def _(dve):
            for k in range(2):
                dve.sem_inc(stored[k], 1)
            dve.sem_inc(z_done, 1)
            dve.sem_inc(b_done, 2)
            dve.sem_inc(post_done, 2)
            dve.sem_inc(sum_done, 1)

            def low_z(n, i):
                dve.wait_ge(zh_done, n + 1)
                nc.vector.scalar_tensor_tensor(whole(zl[i % 2][:, :, :]), whole(ps_a[:, i % 2, :, :]), 1.0 / UP,
                                               whole(zh[i % 2][:, :, :]), ALU.mult, ALU.subtract).then_inc(z_done, 1)

            def normalise(q, k, u):
                dve.wait_ge(loaded[k], (u + 1) * (16 * R))
                for i in range(CI):
                    ins = nc.vector.tensor_scalar(xf[:, :, i, :], raw[k][:, :, i, :],
                                                  img_scale[:, bass.ds(q * CI + i, 1)],
                                                  img_bias[:, bass.ds(q * CI + i, 1)], ALU.mult, ALU.add)
                ins.then_inc(xf_ready, 1)

            STEPS = 4
            def total(q, k):
                dve.wait_ge(post_done, q + 2)
                dve.wait_ge(sq_done, (q + 1) * 2)
                nc.vector.scalar_tensor_tensor(d[:, :, :], halves(sq[:, :, :, :], 0), 1.5e-35,
                                               halves(sq[:, :, :, :], 1), ALU.add, ALU.add).then_inc(sum_done, 1)

            def turns(q, k):
                re, im = halves(y[k][:, :, :, :], 0), halves(y[k][:, :, :, :], 1)
                nc.vector.tensor_scalar(turn[:, :, :], im, 0.0, 0.5, ALU.is_ge, ALU.subtract).then_inc(step, 1)
                dve.wait_ge(step, q * STEPS + 1)
                nc.vector.scalar_tensor_tensor(turn[:, :, :], re, 0.0, turn[:, :, :], ALU.is_lt, ALU.mult) \
                    .then_inc(step, 1)

            def flips(q, k):
                re, im = halves(y[k][:, :, :, :], 0), halves(y[k][:, :, :, :], 1)
                nc.vector.scalar_tensor_tensor(flip[:, :, :].bitcast(U32), re.bitcast(U32), 0x80000000,
                                               im.bitcast(U32), ALU.bitwise_and, ALU.bitwise_xor).then_inc(step, 1)

            def size(q, k):
                dve.wait_ge(mag_done, (q + 1) * 2)
                nc.vector.tensor_tensor(d[:, :, :], flat(mg[k][:, :, :, :]), e[:, :, :], ALU.add).then_inc(sized, 1)

            def ratio(q):
                dve.wait_ge(inv_done, q + 1)
                nc.vector.tensor_tensor(f[:, :, :], d[:, :, :], e[:, :, :], ALU.mult).then_inc(step, 1)
                dve.wait_ge(step, (q + 1) * STEPS)
                nc.vector.scalar_tensor_tensor(f[:, :, :], f[:, :, :], 2.0, e[:, :, :], ALU.subtract, ALU.mult) \
                    .then_inc(newton_done, 1)
                dve.wait_ge(newton_done, q + 1)
                nc.vector.tensor_tensor(d[:, :, :], f[:, :, :], flip[:, :, :], ALU.mult).then_inc(ratio_done, 1)

            def angle(q, k, u):
                dve.wait_ge(stored[k], u * (16 * 2 * R) + 1)
                dve.wait_ge(atan_done, q + 1)
                nc.vector.scalar_tensor_tensor(flat(an[k][:, :, :, :]), e[:, :, :], -1.0 / np.pi, turn[:, :, :],
                                               ALU.mult, ALU.add).then_inc(post_done, 1)

            def part(q, k, u, before, last):
                p, pk, pu = q - 1, 1 - k, u - (1 - k)
                for i in range(CI):
                    low_z(q * CI + i, i)
                    if i == 0 and not last:
                        if before:
                            dve.wait_ge(a_done, q * CI)
                        dve.wait_ge(xn_ready, q + 1)
                        normalise(q + 1, 1 - k, pu + 1)
                    if i == 0 and before == 2:
                        angle(q - 2, k, u - 1)
                    if i == 1 and before:
                        total(p, pk)
                        turns(p, pk)
                        size(p, pk)
                    if i == 2 and before:
                        flips(p, pk)
                    if i == 3 and before:
                        ratio(p)

            normalise(0, 0, 0)
            groups(dve, part)
            angle(NG - 2, 0, NG // 2 - 1)
            total(NG - 1, 1)
            turns(NG - 1, 1)
            size(NG - 1, 1)
            flips(NG - 1, 1)
            ratio(NG - 1)
            angle(NG - 1, 1, NG // 2 - 1)


def fourier_tables(nc, B, t, keep, row_m, col_m, img_scale, img_bias, NPH):
    K2 = 2 * W
    with ExitStack() as ctx:
        sb = lambda name, shape: ctx.enter_context(nc.sbuf_tensor("fm_" + name, shape, FP32))
        sem = lambda name: ctx.enter_context(nc.semaphore("fm_" + name))
        dft = sb("dft", [P, 2, 4, W])
        nsq = sb("nsq", [P, NPH])
        ident = sb("ident", [C, C])
        ones = sb("ones", [C, P])
        spread = sb("spread", [C, 2, B, C])
        ph, turns, co, si = sb("ph", [P, NPH]), sb("turns", [P, NPH]), sb("co", [P, NPH]), sb("si", [P, NPH])
        rhs = sb("rhs", [P, 2, 4, 2, W])
        circ = sb("circ", [P, 2, 2, 2, W])
        dd = sb("dd", [P, 2, 2, 2, W])
        tmp = sb("tmp", [P, 2, W])
        row_f, col_f = sb("row_f", [P, 2, 2, W]), sb("col_f", [P, 2, 3, W])
        a = sb("a", [P, 16])
        c2 = sb("c2", [P, 2, 2])
        ps = ctx.enter_context(nc.psum_tensor("fm_ps", [P, 8, 512], FP32))
        const_in, chain, to_pe, from_pe, to_act, from_act = (
            sem("const_in"), sem("chain"), sem("to_pe"), sem("from_pe"), sem("to_act"), sem("from_act"))
        block = ctx.enter_context(nc.Block())
        col = lambda n: a[:, n:n + 1]

        @block.sync
        def _(sp):
            sp.dma_start(dft[:, :, :, :], t["dft"]).then_inc(const_in, 16)
            sp.dma_start(nsq[:, :], t["nsq"]).then_inc(const_in, 16)
            sp.dma_start(ident[:, :], t["ident"]).then_inc(const_in, 16)

        @block.scalar
        def _(act):
            act.wait_ge(to_act, 1)
            nc.scalar.activation(a[:, 4:7], a[:, 1:4], ACT.Sin).then_inc(from_act, 1)
            act.wait_ge(to_act, 2)
            nc.scalar.activation(si[:, :], ph[:, :], ACT.Sin).then_inc(from_act, 1)
            nc.scalar.activation(co[:, :], ph[:, :], ACT.Sin, scale=0.5).then_inc(from_act, 1)
            act.wait_ge(to_act, 3)
            nc.scalar.activation(col(11), col(10), ACT.Sqrt).then_inc(from_act, 1)

        @block.tensor
        def _(pe):
            pe.wait_ge(to_pe, 1)
            for n in range(2):
                ins = nc.tensor.matmul(ps[:, n, 0:B * C], ones[:, :], spread[:, n, :, :].rearrange("p b c -> p (b c)"),
                                       start=True, stop=True)
            ins.then_inc(from_pe, 1)
            pe.wait_ge(to_pe, 2)
            for v in range(2):
                for pc in range(2):
                    for kk in range(4):
                        ins = nc.tensor.matmul(ps[:, 4 + 2 * v + pc, :], dft[:, v, kk, pc * P:(pc + 1) * P],
                                               rhs[:, v, kk, :, :].rearrange("p a w -> p (a w)"),
                                               start=(kk == 0), stop=(kk == 3))
            ins.then_inc(from_pe, 1)

        @block.vector
        def _(dve):
            link = Chain(dve, chain)
            dve.wait_ge(const_in, 48)
            link(nc.vector.memset(ones[:, :], 1.0))
            for n, src in enumerate((keep["scale"], keep["bias"])):
                link(nc.vector.tensor_tensor(spread[:, n, :, :], src[0:C, :].unsqueeze(2).to_broadcast([C, B, C]),
                                             ident[:, :].unsqueeze(1).to_broadcast([C, B, C]), ALU.mult))
            dve.sem_inc(to_pe, 1)
            alpha = keep["cols"][:, COL_ALPHA:COL_ALPHA + 1]
            link(nc.vector.tensor_scalar(col(0), alpha, 1e-4, float(np.float32(2.0 - 1e-4)), ALU.max, ALU.min))
            link(nc.vector.tensor_scalar(col(1), col(0), float(np.pi / 4), None, ALU.mult))
            link(nc.vector.tensor_scalar(col(2), col(1), -1.0, float(np.pi / 2), ALU.mult, ALU.add))
            link(nc.vector.tensor_scalar(col(3), col(0), float(np.pi / 2), None, ALU.mult))
            dve.sem_inc(to_act, 1)
            dve.wait_ge(from_act, 1)
            link(nc.vector.reciprocal(a[:, 8:10], a[:, 5:7]))
            link(nc.vector.tensor_tensor(col(7), col(4), col(8), ALU.mult))
            link(nc.vector.tensor_scalar(ph[:, :], nsq[:, :], float(np.pi), None, ALU.mult))
            link(nc.vector.tensor_scalar(ph[:, 0:NPH - 2], ph[:, 0:NPH - 2], col(7), 1.0 / W, ALU.mult, ALU.mult))
            link(nc.vector.tensor_scalar(ph[:, NPH - 2:NPH], ph[:, NPH - 2:NPH], col(9), 1.0 / W, ALU.mult, ALU.mult))
            link(nc.vector.tensor_scalar(turns[:, :], ph[:, :], float(0.5 / np.pi), BIG, ALU.mult, ALU.add))
            link(nc.vector.tensor_scalar(turns[:, :], turns[:, :], BIG, None, ALU.subtract))
            for part in (6.28125, float(2 * np.pi - 6.28125)):
                link(nc.vector.scalar_tensor_tensor(ph[:, :], turns[:, :], -part, ph[:, :], ALU.mult, ALU.add))
            link(nc.vector.tensor_scalar(ph[:, :], ph[:, :], 3.1415925, -3.1415925, ALU.min, ALU.max))
            dve.sem_inc(to_act, 1)
            link(nc.vector.tensor_scalar(col(13), col(6), -1.0, None, ALU.mult))
            link(nc.vector.tensor_tensor(col(10), col(6), col(13), ALU.max))
            link(nc.vector.tensor_scalar(col(10), col(10), 1e-12, None, ALU.add))
            dve.sem_inc(to_act, 1)
            dve.wait_ge(from_act, 4)
            link(nc.vector.reciprocal(col(12), col(11)))
            link(nc.vector.tensor_tensor(co[:, :], co[:, :], co[:, :], ALU.mult))
            link(nc.vector.tensor_scalar(co[:, :], co[:, :], -2.0, 1.0, ALU.mult, ALU.add))
            link(nc.vector.tensor_scalar(c2[:, 0, :], co[:, NPH - 2:NPH], 1.0 / W, None, ALU.mult))
            link(nc.vector.tensor_scalar(c2[:, 1, :], si[:, NPH - 2:NPH], -1.0 / W, None, ALU.mult))
            for v in range(2):
                for kk in range(4):
                    for im in range(2):
                        link(nc.vector.tensor_scalar(rhs[:, v, kk, im, :], dft[:, v, kk, :], c2[:, im, kk % 2:kk % 2 + 1],
                                                     None, ALU.mult))
            dve.sem_inc(to_pe, 1)
            dve.wait_ge(from_pe, 1)
            link(nc.vector.tensor_copy(img_scale[:, :], ps[:, 0, 0:B * C]))
            link(nc.vector.tensor_copy(img_bias[:, :], ps[:, 1, 0:B * C]))
            dve.wait_ge(from_pe, 2)
            for v in range(2):
                link(nc.vector.tensor_copy(circ[:, v, :, :, :].rearrange("p c a w -> p c (a w)"),
                                           ps[:, 4 + 2 * v:6 + 2 * v, :]))
            link(nc.vector.tensor_scalar(co[:, K2:K2 + 4], co[:, K2:K2 + 4], col(12), None, ALU.mult))
            link(nc.vector.tensor_scalar(si[:, K2:K2 + 4], si[:, K2:K2 + 4], col(12), None, ALU.mult))
            for v in range(2):
                cr = co[:, v * W:(v + 1) * W].unsqueeze(1).to_broadcast([P, 2, W])
                sr = si[:, v * W:(v + 1) * W].unsqueeze(1).to_broadcast([P, 2, W])
                re, im = circ[:, v, :, 0, :], circ[:, v, :, 1, :]
                link(nc.vector.tensor_tensor(dd[:, v, :, 0, :], re, cr, ALU.mult))
                link(nc.vector.tensor_tensor(tmp[:, :, :], im, sr, ALU.mult))
                link(nc.vector.tensor_tensor(dd[:, v, :, 0, :], dd[:, v, :, 0, :], tmp[:, :, :], ALU.add))
                link(nc.vector.tensor_tensor(dd[:, v, :, 1, :], im, cr, ALU.mult))
                link(nc.vector.tensor_tensor(tmp[:, :, :], re, sr, ALU.mult))
                link(nc.vector.tensor_tensor(dd[:, v, :, 1, :], dd[:, v, :, 1, :], tmp[:, :, :], ALU.subtract))
                for pc in range(2):
                    cc, sc = co[:, K2 + 2 * v + pc:K2 + 2 * v + pc + 1], si[:, K2 + 2 * v + pc:K2 + 2 * v + pc + 1]
                    o_re, o_im = ((col_f[:, pc, 1, :], col_f[:, pc, 2, :]) if v == 0 else
                                  (row_f[:, pc, 0, :], row_f[:, pc, 1, :]))
                    link(nc.vector.tensor_scalar(tmp[:, 0, :], dd[:, v, pc, 1, :], sc, None, ALU.mult))
                    link(nc.vector.scalar_tensor_tensor(o_re, dd[:, v, pc, 0, :], cc, tmp[:, 0, :], ALU.mult, ALU.add))
                    link(nc.vector.tensor_scalar(tmp[:, 1, :], dd[:, v, pc, 0, :], sc, None, ALU.mult))
                    link(nc.vector.scalar_tensor_tensor(o_im, dd[:, v, pc, 1, :], cc, tmp[:, 1, :], ALU.mult, ALU.subtract))
            link(nc.vector.tensor_scalar(col_f[:, :, 0, :], col_f[:, :, 2, :], -1.0, None, ALU.mult))
            for part, whole in ((row_m, row_f), (col_m, col_f)):
                link(nc.vector.tensor_scalar(whole[:, :, :, :], whole[:, :, :, :], UP, None, ALU.mult))
                link(nc.vector.tensor_copy(part[:, 0, :, :, :], whole[:, :, :, :]))
                link(nc.vector.tensor_tensor(part[:, 1, :, :, :], whole[:, :, :, :], part[:, 0, :, :, :], ALU.subtract))


_COLS = ("L0_conv_gamma", "L0_conv_beta", "L0_conv_prelu_a", "L0_conv_conv_b", "L1_conv_b", "L3_conv_dw_b",
         "L3_conv_bn_g", "L3_conv_bn_b", "L2_conv_alpha")


HALF_ROWS = ((0, 1, -1, 2), (1, 4, 2, 3))


def _band(w):
    m = np.zeros((R, C, 2, 3, 2, C), w.dtype)
    for half, rows in enumerate(HALF_ROWS):
        for a, row in enumerate(rows):
            for q in range(2):
                ky = row - (2 * half + q) + 1
                if 0 <= ky <= 2:
                    m[a, :, half, :, q, :] = w[:, :, ky, :].transpose(1, 2, 0)
    return m.reshape(P, 2, 3, 2 * C)


def _block_diagonal(w):
    m = np.zeros((R, C, R, C), w.dtype)
    for r in range(R):
        m[r, :, r, :] = w.T
    return m.reshape(P, P)


BF16_ONE = 0x3F80


def _constants():
    c = np.arange(P) % C
    gavg = ((c[:, None] // 2 == c[None, :] // 2) / (2.0 * R)).astype(np.float32)
    cavg = ((c[:, None] == c[None, :]) / float(R)).astype(np.float32)
    perm = np.array([R * (p % G) + p // G for p in range(H)])
    j = np.arange(W)
    dft = np.zeros((P, 2, 4, W), np.float32)
    for v, rows in enumerate((j, perm)):
        x = 2 * np.pi * ((j[:, None] * rows[None, :]) % W) / W
        dft[:, v] = np.concatenate([np.cos(x).reshape(2, P, W), np.sin(x).reshape(2, P, W)]).transpose(1, 0, 2)
    n2 = (((j + W // 2) % W) - W // 2) ** 2
    nsq = np.zeros((P, 2 * W + 6), np.float32)
    nsq[:, 0:W] = n2
    nsq[:, W:2 * W] = n2[perm]
    nsq[:, 2 * W:2 * W + 2] = n2.reshape(2, P).T
    nsq[:, 2 * W + 2:2 * W + 4] = n2[perm].reshape(2, P).T
    nsq[:, 2 * W + 4:] = ((j - W // 2) ** 2).reshape(2, P).T
    ind = np.zeros((R, C, G, W), np.uint16)
    for q in range(6):
        h = R * np.arange(G) - 1 + q
        for kx in range(3):
            c = j + kx - 1
            inside = ((h >= 0) & (h < H))[:, None] & ((c >= 0) & (c < W))[None, :]
            ind[0:3, q * 3 + kx] = np.where(inside, BF16_ONE, 0)
    ind = ind.reshape(P, G, W)
    return dict(gavg=gavg, cavg=cavg, dft=dft, nsq=nsq, ident=np.eye(C, dtype=np.float32), ind=ind)


def layout(inputs):
    x = np.asarray(inputs["x"])
    B = x.shape[0]
    a = _constants()
    xr = np.zeros((B, R, C, G + 2, W), x.dtype)
    xr[:, :, :, 1:G + 1] = x.reshape(B, C, G, R, W).transpose(0, 3, 1, 2, 4)
    a["xr"] = xr.reshape(B, P, G + 2, W)
    cols = np.zeros((P, NCOL), np.float32)
    for n, name in enumerate(_COLS):
        v = np.asarray(inputs[name]).reshape(-1)
        cols[:, n] = np.tile(v, R) if v.size == C else v[0]
    a["cols"] = cols
    a["w0"] = _band(np.asarray(inputs["L0_conv_conv_w"]))
    a["w1"] = _band(np.asarray(inputs["L1_conv_W"]))
    pw = np.asarray(inputs["L3_conv_proj_w"])[:, :, 0, 0]
    dw = np.asarray(inputs["L3_conv_dw_w"])[:, 0]
    pb = np.asarray(inputs["L3_conv_proj_b"])
    a["w3_p"] = _band(np.broadcast_to(pw[:, :, None, None], (C, C, 3, 3)))
    a["w3_d"] = _band(np.broadcast_to(dw[:, None, :, :], (C, C, 3, 3)))
    ind_d = np.zeros((R, C, R, C), np.float32)
    for q in range(6):
        for r in range(R):
            if 0 <= q - r <= 2:
                for kx in range(3):
                    ind_d[0:3, q * 3 + kx, r, :] = dw[:, q - r, kx]
    a["ind_d"] = ind_d.reshape(P, P)
    a["ind_p"] = np.broadcast_to(np.tile(pb, R), (P, P))
    w = np.asarray(inputs["L2_conv_w"])
    a["wmag"], a["wang"] = _block_diagonal(w[:, :C]), _block_diagonal(w[:, C:])
    off = np.asarray(inputs["L3_conv_off_w"])[:, :, 0, 0]
    a["woff"] = np.stack([_block_diagonal(np.broadcast_to(off[n], (C, C))) for n in range(2)], axis=1)
    return {k: np.ascontiguousarray(v) for k, v in a.items()}, B


def program(nc, arrays, B):
    t = {k: nc.dram_tensor("in_" + k, v.shape, mybir.dt.from_np(v.dtype), kind="ExternalInput").ap()
         for k, v in arrays.items()}
    t["out"] = nc.dram_tensor("out_0", [B * STRIPS, P, GS * W], FP32, kind="ExternalOutput").ap()
    build(nc, B, t)


def unlay(o, B):
    return np.ascontiguousarray(o.reshape(B, STRIPS, R, C, GS, W).transpose(0, 3, 1, 4, 2, 5)).reshape(B, C, H, W)


def kernel(**inputs):
    import concourse.bacc as _bacc
    from concourse.bass_utils import run_bass_kernel_spmd as _run

    arrays, B = layout(inputs)
    nc = _bacc.Bacc("TRN2", target_bir_lowering=False, num_devices=1)
    program(nc, arrays, B)
    r = _run(nc, [{"in_" + k: v for k, v in arrays.items()}], core_ids=[0])
    return unlay(r.results[0]["out_0"], B)
```
